# Optimizing a Trainium2 kernel written in Bass

```python
import numpy as np
import jax
import jax.numpy as jnp

def _softmax(x, axis=-1):
    return jax.nn.softmax(x, axis=axis)

def _gelu(x):
    return jax.nn.gelu(x, approximate=True)

def _silu(x):
    return jax.nn.silu(x)

def _sigmoid(x):
    return jax.nn.sigmoid(x)

def _layernorm(x, axis=-1, eps=1e-05):
    m = jnp.mean(x, axis=axis, keepdims=True)
    v = jnp.var(x, axis=axis, keepdims=True)
    return (x - m) / jnp.sqrt(v + eps)

def _scatter_add(tgt, idx, src, axis=0):
    return tgt.at[idx].add(src)

def _segment_sum(src, seg, n):
    return jax.ops.segment_sum(src, seg, n)
kernel_name = 'mk_gnn_preln_d4_gnn_r32_39a372'

def setup_inputs(seed: int=0):
    np.random.seed(seed)
    _w = jnp.asarray

    def _rec_inputs():
        import jax
        import jax.numpy as jnp
        _gk = jax.random.key(seed)
        x = -0.0003713 + 1 * jax.random.normal(jax.random.fold_in(_gk, 1), (3125, 256), jnp.float32)
        src = jax.random.randint(jax.random.fold_in(_gk, 2), (50000,), 0, 3125, jnp.int32)
        dst = jnp.minimum((3125 * jax.random.uniform(jax.random.fold_in(_gk, 3), (50000,)) ** 2.0).astype(jnp.int32), 99999)
        _o = jnp.argsort(dst, stable=True)
        src = src[_o]
        dst = dst[_o]
        edge_attr_64 = 0.000151818 + 1.00006 * jax.random.normal(jax.random.fold_in(_gk, 12), (50000, 64), jnp.float32)
        edge_type_8 = jax.random.randint(jax.random.fold_in(_gk, 14), (50000,), 0, 8, jnp.int32)
        edge_weight = jax.random.uniform(jax.random.fold_in(_gk, 15), (50000,), jnp.float32, 0.0, 4.99999)
        return (x, src, dst, edge_attr_64, edge_type_8, edge_weight)
    x, src, dst, edge_attr_64, edge_type_8, edge_weight = _rec_inputs()

    def _L0_gnn_setup():
        import jax, jax.numpy as jnp
        import numpy as np
        N, E, D_IN, D_OUT = (50000, 50000, 256, 256)
        key = jax.random.key(seed)
        k1, k2, k3, k4, k5, k6 = jax.random.split(key, 6)
        x = jax.random.normal(k1, (N, D_IN), dtype=jnp.float32)
        edge_index = jax.random.randint(k2, (2, E), 0, N, dtype=jnp.int64)
        s = 1.0 / np.sqrt(D_IN)
        W1 = jax.random.uniform(k3, (D_OUT, D_IN), minval=-s, maxval=s, dtype=jnp.float32)
        b1 = jax.random.uniform(k4, (D_OUT,), minval=-s, maxval=s, dtype=jnp.float32)
        W2 = jax.random.uniform(k5, (D_OUT, D_IN), minval=-s, maxval=s, dtype=jnp.float32)
        b2 = jax.random.uniform(k6, (D_OUT,), minval=-s, maxval=s, dtype=jnp.float32)
        return {'x': x, 'W1': W1, 'b1': b1, 'W2': W2, 'b2': b2, 'edge_index': edge_index}
    _L0_gnn_all = _L0_gnn_setup()
    _L0_gnn_in = {k: v for k, v in _L0_gnn_all.items() if k in ('W1', 'b1', 'W2', 'b2')}
    del _L0_gnn_all

    def _L1_gnn_setup():
        import jax, jax.numpy as jnp
        import numpy as np
        N_NODES = 625
        N_EDGES = 10000
        NUM_RELS = 8
        DIM = 256
        BN_EPS = 1e-05
        key = jax.random.key(seed)
        k1, k2, k3, k4, k5 = jax.random.split(key, 5)
        h = jax.random.normal(k1, (N_NODES, DIM), dtype=jnp.float32)
        weight = jax.random.normal(k2, (NUM_RELS, DIM, DIM), dtype=jnp.float32) * 0.05
        gamma = jnp.ones((DIM,), dtype=jnp.float32)
        beta = jnp.zeros((DIM,), dtype=jnp.float32)
        src = jax.random.randint(k3, (N_EDGES,), 0, N_NODES, dtype=jnp.int32)
        dst = jax.random.randint(k4, (N_EDGES,), 0, N_NODES, dtype=jnp.int32)
        rel = jax.random.randint(k5, (N_EDGES,), 0, NUM_RELS, dtype=jnp.int32)
        return {'h': h, 'weight': weight, 'gamma': gamma, 'beta': beta, 'src': src, 'dst': dst, 'rel': rel}
    _L1_gnn_all = _L1_gnn_setup()
    _L1_gnn_in = {k: v for k, v in _L1_gnn_all.items() if k in ('weight', 'gamma', 'beta')}
    del _L1_gnn_all

    def _L2_gnn_setup():
        import jax, jax.numpy as jnp
        import numpy as np
        H = 256
        R = 64
        N = 625
        E = 10000
        CUTOFF_LO = 0.0
        CUTOFF_UP = 5.0
        LN_EPS = 1e-05

        def _layernorm(x, g, b):
            mu = jnp.mean(x, axis=-1, keepdims=True)
            var = jnp.var(x, axis=-1, keepdims=True)
            return (x - mu) * jax.lax.rsqrt(var + LN_EPS) * g + b

        def _cosine_cutoff(r):
            c = 0.5 * (jnp.cos(r * (jnp.pi / CUTOFF_UP)) + 1.0)
            return c * (r < CUTOFF_UP).astype(r.dtype)
        key = jax.random.key(seed)
        ks = jax.random.split(key, 16)

        def xavier(k, shape):
            fan_in, fan_out = (shape[1], shape[0])
            lim = np.sqrt(6.0 / (fan_in + fan_out))
            return jax.random.uniform(k, shape, jnp.float32, -lim, lim)
        x = jax.random.normal(ks[0], (N, H), jnp.float32)
        edge_index = jax.random.randint(ks[1], (2, E), 0, N, jnp.int64)
        edge_weight = jax.random.uniform(ks[2], (E,), jnp.float32, 0.0, CUTOFF_UP)
        edge_attr = jax.random.normal(ks[3], (E, R), jnp.float32)
        return {'x': x, 'edge_index': edge_index, 'edge_weight': edge_weight, 'edge_attr': edge_attr, 'ln_g': jnp.ones((H,), jnp.float32), 'ln_b': jnp.zeros((H,), jnp.float32), 'Wq': xavier(ks[4], (H, H)), 'bq': jnp.zeros((H,), jnp.float32), 'Wk': xavier(ks[5], (H, H)), 'bk': jnp.zeros((H,), jnp.float32), 'Wv': xavier(ks[6], (H, H)), 'bv': jnp.zeros((H,), jnp.float32), 'Wo': xavier(ks[7], (H, H)), 'bo': jnp.zeros((H,), jnp.float32), 'Wdk': xavier(ks[8], (H, R)), 'bdk': jnp.zeros((H,), jnp.float32), 'Wdv': xavier(ks[9], (H, R)), 'bdv': jnp.zeros((H,), jnp.float32)}
    _L2_gnn_all = _L2_gnn_setup()
    _L2_gnn_in = {k: v for k, v in _L2_gnn_all.items() if k in ('ln_g', 'ln_b', 'Wq', 'bq', 'Wk', 'bk', 'Wv', 'bv', 'Wo', 'bo', 'Wdk', 'bdk', 'Wdv', 'bdv')}
    del _L2_gnn_all

    def _L3_gnn_setup():
        import jax, jax.numpy as jnp
        import numpy as np
        N_NODES = 50000
        N_EDGES = 50000
        IN_DIM, OUT_DIM, N_HEADS = (256, 64, 4)
        EPS = 1e-12
        key = jax.random.key(seed)
        k1, k2, k3, k4, k5 = jax.random.split(key, 5)
        h = jax.random.normal(k1, (N_NODES, IN_DIM), dtype=jnp.float32)
        edge_index = jax.random.randint(k2, (2, N_EDGES), 0, N_NODES, dtype=jnp.int32)
        W = jax.random.normal(k3, (IN_DIM, OUT_DIM), dtype=jnp.float32) * 0.05
        Wl = jax.random.normal(k4, (N_HEADS, OUT_DIM), dtype=jnp.float32) * 0.05
        Wr = jax.random.normal(k5, (N_HEADS, OUT_DIM), dtype=jnp.float32) * 0.05
        b = jnp.zeros((OUT_DIM,), dtype=jnp.float32)
        return {'h': h, 'W': W, 'Wl': Wl, 'Wr': Wr, 'b': b, 'edge_index': edge_index}
    _L3_gnn_all = _L3_gnn_setup()
    _L3_gnn_in = {k: v for k, v in _L3_gnn_all.items() if k in ('W', 'Wl', 'Wr', 'b')}
    del _L3_gnn_all
    return {'x': x, 'src': src, 'dst': dst, 'edge_attr_64': edge_attr_64, 'edge_type_8': edge_type_8, 'edge_weight': edge_weight, 'L0_gnn_W1': _L0_gnn_in['W1'], 'L0_gnn_b1': _L0_gnn_in['b1'], 'L0_gnn_W2': _L0_gnn_in['W2'], 'L0_gnn_b2': _L0_gnn_in['b2'], 'L1_gnn_weight': _L1_gnn_in['weight'], 'L1_gnn_gamma': _L1_gnn_in['gamma'], 'L1_gnn_beta': _L1_gnn_in['beta'], 'L2_gnn_ln_g': _L2_gnn_in['ln_g'], 'L2_gnn_ln_b': _L2_gnn_in['ln_b'], 'L2_gnn_Wq': _L2_gnn_in['Wq'], 'L2_gnn_bq': _L2_gnn_in['bq'], 'L2_gnn_Wk': _L2_gnn_in['Wk'], 'L2_gnn_bk': _L2_gnn_in['bk'], 'L2_gnn_Wv': _L2_gnn_in['Wv'], 'L2_gnn_bv': _L2_gnn_in['bv'], 'L2_gnn_Wo': _L2_gnn_in['Wo'], 'L2_gnn_bo': _L2_gnn_in['bo'], 'L2_gnn_Wdk': _L2_gnn_in['Wdk'], 'L2_gnn_bdk': _L2_gnn_in['bdk'], 'L2_gnn_Wdv': _L2_gnn_in['Wdv'], 'L2_gnn_bdv': _L2_gnn_in['bdv'], 'L3_gnn_W': _L3_gnn_in['W'], 'L3_gnn_Wl': _L3_gnn_in['Wl'], 'L3_gnn_Wr': _L3_gnn_in['Wr'], 'L3_gnn_b': _L3_gnn_in['b']}

def reference(x, src, dst, edge_attr_64, edge_type_8, edge_weight, L0_gnn_W1, L0_gnn_b1, L0_gnn_W2, L0_gnn_b2, L1_gnn_weight, L1_gnn_gamma, L1_gnn_beta, L2_gnn_ln_g, L2_gnn_ln_b, L2_gnn_Wq, L2_gnn_bq, L2_gnn_Wk, L2_gnn_bk, L2_gnn_Wv, L2_gnn_bv, L2_gnn_Wo, L2_gnn_bo, L2_gnn_Wdk, L2_gnn_bdk, L2_gnn_Wdv, L2_gnn_bdv, L3_gnn_W, L3_gnn_Wl, L3_gnn_Wr, L3_gnn_b):
    import jax
    import jax.numpy as jnp

    def _L0_gnn_ref(x, W1, b1, W2, b2, edge_index):
        import jax, jax.numpy as jnp
        import numpy as np
        N, E, D_IN, D_OUT = (50000, 50000, 256, 256)
        dst = edge_index[0]
        nbr = edge_index[1]
        n = x.shape[0]
        agg = jax.ops.segment_sum(x[nbr], dst, num_segments=n)
        cnt = jax.ops.segment_sum(jnp.ones((nbr.shape[0],), x.dtype), dst, num_segments=n)
        mean = agg / jnp.maximum(cnt, 1.0)[:, None]
        return x @ W1.T + b1 + mean @ W2.T + b2

    def _L1_gnn_ref(h, weight, gamma, beta, src, dst, rel):
        import jax, jax.numpy as jnp
        import numpy as np
        N_NODES = 625
        N_EDGES = 10000
        NUM_RELS = 8
        DIM = 256
        BN_EPS = 1e-05
        all_h = jnp.einsum('ni,rio->nro', h, weight)
        msg = all_h[src, rel]
        agg = jax.ops.segment_sum(msg, dst, num_segments=h.shape[0])
        mean = jnp.mean(agg, axis=0)
        var = jnp.mean(jnp.square(agg - mean), axis=0)
        out = (agg - mean) * jax.lax.rsqrt(var + BN_EPS) * gamma + beta
        return out

    def _L2_gnn_ref(x, edge_index, edge_weight, edge_attr, ln_g, ln_b, Wq, bq, Wk, bk, Wv, bv, Wo, bo, Wdk, bdk, Wdv, bdv):
        import jax, jax.numpy as jnp
        import numpy as np
        H = 256
        R = 64
        N = 625
        E = 10000
        CUTOFF_LO = 0.0
        CUTOFF_UP = 5.0
        LN_EPS = 1e-05

        def _layernorm(x, g, b):
            mu = jnp.mean(x, axis=-1, keepdims=True)
            var = jnp.var(x, axis=-1, keepdims=True)
            return (x - mu) * jax.lax.rsqrt(var + LN_EPS) * g + b

        def _cosine_cutoff(r):
            c = 0.5 * (jnp.cos(r * (jnp.pi / CUTOFF_UP)) + 1.0)
            return c * (r < CUTOFF_UP).astype(r.dtype)
        src = edge_index[0]
        dst = edge_index[1]
        x_norm = _layernorm(x, ln_g, ln_b)
        q = x_norm @ Wq.T + bq
        k = x_norm @ Wk.T + bk
        v = x_norm @ Wv.T + bv
        dk = jax.nn.silu(edge_attr @ Wdk.T + bdk)
        dv = jax.nn.silu(edge_attr @ Wdv.T + bdv)
        q_i = q[dst]
        k_j = k[src]
        v_j = v[src]
        attn = jnp.sum(q_i * k_j * dk, axis=1)
        attn = jax.nn.silu(attn) * _cosine_cutoff(edge_weight)
        msg = v_j * dv * attn[:, None]
        agg = jax.ops.segment_sum(msg, dst, num_segments=x.shape[0])
        out = agg @ Wo.T + bo
        return x + out

    def _L3_gnn_ref(h, W, Wl, Wr, b, edge_index):
        import jax, jax.numpy as jnp
        import numpy as np
        N_NODES = 50000
        N_EDGES = 50000
        IN_DIM, OUT_DIM, N_HEADS = (256, 64, 4)
        EPS = 1e-12
        N = h.shape[0]
        H = Wl.shape[0]
        x = h @ W
        el = x @ Wl.T
        er = x @ Wr.T
        src, dst = (edge_index[0], edge_index[1])
        e = el[src] + er[dst]
        e = jnp.exp(jax.nn.leaky_relu(e, negative_slope=0.2))
        rowsum = jax.ops.segment_sum(e, src, num_segments=N)
        w = e / jnp.maximum(rowsum, EPS)[src]
        heads = [jax.ops.segment_sum(w[:, hd:hd + 1] * x[dst], src, num_segments=N) for hd in range(H)]
        out = jnp.stack(heads, axis=1)
        out = jax.nn.elu(out + b)
        return out.reshape(N, H * x.shape[1])
    edge_index = jnp.stack([src, dst])
    h = jnp.maximum(_layernorm(x, axis=-1), 0.0)
    x = x + _L0_gnn_ref(h, L0_gnn_W1, L0_gnn_b1, L0_gnn_W2, L0_gnn_b2, edge_index)
    h = jnp.maximum(_layernorm(x, axis=-1), 0.0)
    x = x + _L1_gnn_ref(h, L1_gnn_weight, L1_gnn_gamma, L1_gnn_beta, src, dst, edge_type_8)
    h = jnp.maximum(_layernorm(x, axis=-1), 0.0)
    x = x + _L2_gnn_ref(h, edge_index, edge_weight, edge_attr_64, L2_gnn_ln_g, L2_gnn_ln_b, L2_gnn_Wq, L2_gnn_bq, L2_gnn_Wk, L2_gnn_bk, L2_gnn_Wv, L2_gnn_bv, L2_gnn_Wo, L2_gnn_bo, L2_gnn_Wdk, L2_gnn_bdk, L2_gnn_Wdv, L2_gnn_bdv)
    h = jnp.maximum(_layernorm(x, axis=-1), 0.0)
    x = x + _L3_gnn_ref(h, L3_gnn_W, L3_gnn_Wl, L3_gnn_Wr, L3_gnn_b, edge_index)
    return x

_drawn_inputs = setup_inputs


def setup_inputs(seed=0):
    import zlib

    import numpy as np

    out = dict(_drawn_inputs(seed))
    spreads = {'L1_gnn_gamma': (1.0, 0.2),
     'L1_gnn_beta': (0.0, 0.1),
     'L2_gnn_ln_g': (1.0, 0.2),
     'L2_gnn_ln_b': (0.0, 0.1),
     'L2_gnn_bq': (0.0, 0.1),
     'L2_gnn_bk': (0.0, 0.1),
     'L2_gnn_bv': (0.0, 0.1),
     'L2_gnn_bo': (0.0, 0.384),
     'L2_gnn_bdk': (0.0, 0.1),
     'L2_gnn_bdv': (0.0, 0.1),
     'L3_gnn_b': (0.0, 0.433)}
    factors = {'L3_gnn_Wl': 8.0, 'L3_gnn_Wr': 8.0}
    for name, (base, spread) in spreads.items():
        noise = np.random.default_rng([zlib.crc32(name.encode()), seed]).standard_normal(out[name].shape)
        drawn = base * np.exp(spread * noise) if base else spread * noise
        out[name] = jnp.asarray(drawn.astype(out[name].dtype))
    for name, factor in factors.items():
        out[name] = (out[name] * factor).astype(out[name].dtype)
    return out
```

```python
import numpy as np
import concourse.bass as bass
import concourse.mybir as mybir
from contextlib import ExitStack

P = 128
N_NODES, N_EDGES, D, D_EDGE, N_RELS, HEADS, D_HEAD = 3125, 50000, 256, 64, 8, 4, 64
NODE_TILES = -(-N_NODES // P)
NODE_ROWS = NODE_TILES * P
PAD_NODE = NODE_ROWS - 1
LAST_ROWS = N_NODES - (NODE_TILES - 1) * P
EDGE_COLS = 8 * -(-N_EDGES // (8 * P))
EDGE_ROWS = EDGE_COLS * P
SLOT_TILES = (EDGE_COLS + NODE_TILES - 1) // 8 * 8
SLOTS = SLOT_TILES * P
ROW = D_EDGE + 1
AGG_W = D + HEADS
LN_EPS, BN_EPS, SUM_EPS = 1e-5, 1e-5, 1e-12
U = 8
UH = 16
G = 4
NK = 5
WORK = 12800
D_T3 = D_HEAD + HEADS

f32, bf16, i32 = mybir.dt.float32, mybir.dt.bfloat16, mybir.dt.int32
ALU = mybir.AluOpType
ACT = mybir.ActivationFunctionType
AXX = mybir.AxisListType.X
assert EDGE_COLS * P + NODE_TILES * (P - 1) < (SLOT_TILES + 1) * P

BIAS = {}
_at = 0
for _n, _w in (("b1", D), ("b2", D), ("gamma", D), ("beta", D), ("ln_g", D), ("ln_b", D),
               ("bqkv", 3 * D), ("bo", D), ("b3", D_HEAD)):
    BIAS[_n] = (_at, _at + _w)
    _at += _w
BIAS_W = _at


def wait(eng, sem, value):
    if isinstance(value, int) and value <= 0:
        return
    eng.wait_ge(sem, value)


def at(t, n=1):
    return bass.ds(t, n)


class Chip:

    def __init__(self, nc, ctx):
        self.nc, self.ctx = nc, ctx
        sb, ps = self.sb, self.ps
        self.X = sb("X", [P, NODE_TILES, D], f32)
        self.AGG = sb("AGG", [P, NODE_TILES, AGG_W], f32)
        self.Q = sb("Q", [P, NODE_TILES, D], f32)
        self.work = sb("work", [P, WORK], f32)
        self.w12 = sb("w12", [P, 2, 2 * D], f32)
        self.wrel = sb("wrel", [P, 2, N_RELS * D], f32)
        self.wqkv = sb("wqkv", [P, 2, 3 * D], f32)
        self.wo = sb("wo", [P, 2, D], f32)
        self.wd = sb("wd", [D_EDGE + 1, 2 * D], f32)
        self.w3 = sb("w3", [P, 2, D_HEAD], f32)
        self.wlr = sb("wlr", [D_HEAD, D_HEAD + 2 * HEADS], f32)
        self.bias = sb("bias", [P, BIAS_W], f32)
        self.iota_f = sb("iota_f", [P, P], f32)
        self.iota_b = sb("iota_b", [P, P], bf16)
        self.iota_slot = sb("iota_slot", [P, SLOT_TILES], bf16)
        self.ident = sb("ident", [P, P], f32)
        self.ident_b = sb("ident_b", [P, P], bf16)
        self.lower = sb("lower", [P, P], f32)
        self.ones = sb("ones", [P, P], f32)
        self.ones_last = sb("ones_last", [P, P], f32)
        self.eps = sb("eps", [P, 3], f32)
        self.idx_s = sb("idx_s", [P, SLOT_TILES], i32)
        self.idx_d1 = sb("idx_d1", [P, SLOT_TILES], i32)
        self.idx_d2 = sb("idx_d2", [P, SLOT_TILES], i32)
        self.lo_s = sb("lo_s", [P, SLOT_TILES], f32)
        self.lo_d = sb("lo_d", [P, SLOT_TILES], f32)
        self.nt_s = sb("nt_s", [1, SLOT_TILES], i32)
        self.nt_d = sb("nt_d", [1, SLOT_TILES], i32)
        self.bank = [ps(f"bank{k}", [P, 512], f32) for k in range(8)]
        self.ix = sb("ix", [P, UH], i32)
        self.EL = sb("EL", [P, NODE_TILES, HEADS], f32)
        self.mv = sb("mv", [P, NODE_TILES, 2], f32)
        self.st = sb("st", [P, NODE_TILES, 6], f32)
        self.rs = sb("rs", [P, NODE_TILES], f32)
        self.nmr = sb("nmr", [P, NODE_TILES], f32)
        self.s_rows = [self.sem(f"s_rows{k}") for k in range(UH)]
        self.rows_base = [0] * UH
        self.s_ix, self.s_go = self.sem("s_ix"), self.sem("s_go")
        self.ix_base = 0
        self.s_store = [self.sem(f"s_store{k}") for k in range(NK)]
        self.store_base = 0
        self.s_st, self.s_sq, self.s_rs = self.sem("s_stats"), self.sem("s_sqrt"), self.sem("s_rstd")
        self.norms = 0
        self.own = Own(self.sem("s_own"))

    def sb(self, name, shape, dt):
        return self.ctx.enter_context(self.nc.sbuf_tensor(name, shape, dt))

    def ps(self, name, shape, dt):
        return self.ctx.enter_context(self.nc.psum_tensor(name, shape, dt))

    def sem(self, name):
        return self.ctx.enter_context(self.nc.semaphore(name))

    def b(self, name):
        return self.bias[:, BIAS[name][0]:BIAS[name][1]]


class Own:

    def __init__(self, sem):
        self.sem, self.n = sem, 0

    def __call__(self, ins):
        self.n += 1
        ins.then_inc(self.sem, 1)
        return self.n


class Carve:

    def __init__(self, work):
        self.work, self.n = work, 0

    def __call__(self, *shape, dt=f32):
        n = int(np.prod(shape))
        words = n if dt != bf16 else (n + 1) // 2
        v = self.work[:, self.n:self.n + words]
        self.n += words
        assert self.n <= WORK, self.n
        if dt != f32:
            v = v.bitcast(dt)
        names = "abcd"[:len(shape)]
        if len(shape) > 1:
            v = v.rearrange(f"p ({' '.join(names)}) -> p {' '.join(names)}", **dict(zip(names, shape)))
        return v


def rank_stage(nc, c, src, dst, typ, wgt, x, weights, att_rows, prep):
    s_key, s_load, s_zero, s_fill = c.sem("s_key"), c.sem("s_load"), c.sem("s_zero"), c.sem("s_fill")
    s_const, s_mm, s_off, s_sin, s_turn = (c.sem("s_const"), c.sem("s_rank_mm"), c.sem("s_rank_cnt"), c.sem("s_sin"),
                                   c.sem("s_turn"))
    s_cst = c.sem("s_cst_own")
    onehot = c.Q[:, :, :].rearrange("p a b -> p (a b)").bitcast(bf16)[:, 0:NODE_TILES * EDGE_COLS]
    scan = c.work[:, 0:NODE_TILES * EDGE_COLS]
    onehot3 = onehot.rearrange("p (b t) -> p b t", b=NODE_TILES)
    scan3 = scan.rearrange("p (b t) -> p b t", b=NODE_TILES)
    zeros = c.work[:, WORK - 2080:WORK]
    ztiles = 2080 // ROW
    keyI = c.AGG[:, :, :].rearrange("p a b -> p (a b)").bitcast(i32)
    raw = [keyI[:, k * EDGE_COLS:(k + 1) * EDGE_COLS] for k in range(3)]
    tmpI = [keyI[:, (3 + k) * EDGE_COLS:(4 + k) * EDGE_COLS] for k in range(2)]
    aggF = c.AGG[:, :, :].rearrange("p a b -> p (a b)")
    w_in = aggF[:, 5 * EDGE_COLS:6 * EDGE_COLS]
    tF = [aggF[:, (6 + k) * EDGE_COLS:(7 + k) * EDGE_COLS] for k in range(6)]
    small = prep["sb"]("rank_small", [P, 8, NODE_TILES + 1], f32)
    smallI = prep["sb"]("rank_smallI", [P, NODE_TILES], i32)
    bucket = prep["sb"]("bucket", [P, NODE_TILES], f32)
    tile_no = prep["sb"]("tile_no", [1, SLOT_TILES], f32)
    tiles_f = prep["sb"]("tiles_f", [1, SLOT_TILES], f32)
    n_loads = len(weights) + 1

    with nc.Block() as block:
        @block.sync
        def _(sp):
            for k, a in enumerate((src, dst, typ)):
                sp.dma_start(raw[k], a[:, :]).then_inc(s_key, 16)
            sp.dma_start(w_in, wgt[:, :]).then_inc(s_key, 16)
            sp.wait_ge(s_zero, 1)
            dest = att_rows.rearrange("(p r) c -> p (r c)", p=P)
            fills = SLOT_TILES // ztiles
            for k in range(fills):
                sp.dma_start(dest[:, k * 2080:(k + 1) * 2080], zeros).then_inc(s_fill, 16)
            sp.dma_start(c.X[:, :, :], x.rearrange("(i p) d -> p i d", p=P)).then_inc(s_load, 16)
            for into, a in weights:
                sp.dma_start(into, a).then_inc(s_load, 16)
            sp.wait_ge(s_fill, 16 * fills)
            sp.wait_ge(s_load, 16 * n_loads)

        @block.gpsimd
        def _(p):
            n = [0]

            def own(ins):
                n[0] += 1
                ins.then_inc(s_cst, 1)
                p.wait_ge(s_cst, n[0])

            nc.gpsimd.memset(zeros, 0.0).then_inc(s_zero, 1)
            nc.gpsimd.memset(c.ones[:], 1.0).then_inc(s_const, 1)
            nc.gpsimd.iota(bucket[:], [[1, NODE_TILES]], base=0, channel_multiplier=0,
                           allow_small_or_imprecise_dtypes=True).then_inc(s_const, 1)
            nc.gpsimd.iota(tile_no[:], [[1, SLOT_TILES]], base=0, channel_multiplier=0,
                           allow_small_or_imprecise_dtypes=True).then_inc(s_const, 1)
            nc.gpsimd.iota(c.iota_f[:], [[1, P]], base=0, channel_multiplier=0,
                           allow_small_or_imprecise_dtypes=True).then_inc(s_const, 1)
            nc.gpsimd.iota(c.iota_b[:], [[1, P]], base=0, channel_multiplier=0,
                           allow_small_or_imprecise_dtypes=True).then_inc(s_const, 1)
            nc.gpsimd.iota(c.iota_slot[:], [[1, SLOT_TILES]], base=-(SLOT_TILES // 2), channel_multiplier=0,
                           allow_small_or_imprecise_dtypes=True).then_inc(s_const, 1)
            own(nc.gpsimd.memset(c.lower[:], 0.0))
            nc.gpsimd.affine_select(out=c.lower[:], in_=c.lower[:], compare_op=ALU.is_ge, fill=1.0, base=0,
                                    pattern=[[-1, P]], channel_multiplier=1).then_inc(s_const, 1)
            own(nc.gpsimd.memset(c.ident[:], 0.0))
            nc.gpsimd.affine_select(out=c.ident[:], in_=c.ident[:], compare_op=ALU.not_equal, fill=1.0, base=0,
                                    pattern=[[-1, P]], channel_multiplier=1).then_inc(s_const, 1)
            own(nc.gpsimd.memset(c.ident_b[:], 0.0))
            nc.gpsimd.affine_select(out=c.ident_b[:], in_=c.ident_b[:], compare_op=ALU.not_equal, fill=1.0,
                                    base=0, pattern=[[-1, P]], channel_multiplier=1).then_inc(s_const, 1)
            own(nc.gpsimd.memset(c.ones_last[:], 1.0))
            nc.gpsimd.affine_select(out=c.ones_last[:], in_=c.ones_last[:], compare_op=ALU.is_ge, fill=0.0,
                                    base=LAST_ROWS - 1, pattern=[[0, P]],
                                    channel_multiplier=-1).then_inc(s_const, 1)
            nc.gpsimd.memset(c.eps[:, 0:1], LN_EPS).then_inc(s_const, 1)
            nc.gpsimd.memset(c.eps[:, 1:2], float(np.pi / 2)).then_inc(s_const, 1)
            nc.gpsimd.memset(c.eps[:, 2:3], BN_EPS).then_inc(s_const, 1)

        @block.scalar
        def _(act):
            act.wait_ge(s_turn, 1)
            nc.scalar.activation(tF[1], tF[0], ACT.Sin, bias=c.eps[:, 1:2],
                                 scale=-2.0 * float(np.pi)).then_inc(s_sin, 1)

        @block.tensor
        def _(pe):
            pe.wait_ge(s_const, 13)
            for k in range(2):
                pe.wait_ge(s_off, k + 1)
                cnt = small[:, 1, 0:NODE_TILES]
                nc.tensor.matmul(c.bank[0][:, 0:NODE_TILES], c.lower[:], cnt, start=True, stop=True)
                nc.tensor.matmul(c.bank[1][:, 0:NODE_TILES], c.ones[:], cnt, start=True,
                                 stop=True).then_inc(s_mm, 1)

        @block.vector
        def _(v):
            def own(ins):
                v.wait_ge(c.own.sem, c.own(ins))

            V = nc.vector
            v.wait_ge(s_key, 64)
            v.wait_ge(s_const, 13)
            own(V.tensor_scalar(tF[0], w_in, 0.1, None, ALU.mult))
            own(V.tensor_copy(tmpI[0], tF[0]))
            own(V.tensor_copy(tF[1], tmpI[0]))
            own(V.tensor_tensor(tF[0], tF[0], tF[1], ALU.subtract))
            own(V.scalar_tensor_tensor(out=tF[0], in0=tF[0], scalar=-1.0, in1=tF[0], op0=ALU.mult, op1=ALU.max))
            own(V.tensor_scalar(tF[1], tF[0], -1.0, 1.0, ALU.mult, ALU.add))
            own(V.tensor_tensor(tF[0], tF[0], tF[1], ALU.min))
            V.tensor_scalar(tF[2], w_in, 5.0, 0.5, ALU.is_lt, ALU.mult).then_inc(s_turn, 1)
            v.wait_ge(s_sin, 1)
            own(V.tensor_scalar(tF[1], tF[1], 1.0, None, ALU.add))
            own(V.tensor_tensor(prep["cut"][:], tF[1], tF[2], ALU.mult))
            for k, (key, other, nt) in enumerate((("src", "dst", c.nt_s), ("dst", "src", c.nt_d))):
                me, ot = (raw[0], raw[1]) if k == 0 else (raw[1], raw[0])
                own(V.tensor_scalar(tmpI[0], me, 7, None, ALU.logical_shift_right))
                own(V.tensor_scalar(tmpI[1], me, P - 1, None, ALU.bitwise_and))
                own(V.tensor_copy(tF[0], tmpI[0]))
                own(V.tensor_copy(tF[1], tmpI[1]))
                own(V.tensor_tensor(onehot3, tF[0].unsqueeze(1).broadcast_to([P, NODE_TILES, EDGE_COLS]),
                                    bucket[:].unsqueeze(2).broadcast_to([P, NODE_TILES, EDGE_COLS]),
                                    ALU.is_equal))
                own(V.tensor_tensor_scan(scan, onehot, onehot, 0.0, ALU.add, ALU.max))
                own(V.memset(small[:, 0, 0:1], 0.0))
                own(V.tensor_copy(small[:, 0, 1:NODE_TILES + 1], scan3[:, :, EDGE_COLS - 1]))
                own(V.tensor_tensor(small[:, 1, 0:NODE_TILES], small[:, 0, 1:NODE_TILES + 1],
                                    small[:, 0, 0:NODE_TILES], ALU.subtract))
                V.memset(small[:, 7, 0:1], 0.0).then_inc(s_off, 1)
                v.wait_ge(s_mm, k + 1)
                own(V.tensor_scalar(small[:, 2, 0:NODE_TILES], c.bank[1][:, 0:NODE_TILES], float(P - 1), None,
                                    ALU.add))
                own(V.tensor_copy(smallI[:], small[:, 2, 0:NODE_TILES]))
                own(V.tensor_scalar(smallI[:], smallI[:], 7, None, ALU.logical_shift_right))
                own(V.tensor_copy(small[:, 2, 0:NODE_TILES], smallI[:]))
                own(V.tensor_tensor_scan(small[:, 3, 0:NODE_TILES], small[:, 2, 0:NODE_TILES],
                                         small[:, 2, 0:NODE_TILES], 0.0, ALU.add, ALU.max))
                own(V.tensor_tensor(small[:, 4, 0:NODE_TILES], small[:, 3, 0:NODE_TILES],
                                    small[:, 2, 0:NODE_TILES], ALU.subtract))
                own(V.scalar_tensor_tensor(out=small[:, 4, 0:NODE_TILES], in0=small[:, 4, 0:NODE_TILES],
                                           scalar=float(P), in1=c.bank[0][:, 0:NODE_TILES], op0=ALU.mult,
                                           op1=ALU.add))
                own(V.tensor_tensor(small[:, 4, 0:NODE_TILES], small[:, 4, 0:NODE_TILES],
                                    small[:, 0, 0:NODE_TILES], ALU.subtract))
                own(V.tensor_scalar(small[:, 4, 0:NODE_TILES], small[:, 4, 0:NODE_TILES], -1.0, None, ALU.add))
                own(V.tensor_tensor(scan3, scan3,
                                    small[:, 4, 0:NODE_TILES].unsqueeze(2).broadcast_to(
                                        [P, NODE_TILES, EDGE_COLS]), ALU.add))
                own(V.tensor_tensor(scan, scan, onehot, ALU.mult))
                own(V.tensor_reduce(tF[2], scan3.rearrange("p b t -> p t b"), AXX, ALU.add))
                own(V.tensor_copy(tmpI[0], tF[2]))
                if k == 1:
                    own(V.tensor_copy(prep["slot_d"][:], tmpI[0]))
                own(V.tensor_scalar(tmpI[1], tmpI[0], P - 1, None, ALU.bitwise_and))
                own(V.tensor_copy(prep["pos_lo"][:, k, :], tmpI[1]))
                own(V.tensor_scalar(tmpI[1], tmpI[0], 7, None, ALU.logical_shift_right))
                own(V.tensor_scalar(prep["pos_hi"][:, k, :], tmpI[1], float(-(SLOT_TILES // 2)), None, ALU.add))
                own(V.tensor_copy(tF[3], ot))
                if k == 0:
                    own(V.scalar_tensor_tensor(out=tF[3], in0=tF[3], scalar=-float(2 * P), in1=tF[1],
                                               op0=ALU.mult, op1=ALU.subtract))
                    own(V.tensor_scalar(tmpI[0], tF[3], float(PAD_NODE * 2 * P + P), None, ALU.add))
                else:
                    own(V.scalar_tensor_tensor(out=tF[3], in0=tF[3], scalar=-float(2 * P * N_RELS), in1=tF[1],
                                               op0=ALU.mult, op1=ALU.subtract))
                    own(V.tensor_copy(tF[4], raw[2]))
                    own(V.scalar_tensor_tensor(out=tF[3], in0=tF[4], scalar=float(2 * P), in1=tF[3],
                                               op0=ALU.mult, op1=ALU.add))
                    own(V.tensor_scalar(tmpI[0], tF[3], float(PAD_NODE * N_RELS * 2 * P + P), None, ALU.add))
                for j in range(3):
                    own(V.tensor_scalar(tmpI[1], tmpI[0], 8 * j, 255, ALU.logical_shift_right,
                                        ALU.bitwise_and))
                    own(V.tensor_copy(prep["part"][:, k, j, :], tmpI[1]))
                cmp = c.work[0:1, 0:SLOT_TILES * (NODE_TILES - 1)].rearrange("p (t b) -> p t b",
                                                                               b=NODE_TILES - 1)
                own(V.tensor_tensor(cmp, small[0:1, 3, 0:NODE_TILES - 1].unsqueeze(1).broadcast_to(
                    [1, SLOT_TILES, NODE_TILES - 1]), tile_no[:].unsqueeze(2).broadcast_to(
                        [1, SLOT_TILES, NODE_TILES - 1]), ALU.is_le))
                own(V.tensor_reduce(tiles_f[:], cmp, AXX, ALU.add))
                own(V.tensor_copy(nt[:], tiles_f[:]))


def place_stage(nc, c, attr, att_rows, prep):
    S4 = 4
    cv = Carve(c.work)
    hi1 = cv(S4, 2, SLOT_TILES, dt=bf16)
    lo1 = cv(S4, 2, 3, P, dt=bf16)
    zero = cv(512, dt=bf16)
    rows = cv(U, ROW)
    tmp = cv(SLOT_TILES)
    vI = cv(SLOT_TILES, dt=i32)
    wI = cv(SLOT_TILES, dt=i32)
    s_z, s_oh, s_acc, s_ixc, s_done = c.sem("s_place_zero"), c.sem("s_place_oh"), c.sem("s_place_mm"), c.s_ix, c.s_go
    s_row = [c.sem(f"s_row{h}") for h in range(2)]
    s_sc = c.s_rows
    loops = EDGE_COLS // U
    c.rows_base[0:U], c.ix_base = [16 * loops] * U, 2 * loops

    with nc.Block() as block:
        @block.sync
        def _(sp):
            def load(it, h):
                sp.dma_start(rows[:, G * h:G * h + G, 0:D_EDGE],
                             attr[:, at(it * U + G * h, G), :]).then_inc(s_row[h], 16)
            for h in range(2):
                load(0, h)
            with sp.Fori(1, loops) as it:
                for h in range(2):
                    for k in range(G * h, G * h + G):
                        sp.wait_ge(s_sc[k], it * 16)
                    load(it, h)

        @block.scalar
        def _(act):
            def fill(it, h):
                nc.scalar.copy(rows[:, G * h:G * h + G, D_EDGE:ROW].rearrange("p a b -> p (a b)"),
                               prep["cut"][:, at(it * U + G * h, G)])
                nc.scalar.copy(c.ix[:, G * h:G * h + G],
                               prep["slot_d"][:, at(it * U + G * h, G)]).then_inc(s_ixc, 1)
            for h in range(2):
                fill(0, h)
            with act.Fori(1, loops) as it:
                for h in range(2):
                    for k in range(G * h, G * h + G):
                        act.wait_ge(s_sc[k], it * 16)
                    fill(it, h)

        @block.gpsimd
        def _(p):
            with p.Fori(0, loops) as it:
                for h in range(2):
                    p.wait_ge(s_row[h], it * 16 + 16)
                    p.wait_ge(s_ixc, it * 2 + h + 1)
                    p.sem_inc(s_done, 1)
                    for k in range(G * h, G * h + G):
                        p.indirect_dma_start(att_rows, bass.IndirectOffsetOnAxis(ap=c.ix[:, k:k + 1], axis=0),
                                             rows[:, k, :], None).then_inc(s_sc[k], 16)
            for k in range(U):
                p.wait_ge(s_sc[k], 16 * loops)

        @block.tensor
        def _(pe):
            pe.wait_ge(s_z, 1)
            for k in range(6):
                nc.tensor.matmul(c.bank[k][:, 0:SLOT_TILES], zero[:, 0:P], zero[:, 0:SLOT_TILES], start=True,
                                 stop=False, skip_group_check=True)
            with pe.Fori(0, EDGE_COLS // S4) as it:
                for s in range(S4):
                    pe.wait_ge(s_oh, it * S4 + s + 1)
                    for k in range(2):
                        for j in range(3):
                            mm = nc.tensor.matmul(c.bank[3 * k + j][:, 0:SLOT_TILES], lo1[:, s, k, j, :],
                                                  hi1[:, s, k, :], start=False, stop=False,
                                                  skip_group_check=True)
                    mm.then_inc(s_acc, 1)
            for k in range(6):
                mm = nc.tensor.matmul(c.bank[k][:, 0:SLOT_TILES], zero[:, 0:P], zero[:, 0:SLOT_TILES], start=False,
                                      stop=True, skip_group_check=True)
            mm.then_inc(s_acc, 1)

        @block.vector
        def _(v):
            V = nc.vector
            V.memset(zero, 0.0).then_inc(s_z, 1)

            def onehots(it, first):
                for s in range(S4):
                    t = it * S4 + s
                    if not first:
                        v.wait_ge(s_acc, t - S4 + 1)
                    for k in range(2):
                        V.tensor_scalar(hi1[:, s, k, :], c.iota_slot[:], prep["pos_hi"][:, k, at(t)], None,
                                        ALU.is_equal)
                        for j in range(3):
                            ins = V.tensor_scalar(lo1[:, s, k, j, :], c.iota_b[:], prep["pos_lo"][:, k, at(t)],
                                                  prep["part"][:, k, j, at(t)], ALU.is_equal, ALU.mult)
                    ins.then_inc(s_oh, 1)
            onehots(0, True)
            with v.Fori(1, EDGE_COLS // S4) as it:
                onehots(it, False)

            def own(ins):
                v.wait_ge(c.own.sem, c.own(ins))
            v.wait_ge(s_acc, EDGE_COLS + 1)
            for k in range(2):
                own(V.tensor_copy(tmp, c.bank[3 * k][:, 0:SLOT_TILES]))
                own(V.scalar_tensor_tensor(out=tmp, in0=c.bank[3 * k + 1][:, 0:SLOT_TILES], scalar=256.0, in1=tmp,
                                           op0=ALU.mult, op1=ALU.add))
                own(V.scalar_tensor_tensor(out=vI, in0=c.bank[3 * k + 2][:, 0:SLOT_TILES], scalar=65536.0, in1=tmp,
                                           op0=ALU.mult, op1=ALU.add))
                own(V.tensor_scalar(wI, vI, 2 * P - 1, None, ALU.bitwise_and))
                own(V.tensor_scalar((c.lo_s, c.lo_d)[k][:], wI, -1.0, float(P), ALU.mult, ALU.add))
                own(V.tensor_scalar(vI, vI, 8, None, ALU.logical_shift_right))
                if k == 0:
                    own(V.tensor_scalar(c.idx_s[:], vI, -1.0, float(PAD_NODE), ALU.mult, ALU.add))
                else:
                    own(V.tensor_scalar(wI, vI, N_RELS - 1, None, ALU.bitwise_and))
                    own(V.tensor_copy(tmp, wI))
                    own(V.tensor_scalar(vI, vI, 3, None, ALU.logical_shift_right))
                    own(V.tensor_scalar(c.idx_d2[:], vI, -1.0, float(PAD_NODE), ALU.mult, ALU.add))
                    own(V.scalar_tensor_tensor(out=c.idx_d1[:], in0=c.idx_d2[:], scalar=float(N_RELS), in1=tmp,
                                               op0=ALU.mult, op1=ALU.add))


class Norm:

    def __init__(self, nc, c):
        self.nc, self.c, self.n = nc, c, c.norms
        c.norms += 1

    def vector(self, v, of, before=None):
        nc, c = self.nc, self.c
        with v.Fori(0, NODE_TILES // NK) as it:
            for k in range(NK):
                i = it * NK + k
                if before:
                    before(v, i)
                nc.vector.bn_stats(c.st[:, at(i), :], of[:, at(i), 0:D]).then_inc(c.s_st, 1)
        v.wait_ge(c.s_st, (NODE_TILES + 1) * self.n + NODE_TILES)

        def own(ins):
            v.wait_ge(c.own.sem, c.own(ins))
        mean, var, diff = c.mv[:, :, 0], c.mv[:, :, 1], c.rs[:]
        own(nc.vector.tensor_tensor(diff, c.st[:, :, 1], c.st[:, :, 4], ALU.subtract))
        own(nc.vector.tensor_tensor(mean, c.st[:, :, 1], c.st[:, :, 4], ALU.add))
        own(nc.vector.tensor_scalar(mean, mean, 0.5, None, ALU.mult))
        own(nc.vector.scalar_tensor_tensor(out=diff, in0=diff, scalar=D / 4.0, in1=diff, op0=ALU.mult,
                                           op1=ALU.mult))
        own(nc.vector.tensor_tensor(var, c.st[:, :, 2], c.st[:, :, 5], ALU.add))
        nc.vector.tensor_tensor(var, var, diff, ALU.add).then_inc(c.s_st, 1)
        v.wait_ge(c.s_sq, self.n + 1)
        nc.vector.reciprocal(c.rs[:], c.rs[:]).then_inc(c.s_rs, 1)
        v.wait_ge(c.s_rs, 2 * self.n + 1)
        nc.vector.scalar_tensor_tensor(out=c.nmr[:], in0=c.mv[:, :, 0], scalar=-1.0, in1=c.rs[:],
                                       op0=ALU.mult, op1=ALU.mult).then_inc(c.s_rs, 1)

    def scalar(self, act):
        act.wait_ge(self.c.s_st, (NODE_TILES + 1) * (self.n + 1))
        self.nc.scalar.activation(self.c.rs[:], self.c.mv[:, :, 1], ACT.Sqrt, bias=self.c.eps[:, 0:1],
                                  scale=1.0 / D).then_inc(self.c.s_sq, 1)

    def ready(self, eng):
        eng.wait_ge(self.c.s_rs, 2 * self.n + 2)


class Product:

    def __init__(self, nc, c, name, carve, chunks, first_bank=2):
        self.nc, self.c, self.chunks, self.fb = nc, c, chunks, first_bank
        self.h = carve(NK, D)
        self.hT = carve(NK, 2, P)
        self.s_h, self.s_tp, self.s_ht = (c.sem(f"s_{name}_h"), c.sem(f"s_{name}_tp"), c.sem(f"s_{name}_ht"))
        self.s_mm = [c.sem(f"s_{name}_mm{q}") for q in range(len(chunks))]
        self.s_ev = [c.sem(f"s_{name}_ev{q}") for q in range(len(chunks))]

    def loop(self, eng, body):
        last = NODE_TILES // NK - 1
        body(0, True)
        with eng.Fori(1, last) as it:
            body(it, False)
        body(last, False)

    def products(self, pe, i, k):
        for q, (w, n, _, _) in enumerate(self.chunks):
            wait(pe, self.s_ev[q], i)
            for z in range(2):
                mm = self.nc.tensor.matmul(self.c.bank[self.fb + q][:, 0:n], self.hT[:, k, z, :], w[:, z, :],
                                           start=(z == 0), stop=(z == 1))
            mm.then_inc(self.s_mm[q], 1)

    def tensor(self, pe, ready=None):
        def body(it, first):
            for k in range(NK):
                i = it * NK + k
                pe.wait_ge(ready or self.s_h, i + 1)
                wait(pe, self.s_ht, i)
                for q in range(2):
                    mm = self.nc.tensor.transpose(self.c.bank[0][:, q * P:(q + 1) * P],
                                                  self.h[:, k, q * P:(q + 1) * P], self.c.ident[:])
                mm.then_inc(self.s_tp, 1)
                pe.wait_ge(self.s_ht, i + 1)
                self.products(pe, i, k)
        self.loop(pe, body)

    def take(self, eng, name, it, i, k):
        for q, (_, n, who, f) in enumerate(self.chunks):
            if who == name:
                eng.wait_ge(self.s_mm[q], i + 1)
                f(eng, it, i, k, self.c.bank[self.fb + q][:, 0:n]).then_inc(self.s_ev[q], 1)

    def ahead(self, eng, name, begin):
        begin(0, 0)

        def body(it, first):
            for k in range(NK):
                i = it * NK + k
                if not (isinstance(i, int) and i == NODE_TILES - 1):
                    begin(i + 1, (k + 1) % NK)
                self.take(eng, name, it, i, k)
        self.loop(eng, body)

    def scalar(self, act, make):
        def begin(i, k):
            wait(act, self.s_tp, i - NK + 1)
            make(i, self.h[:, k, :]).then_inc(self.s_h, 1)
        self.ahead(act, "act", begin)

    def vector(self, v, finish=None):
        def begin(i, k):
            if finish:
                v.wait_ge(self.s_h, i + 1)
                finish(i, self.h[:, k, :])
            v.wait_ge(self.s_tp, i + 1)
            self.nc.vector.tensor_copy(self.hT[:, k, :, :].rearrange("p a b -> p (a b)"),
                                       self.c.bank[0][:, 0:2 * P]).then_inc(self.s_ht, 1)
        self.ahead(v, "dve", begin)


def flat(ap):
    return ap.rearrange("p a b -> p (a b)")


def normed(nc, c, of, func):
    return lambda i, out: nc.scalar.activation(out, flat(of[:, at(i), 0:D]), func, bias=c.nmr[:, at(i)],
                                               scale=c.rs[:, at(i)])


class Store:

    def __init__(self, c, rows, table, signals):
        self.rows, self.table, self.signals = rows, table, signals
        self.s, self.base = c.s_store, c.store_base
        c.store_base += 16 * (NODE_TILES // NK)

    def free(self, eng, it, k):
        wait(eng, self.s[k], it * 16 + self.base)

    def sync(self, sp):
        with sp.Fori(0, NODE_TILES // NK) as it:
            for k in range(NK):
                i = it * NK + k
                for s in self.signals:
                    sp.wait_ge(s, i + 1)
                sp.dma_start(self.table[at(i * P, P), :], self.rows(k)).then_inc(self.s[k], 16)
        for k in range(NK):
            sp.wait_ge(self.s[k], self.base + 16 * (NODE_TILES // NK))


def node_stage_0(nc, c, table):
    cv = Carve(c.work)
    out = cv(NK, D)
    b12 = cv(D)
    s_b, s_x = c.sem("s_n0_b"), c.sem("s_n0_x")
    norm = Norm(nc, c)

    def keep_x(v, it, i, k, ps):
        nc.vector.tensor_tensor(c.X[:, at(i), :], ps.unsqueeze(1), c.X[:, at(i), :], ALU.add).then_inc(s_x, 1)
        v.wait_ge(s_x, i + 1)
        return nc.vector.tensor_tensor(c.X[:, at(i), :], c.X[:, at(i), :], b12.unsqueeze(1), ALU.add)

    def keep_table(act, it, i, k, ps):
        store.free(act, it, k)
        return nc.scalar.copy(out[:, k, :], ps)

    prod = Product(nc, c, "n0", cv, [(c.w12[:, :, 0:D], D, "dve", keep_x),
                                     (c.w12[:, :, D:2 * D], D, "act", keep_table)])
    store = Store(c, lambda k: out[:, k, :], table, [prod.s_ev[1]])

    with nc.Block() as block:
        @block.vector
        def _(v):
            nc.vector.tensor_tensor(b12, c.b("b1"), c.b("b2"), ALU.add).then_inc(s_b, 1)
            norm.vector(v, c.X)
            v.wait_ge(s_b, 1)
            prod.vector(v)

        @block.scalar
        def _(act):
            norm.scalar(act)
            norm.ready(act)
            prod.scalar(act, normed(nc, c, c.X, ACT.Relu))

        @block.tensor
        def _(pe):
            prod.tensor(pe)

        @block.sync
        def _(sp):
            store.sync(sp)


def node_stage_1(nc, c, table):
    cv = Carve(c.work)
    out = cv(NK, N_RELS * D)
    cinv = c.sb("cinv", [P, NODE_TILES], f32)
    s_c = c.sem("s_n1_c")
    s_x = c.sem("s_n1_x")
    norm = Norm(nc, c)

    def add_mean(v, i):
        nc.vector.scalar_tensor_tensor(out=c.X[:, at(i), :], in0=c.AGG[:, at(i), 0:D], scalar=cinv[:, at(i)],
                                       in1=c.X[:, at(i), :], op0=ALU.mult, op1=ALU.add).then_inc(s_x, 1)
        v.wait_ge(s_x, i + 1)

    def keep(q):
        def f(eng, it, i, k, ps):
            store.free(eng, it, k)
            o = out[:, k, q * 2 * D:(q + 1) * 2 * D]
            return nc.scalar.copy(o, ps) if q % 2 == 0 else nc.vector.tensor_copy(o, ps)
        return f

    prod = Product(nc, c, "n1", cv, [(c.wrel[:, :, q * 2 * D:(q + 1) * 2 * D], 2 * D, ("act", "dve")[q % 2], keep(q))
                                     for q in range(N_RELS // 2)])
    store = Store(c, lambda k: out[:, k, :], table, prod.s_ev)

    with nc.Block() as block:
        @block.vector
        def _(v):
            nc.vector.tensor_scalar(cinv[:], c.AGG[:, :, D], 1.0, None, ALU.max).then_inc(s_c, 1)
            v.wait_ge(s_c, 1)
            nc.vector.reciprocal(cinv[:], cinv[:]).then_inc(s_c, 1)
            v.wait_ge(s_c, 2)
            norm.vector(v, c.X, add_mean)
            prod.vector(v)

        @block.scalar
        def _(act):
            norm.scalar(act)
            norm.ready(act)
            prod.scalar(act, normed(nc, c, c.X, ACT.Relu))

        @block.tensor
        def _(pe):
            prod.tensor(pe)

        @block.sync
        def _(sp):
            store.sync(sp)


def batch_norm_stage(nc, c):
    cv = Carve(c.work)
    sq = cv(NODE_TILES, D)
    neg_mean, scale = cv(D), cv(D)
    s_sum, s_nm, s_cen, s_sq, s_std = (c.sem("s_bn_sum"), c.sem("s_bn_nm"), c.sem("s_bn_cen"), c.sem("s_bn_sq"),
                                       c.sem("s_bn_std"))
    agg = c.AGG[:, :, 0:D]

    with nc.Block() as block:
        @block.tensor
        def _(pe):
            def column_sums(bank, of):
                nc.tensor.matmul(bank[:, 0:D], c.ones[:], of[:, 0, 0:D], start=True, stop=False)
                with pe.Fori(1, NODE_TILES - 1) as i:
                    nc.tensor.matmul(bank[:, 0:D], c.ones[:], of[:, at(i), 0:D], start=False, stop=False)
                nc.tensor.matmul(bank[:, 0:D], c.ones_last[:], of[:, NODE_TILES - 1, 0:D], start=False,
                                 stop=True).then_inc(s_sum, 1)
            column_sums(c.bank[0], c.AGG)
            pe.wait_ge(s_sq, 1)
            column_sums(c.bank[1], sq)

        @block.scalar
        def _(act):
            act.wait_ge(s_sum, 1)
            nc.scalar.mul(neg_mean, c.bank[0][:, 0:D], -1.0 / N_NODES).then_inc(s_nm, 1)
            act.wait_ge(s_cen, 1)
            nc.scalar.activation(sq, agg, ACT.Square).then_inc(s_sq, 1)
            act.wait_ge(s_sum, 2)
            nc.scalar.activation(scale, c.bank[1][:, 0:D], ACT.Sqrt, bias=c.eps[:, 2:3],
                                 scale=1.0 / N_NODES).then_inc(s_std, 1)

        @block.vector
        def _(v):
            def own(ins):
                v.wait_ge(c.own.sem, c.own(ins))

            def rows(ap):
                return ap.unsqueeze(1).broadcast_to([P, NODE_TILES, D])
            v.wait_ge(s_nm, 1)
            nc.vector.tensor_tensor(agg, agg, rows(neg_mean), ALU.add).then_inc(s_cen, 1)
            v.wait_ge(s_std, 1)
            own(nc.vector.reciprocal(scale, scale))
            own(nc.vector.tensor_tensor(scale, scale, c.b("gamma"), ALU.mult))
            own(nc.vector.tensor_tensor(agg, agg, rows(scale), ALU.mult))
            own(nc.vector.tensor_tensor(agg, agg, rows(c.b("beta")), ALU.add))
            own(nc.vector.tensor_tensor(c.X[:, :, :], c.X[:, :, :], agg, ALU.add))


def node_stage_2(nc, c, table):
    cv = Carve(c.work)
    out = cv(NK, 2 * D)
    H = c.AGG
    s_h, s_g, s_hn, s_x = c.sem("s_n2_rows"), c.sem("s_n2_g"), c.sem("s_n2_rows_ready"), c.sem("s_n2_x")
    norm, norm2 = Norm(nc, c), Norm(nc, c)

    def keep_q(act, it, i, k, ps):
        return nc.vector.tensor_tensor(c.Q[:, at(i), :], ps.unsqueeze(1), c.b("bqkv")[:, 0:D].unsqueeze(1), ALU.add)

    def keep_kv(v, it, i, k, ps):
        store.free(v, it, k)
        return nc.vector.tensor_tensor(out[:, k, :], ps, c.b("bqkv")[:, D:3 * D], ALU.add)

    prod = Product(nc, c, "n2", cv, [(c.wqkv[:, :, 0:D], D, "dve", keep_q),
                                     (c.wqkv[:, :, D:3 * D], 2 * D, "dve", keep_kv)])
    store = Store(c, lambda k: out[:, k, :], table, [prod.s_ev[1]])

    with nc.Block() as block:
        @block.vector
        def _(v):
            norm.vector(v, c.X)
            v.wait_ge(s_h, NODE_TILES)
            norm2.vector(v, H)
            nc.vector.tensor_tensor(c.X[:, :, :], c.X[:, :, :], H[:, :, 0:D], ALU.add).then_inc(s_x, 1)
            v.wait_ge(s_x, 1)
            nc.vector.tensor_tensor(c.X[:, :, :], c.X[:, :, :],
                                    c.b("bo").unsqueeze(1).broadcast_to([P, NODE_TILES, D]),
                                    ALU.add).then_inc(s_x, 1)

            def gain_and_bias(i, rows):
                nc.vector.tensor_tensor(rows, rows, c.b("ln_g"), ALU.mult).then_inc(s_g, 1)
                v.wait_ge(s_g, i + 1)
                nc.vector.tensor_tensor(rows, rows, c.b("ln_b"), ALU.add).then_inc(s_hn, 1)
            prod.vector(v, gain_and_bias)

        @block.scalar
        def _(act):
            norm.scalar(act)
            norm.ready(act)
            make = normed(nc, c, c.X, ACT.Relu)
            with act.Fori(0, NODE_TILES) as i:
                make(i, flat(H[:, at(i), 0:D])).then_inc(s_h, 1)
            norm2.scalar(act)
            norm2.ready(act)
            prod.scalar(act, normed(nc, c, H, ACT.Identity))

        @block.tensor
        def _(pe):
            prod.tensor(pe, s_hn)

        @block.sync
        def _(sp):
            store.sync(sp)


class HeadProduct(Product):

    def products(self, pe, i, k):
        (w, _, _, _), (wlr, n, _, _) = self.chunks
        wait(pe, self.s_ev[0], i)
        for z in range(2):
            mm = self.nc.tensor.matmul(self.c.bank[self.fb][0:D_HEAD, 0:P], w[:, z, :], self.hT[:, k, z, :],
                                       start=(z == 0), stop=(z == 1))
        mm.then_inc(self.s_mm[0], 1)
        pe.wait_ge(self.s_ev[0], i + 1)
        wait(pe, self.s_ev[1], i)
        self.nc.tensor.matmul(self.c.bank[self.fb + 1][:, 0:n], self.xT[0:D_HEAD, k, :], wlr, start=True,
                              stop=True).then_inc(self.s_mm[1], 1)


def node_stage_3(nc, c, table):
    cv = Carve(c.work)
    xT = cv(NK, P)
    out = cv(NK, D_HEAD + 2 * HEADS)
    s_el = c.sem("s_n3_el")
    norm = Norm(nc, c)

    def add_x(v, it, i, k, ps):
        return nc.vector.tensor_tensor(c.X[:, at(i), :], ps.unsqueeze(1), c.X[:, at(i), :], ALU.add)

    def keep_xT(act, it, i, k, ps):
        return nc.scalar.copy(xT[0:D_HEAD, k, :], c.bank[5][0:D_HEAD, 0:P])

    def keep_rows(act, it, i, k, ps):
        store.free(act, it, k)
        return nc.scalar.copy(out[:, k, :], ps)

    back = Product(nc, c, "n3o", cv, [(c.wo, D, "dve", add_x)])
    prod = HeadProduct(nc, c, "n3", cv, [(c.w3, P, "act", keep_xT),
                                         (c.wlr[:, :], D_HEAD + 2 * HEADS, "act", keep_rows)], first_bank=5)
    prod.xT = xT
    store = Store(c, lambda k: out[:, k, 0:D_T3], table, [prod.s_ev[1], s_el])

    with nc.Block() as block:
        @block.vector
        def _(v):
            back.vector(v)
            v.wait_ge(back.s_ev[0], NODE_TILES)
            norm.vector(v, c.X)
            prod.vector(v)

        @block.scalar
        def _(act):
            back.scalar(act, lambda i, o: nc.scalar.copy(o, flat(c.AGG[:, at(i), 0:D])))
            norm.scalar(act)
            norm.ready(act)
            prod.scalar(act, normed(nc, c, c.X, ACT.Relu))

        @block.tensor
        def _(pe):
            back.tensor(pe)
            prod.tensor(pe)

        @block.gpsimd
        def _(p):
            with p.Fori(0, NODE_TILES // NK) as it:
                for k in range(NK):
                    i = it * NK + k
                    p.wait_ge(prod.s_ev[1], i + 1)
                    nc.gpsimd.tensor_copy(c.EL[:, at(i), :], out[:, k, D_T3:D_T3 + HEADS].unsqueeze(1)).then_inc(s_el, 1)

        @block.sync
        def _(sp):
            store.sync(sp)


def output_stage(nc, c, out):
    cv = Carve(c.work)
    CH = NK
    low = cv(2, CH * D)
    rinv = c.sb("rinv", [P, NODE_TILES, HEADS], f32)
    s_low, s_exp, s_y, s_o = c.sem("s_out_low"), c.sem("s_out_exp"), c.sem("s_out_y"), c.sem("s_out_dma")
    n_ch = NODE_TILES // CH

    with nc.Block() as block:
        @block.vector
        def _(v):
            def own(ins):
                v.wait_ge(c.own.sem, c.own(ins))
            V = nc.vector
            own(V.tensor_scalar(rinv[:, :, :], c.AGG[:, :, D:D + HEADS], SUM_EPS, None, ALU.max))
            own(V.reciprocal(rinv[:, :, :], rinv[:, :, :]))

            def begin(g):
                y = c.AGG[:, g * CH:(g + 1) * CH, 0:D]
                for i in range(g * CH, (g + 1) * CH):
                    yh = c.AGG[:, i, 0:D].rearrange("p (h d) -> p h d", h=HEADS)
                    own(V.tensor_tensor(yh, yh, rinv[:, i, :].unsqueeze(2).broadcast_to([P, HEADS, D_HEAD]),
                                        ALU.mult))
                    own(V.tensor_tensor(yh, yh, c.b("b3").unsqueeze(1).broadcast_to([P, HEADS, D_HEAD]), ALU.add))
                if g >= 2:
                    v.wait_ge(s_y, g - 1)
                V.tensor_scalar(low[:, g % 2, :].rearrange("p (a b) -> p a b", a=CH), y, 0.0, None,
                                ALU.min).then_inc(s_low, 1)

            def end(g):
                y = c.AGG[:, g * CH:(g + 1) * CH, 0:D]
                x = c.X[:, g * CH:(g + 1) * CH, :]
                e = low[:, g % 2, :].rearrange("p (a b) -> p a b", a=CH)
                v.wait_ge(s_exp, g + 1)
                own(V.scalar_tensor_tensor(out=y, in0=y, scalar=0.0, in1=e, op0=ALU.max, op1=ALU.add))
                V.scalar_tensor_tensor(out=x, in0=y, scalar=-1.0, in1=x, op0=ALU.add, op1=ALU.add).then_inc(s_y, 1)
            begin(0)
            for g in range(n_ch):
                if g + 1 < n_ch:
                    begin(g + 1)
                end(g)

        @block.scalar
        def _(act):
            for g in range(n_ch):
                act.wait_ge(s_low, g + 1)
                nc.scalar.activation(low[:, g % 2, :], low[:, g % 2, :], ACT.Exp).then_inc(s_exp, 1)

        @block.sync
        def _(sp):
            for g in range(n_ch):
                sp.wait_ge(s_y, g + 1)
                full = CH if g < n_ch - 1 else CH - 1
                r0 = g * CH * P
                sp.dma_start(out[r0:r0 + full * P, :].rearrange("(i p) d -> p i d", p=P),
                             c.X[:, g * CH:g * CH + full, :]).then_inc(s_o, 16)
            sp.dma_start(out[(NODE_TILES - 1) * P:N_NODES, :], c.X[0:LAST_ROWS, NODE_TILES - 1, :]).then_inc(s_o, 16)
            sp.wait_ge(s_o, 16 * (n_ch + 1))


class Gather:

    def __init__(self, nc, c, idx, table, rows, n=U):
        self.nc, self.c, self.idx, self.table, self.rows, self.n = nc, c, idx, table, rows, n
        self.s, self.s_ix, self.s_go = c.s_rows, c.s_ix, c.s_go
        self.base, self.ix_base = list(c.rows_base), c.ix_base
        for k in range(n):
            c.rows_base[k] += 16 * (SLOT_TILES // n)
        c.ix_base += SLOT_TILES // G

    def copy_indices(self, act, it, h):
        for k in range(G * h, G * h + G):
            wait(act, self.s[k], it * 16 + self.base[k])
        self.nc.scalar.copy(self.c.ix[:, G * h:G * h + G], self.idx[:, at(it * self.n + G * h, G)]).then_inc(self.s_ix, 1)

    def gpsimd(self, p, s_used):
        n = self.n

        def body(it, first):
            for k in range(n):
                if k % G == 0:
                    p.wait_ge(self.s_ix, it * (n // G) + (self.ix_base + k // G + 1))
                if not first:
                    p.wait_ge(s_used, (it - 1) * n + k + 1)
                p.sem_inc(self.s_go, 1)
                p.indirect_dma_start(self.rows(k), None, self.table,
                                     bass.IndirectOffsetOnAxis(ap=self.c.ix[:, k:k + 1], axis=0)).then_inc(self.s[k], 16)
        body(0, True)
        with p.Fori(1, SLOT_TILES // n) as it:
            body(it, False)

    def landed(self, eng, it, k):
        eng.wait_ge(self.s[k], it * 16 + (16 + self.base[k]))


def edge_loop(eng, body, n=U):
    last = SLOT_TILES // n - 1
    body(0, True, False)
    with eng.Fori(1, last) as it:
        body(it, False, False)
    body(last, False, True)


def sum_stage(nc, c, name, idx, lo, nt, table, counted):
    W = D + 1 if counted else D
    cv = Carve(c.work)
    rows, onehot = cv(U, W), cv(U, P)
    s_0, s_oh, s_mm, s_add = c.sem(f"s_{name}_zero"), c.sem(f"s_{name}_oh"), c.sem(f"s_{name}_mm"), c.sem(f"s_{name}_add")
    gather = Gather(nc, c, idx, table, lambda k: rows[:, k, 0:D])

    with nc.Block() as block:
        @block.gpsimd
        def _(p):
            gather.gpsimd(p, s_mm)

        @block.scalar
        def _(act):
            gather.copy_indices(act, 0, 0)
            gather.copy_indices(act, 0, 1)
            with act.Fori(1, SLOT_TILES // U) as it:
                for h in range(2):
                    gather.copy_indices(act, it, h)

        @block.tensor
        def _(pe):
            pe.wait_ge(s_0, 2)

            def body(it, first, last):
                for k in range(U):
                    t = it * U + k
                    gather.landed(pe, it, k)
                    pe.wait_ge(s_oh, t + 1)
                    wait(pe, s_add, t - G + 1)
                    nc.tensor.matmul(c.bank[k % G][:, 0:W], onehot[:, k, :], rows[:, k, :], start=True,
                                     stop=True).then_inc(s_mm, 1)
            edge_loop(pe, body)

        @block.vector
        def _(v):
            V = nc.vector
            if counted:
                V.memset(rows[:, :, D:W], 1.0).then_inc(s_0, 1)
            else:
                v.sem_inc(s_0, 1)
            V.memset(c.AGG[:, :, :], 0.0).then_inc(s_0, 1)
            regs = [v.alloc_register(f"{name}_nt{k}") for k in range(U)]

            def build(t, k):
                V.tensor_scalar(onehot[:, k, :], c.iota_f[:], lo[:, at(t)], None, ALU.is_equal).then_inc(s_oh, 1)
            for t in range(G):
                build(t, t)
            v.wait_ge(s_0, 2)

            def body(it, first, last):
                v.load(regs, nt[0:1, at(it * U, U)])
                for k in range(U):
                    t = it * U + k
                    node_tile = v.snap(regs[k], min_val=0, max_val=NODE_TILES - 1)
                    v.wait_ge(s_mm, t + 1)
                    if not (last and k + G >= U):
                        build(t + G, (k + G) % U)
                    wait(v, s_add, t)
                    sums = c.AGG[:, at(node_tile), 0:W]
                    V.tensor_tensor(sums, c.bank[k % G][:, 0:W].unsqueeze(1), sums, ALU.add).then_inc(s_add, 1)
            edge_loop(v, body)


def attention_stage(nc, c, table, att_rows):
    cv = Carve(c.work)
    kv = cv(U, 2 * D)
    dkv = cv(G, 2 * D)
    prod = cv(2, D)
    scratch = cv(2, D)
    msg = cv(U, D)
    att = cv(U, ROW)
    attT = cv(G, P)
    nodeT = cv(G, P)
    onehot = cv(G, P, dt=bf16)
    weighted = cv(G, P)
    dot, act_dot, weight = cv(U), cv(U), cv(U)
    s_0 = c.sem("s_l2_zero")
    s_att = [c.sem(f"s_l2_att{h}") for h in range(2)]
    s_oh, s_tr, s_cp, s_dk, s_q, s_si = (c.sem("s_l2_oh"), c.sem("s_l2_tr"), c.sem("s_l2_cp"), c.sem("s_l2_dk"),
                                 c.sem("s_l2_q"), c.sem("s_l2_si"))
    s_t1, s_dot, s_msg, s_sd, s_w, s_wo, s_mm, s_add = (c.sem("s_l2_t1"), c.sem("s_l2_dot"), c.sem("s_l2_msg"),
                                                       c.sem("s_l2_sd"), c.sem("s_l2_w"), c.sem("s_l2_wo"),
                                                       c.sem("s_l2_mm"), c.sem("s_l2_add"))
    gather = Gather(nc, c, c.idx_d2, table, lambda k: kv[:, k, :])
    b_oT = c.bank[0][:, 0:G * P // 2].bitcast(bf16).rearrange("p (a b) -> p a b", a=G)
    b_aT, b_d, b_q, b_m = c.bank[1], (c.bank[2], c.bank[3]), (c.bank[4], c.bank[5]), (c.bank[6], c.bank[7])

    def steps(eng, step):
        def body(it, first, last):
            step(it, 0, first, False)
            step(it, 1, False, last)
        edge_loop(eng, body)

    with nc.Block() as block:
        @block.gpsimd
        def _(p):
            gather.gpsimd(p, s_msg)

        @block.sync
        def _(sp):
            def load(it, h):
                g = it * 2 + h
                wait(sp, s_w, g - 1)
                sp.dma_start(att[:, G * h:G * h + G, :],
                             att_rows[at(g * G * P, G * P), :].rearrange("(t p) c -> p t c", p=P)).then_inc(s_att[h], 16)
            load(0, 0)
            load(0, 1)
            with sp.Fori(1, SLOT_TILES // U) as it:
                load(it, 0)
                load(it, 1)

        @block.tensor
        def _(pe):
            pe.wait_ge(s_0, 2)
            regs = [pe.alloc_register(f"l2_pe_nt{k}") for k in range(U)]

            def turn(it, h):
                g = it * 2 + h
                pe.wait_ge(s_oh, g * G + G)
                pe.wait_ge(s_att[h], it * 16 + 16)
                wait(pe, s_cp, g)
                for j in range(G):
                    nc.tensor.transpose(b_oT[:, j, :], onehot[:, j, :], c.ident_b[:])
                for j in range(G):
                    mm = nc.tensor.transpose(b_aT[0:D_EDGE, j * P:(j + 1) * P], att[:, G * h + j, 0:D_EDGE],
                                             c.ident[:])
                mm.then_inc(s_tr, 1)

            def dots(it, h, j):
                k = G * h + j
                t = it * U + k
                wait(pe, s_si, t - 1)
                nc.tensor.matmul(b_d[j % 2][:, :], attT[0:D_EDGE + 1, j, :], c.wd[:, :], start=True,
                                 stop=True).then_inc(s_dk, 1)
                wait(pe, s_t1, t - 1)
                node_tile = pe.snap(regs[k], min_val=0, max_val=NODE_TILES - 1)
                nc.tensor.matmul(b_q[j % 2][:, 0:D], nodeT[:, j, :], c.Q[:, at(node_tile), :], start=True,
                                 stop=True).then_inc(s_q, 1)

            def sums(it, h, j):
                t = it * U + G * h + j
                pe.wait_ge(s_wo, t + 1)
                wait(pe, s_add, t - 1)
                nc.tensor.matmul(b_m[j % 2][:, 0:D], weighted[:, j, :], msg[:, G * h + j, :], start=True,
                                 stop=True).then_inc(s_mm, 1)

            turn(0, 0)
            pe.load(regs[0:G], c.nt_d[0:1, 0:G])
            pe.wait_ge(s_cp, 1)
            for j in range(G):
                dots(0, 0, j)

            def step(it, h, first, last):
                if not last:
                    nit, nh = (it, 1) if h == 0 else (it + 1, 0)
                    pe.load(regs[G * nh:G * nh + G], c.nt_d[0:1, at(nit * U + G * nh, G)])
                    turn(nit, nh)
                    pe.wait_ge(s_cp, nit * 2 + nh + 1)
                for j in range(G):
                    if not last:
                        dots(nit, nh, j)
                    sums(it, h, j)
            steps(pe, step)

        @block.scalar
        def _(act):
            gather.copy_indices(act, 0, 0)
            gather.copy_indices(act, 0, 1)

            def group(it, h):
                g = it * 2 + h
                act.wait_ge(s_tr, g + 1)
                wait(act, s_q, g * G)
                nc.scalar.copy(flat(nodeT), flat(b_oT))
                nc.scalar.copy(flat(attT[0:D_EDGE, :, :]), b_aT[0:D_EDGE, :]).then_inc(s_cp, 1)
                for j in range(G):
                    t = it * U + G * h + j
                    act.wait_ge(s_dk, t + 1)
                    wait(act, s_msg, t - G + 1)
                    nc.scalar.activation(dkv[:, j, :], b_d[j % 2][:, :], ACT.Silu).then_inc(s_si, 1)
                act.wait_ge(s_dot, g * G + G)
                wait(act, s_w, g - 1)
                nc.scalar.activation(act_dot[:, G * h:G * h + G], dot[:, G * h:G * h + G],
                                     ACT.Silu).then_inc(s_sd, 1)

            act.wait_ge(s_0, 1)
            group(0, 0)

            def step(it, h, first, last):
                if last:
                    return
                nit, nh = (it, 1) if h == 0 else (it + 1, 0)
                group(nit, nh)
                gather.copy_indices(act, it + 1, h) if not isinstance(it, int) or it < SLOT_TILES // U - 1 else None
            def body(it, first, last):
                step(it, 0, first, False)
                if not last:
                    step(it, 1, False, False)
            edge_loop(act, body)

        @block.vector
        def _(v):
            V = nc.vector
            V.memset(attT[D_EDGE:D_EDGE + 1, :, :], 1.0).then_inc(s_0, 1)
            V.memset(c.AGG[:, :, :], 0.0).then_inc(s_0, 1)
            v.wait_ge(s_0, 2)
            regs = [v.alloc_register(f"l2_nt{k}") for k in range(U)]

            def build(it, h):
                g = it * 2 + h
                wait(v, s_tr, g)
                for j in range(G):
                    V.tensor_scalar(onehot[:, j, :], c.iota_b[:], c.lo_d[:, at(it * U + G * h + j)], None,
                                    ALU.is_equal).then_inc(s_oh, 1)

            def dots(it, h, j):
                k = G * h + j
                t = it * U + k
                gather.landed(v, it, k)
                v.wait_ge(s_q, t + 1)
                wait(v, s_dot, t - 1)
                V.tensor_tensor(prod[:, j % 2, :], b_q[j % 2][:, 0:D], kv[:, k, 0:D], ALU.mult).then_inc(s_t1, 1)
                v.wait_ge(s_si, t + 1)
                wait(v, s_mm, t - U + 1)
                V.tensor_tensor(msg[:, k, :], kv[:, k, D:2 * D], dkv[:, j, D:2 * D], ALU.mult).then_inc(s_own, 1)
                v.wait_ge(s_t1, t + 1)
                V.tensor_tensor_reduce(scratch[:, j % 2, :], prod[:, j % 2, :], dkv[:, j, 0:D], 1.0, 0.0, ALU.mult,
                                       ALU.add, dot[:, k:k + 1]).then_inc(s_dot, 1)
                v.wait_ge(s_dot, t + 1)
                v.sem_inc(s_msg, 1)

            def weights(it, h):
                g = it * 2 + h
                v.wait_ge(s_sd, g + 1)
                V.tensor_tensor(weight[:, G * h:G * h + G], act_dot[:, G * h:G * h + G],
                                att[:, G * h:G * h + G, D_EDGE], ALU.mult).then_inc(s_w, 1)
                v.wait_ge(s_w, g + 1)
                for j in range(G):
                    t = it * U + G * h + j
                    wait(v, s_mm, t - G + 1)
                    V.tensor_scalar(weighted[:, j, :], c.iota_f[:], c.lo_d[:, at(t)],
                                    weight[:, G * h + j:G * h + j + 1], ALU.is_equal, ALU.mult).then_inc(s_wo, 1)

            def add(it, h, j, node_tile):
                t = it * U + G * h + j
                v.wait_ge(s_mm, t + 1)
                wait(v, s_add, t)
                o = c.AGG[:, at(node_tile), 0:D]
                V.tensor_tensor(o, b_m[j % 2][:, 0:D].unsqueeze(1), o, ALU.add).then_inc(s_add, 1)

            s_own = c.sem("s_l2_own")
            build(0, 0)
            build(0, 1)
            for j in range(G):
                dots(0, 0, j)

            def step(it, h, first, last):
                v.load(regs[G * h:G * h + G], c.nt_d[0:1, at(it * U + G * h, G)])
                last_it = isinstance(it, int) and it == SLOT_TILES // U - 1
                if not last_it:
                    build(it + 1, h)
                weights(it, h)
                nit, nh = (it, 1) if h == 0 else (it + 1, 0)
                for j in range(G):
                    if not last:
                        dots(nit, nh, j)
                    add(it, h, j, v.snap(regs[G * h + j], min_val=0, max_val=NODE_TILES - 1))
            steps(v, step)


def head_stage(nc, c, table):
    cv = Carve(c.work)
    rows, msg, onehot, nodeT = cv(UH, D_T3), cv(UH, AGG_W), cv(UH, P), cv(2, G, P)
    z, z2 = cv(2, G, HEADS), cv(2, G, HEADS)
    s_0, s_oh, s_tr, s_cp, s_el, s_z, s_lk, s_e, s_msg, s_mm, s_add = (
        c.sem(f"s_l3_{n}") for n in ("zero", "oh", "tr", "cp", "el", "z", "lk", "e", "msg", "mm", "add"))
    gather = Gather(nc, c, c.idx_s, table, lambda k: rows[:, k, :], UH)
    b_oT, b_el, b_m = (c.bank[0], c.bank[1]), (c.bank[2], c.bank[3]), c.bank[4:8]
    Q4 = UH // G

    class Group:

        def __init__(self, it, q, ahead=0):
            q = q + ahead
            self.it, self.q = it + q // Q4, q % Q4
            self.g = self.it * Q4 + self.q
            self.lives = not isinstance(it, int) or 0 <= self.g < SLOT_TILES // G
            self.slots = range(G * self.q, G * self.q + G)

        def tile(self, j):
            return self.it * UH + G * self.q + j

    def steps(eng, step):
        def body(it, first, last):
            for q in range(Q4):
                step(it, q)
        edge_loop(eng, body, UH)

    with nc.Block() as block:
        @block.gpsimd
        def _(p):
            gather.gpsimd(p, s_msg)

        @block.tensor
        def _(pe):
            regs = [pe.alloc_register(f"l3_pe_nt{k}") for k in range(UH)]

            def turn(a):
                if not a.lives:
                    return
                pe.wait_ge(s_oh, a.tile(0) + G)
                wait(pe, s_cp, a.g - 1)
                for j, k in enumerate(a.slots):
                    mm = nc.tensor.transpose(b_oT[a.q % 2][:, j * P:(j + 1) * P], onehot[:, k, :], c.ident[:])
                mm.then_inc(s_tr, 1)

            def el(a):
                if not a.lives:
                    return
                if a.q == 0:
                    pe.load(regs, c.nt_s[0:1, at(a.it * UH, UH)])
                pe.wait_ge(s_cp, a.g + 1)
                wait(pe, s_z, a.g - 1)
                for j, k in enumerate(a.slots):
                    node_tile = pe.snap(regs[k], min_val=0, max_val=NODE_TILES - 1)
                    mm = nc.tensor.matmul(b_el[a.q % 2][:, j * HEADS:(j + 1) * HEADS], nodeT[:, a.q % 2, j, :],
                                          c.EL[:, at(node_tile), :], start=True, stop=True)
                mm.then_inc(s_el, 1)

            def sums(a):
                for j, k in enumerate(a.slots):
                    pe.wait_ge(s_msg, a.tile(j) + 1)
                    wait(pe, s_add, a.tile(j) - G + 1)
                    nc.tensor.matmul(b_m[j][:, 0:AGG_W], onehot[:, k, :], msg[:, k, :], start=True,
                                     stop=True).then_inc(s_mm, 1)

            turn(Group(0, 0))
            turn(Group(0, 1))
            el(Group(0, 0))

            def step(it, q):
                el(Group(it, q, 1))
                turn(Group(it, q, 2))
                sums(Group(it, q))
            steps(pe, step)

        @block.scalar
        def _(act):
            for q in range(Q4):
                gather.copy_indices(act, 0, q)

            def copy(a):
                if not a.lives:
                    return
                act.wait_ge(s_tr, a.g + 1)
                wait(act, s_el, a.g - 1)
                nc.scalar.copy(flat(nodeT[:, a.q % 2, :, :]), b_oT[a.q % 2][:, :]).then_inc(s_cp, 1)

            def exp(a):
                if not a.lives:
                    return
                act.wait_ge(s_lk, a.g + 1)
                wait(act, s_mm, (a.g - Q4 + 1) * G)
                nc.scalar.activation(msg[:, a.slots[0]:a.slots[-1] + 1, D:AGG_W], z2[:, a.q % 2, :, :],
                                     ACT.Exp).then_inc(s_e, 1)

            copy(Group(0, 0))
            copy(Group(0, 1))
            exp(Group(0, 0))

            def step(it, q):
                copy(Group(it, q, 2))
                exp(Group(it, q, 1))
                if not isinstance(it, int) or it < SLOT_TILES // UH - 1:
                    gather.copy_indices(act, it + 1, q)
            steps(act, step)

        @block.vector
        def _(v):
            V = nc.vector
            V.memset(c.AGG[:, :, :], 0.0).then_inc(s_0, 1)
            v.wait_ge(s_0, 1)
            regs = [v.alloc_register(f"l3_nt{k}") for k in range(UH)]

            def build(a, j):
                if not a.lives:
                    return
                wait(v, s_mm, a.tile(j) - UH + 1)
                V.tensor_scalar(onehot[:, a.slots[j], :], c.iota_f[:], c.lo_s[:, at(a.tile(j))], None,
                                ALU.is_equal).then_inc(s_oh, 1)

            def leaky(a):
                if not a.lives:
                    return
                for k in a.slots:
                    gather.landed(v, a.it, k)
                v.wait_ge(s_el, a.g + 1)
                V.tensor_tensor(z[:, a.q % 2, :, :], b_el[a.q % 2][:, 0:G * HEADS].rearrange("p (a b) -> p a b", a=G),
                                rows[:, a.slots[0]:a.slots[-1] + 1, D_HEAD:D_T3], ALU.add).then_inc(s_z, 1)
                v.wait_ge(s_z, a.g + 1)
                wait(v, s_e, a.g - 1)
                V.scalar_tensor_tensor(out=z2[:, a.q % 2, :, :], in0=z[:, a.q % 2, :, :], scalar=0.2,
                                       in1=z[:, a.q % 2, :, :], op0=ALU.mult, op1=ALU.max).then_inc(s_lk, 1)

            def message(a, j):
                v.wait_ge(s_e, a.g + 1)
                k = a.slots[j]
                V.tensor_tensor(msg[:, k, 0:D].rearrange("p (h d) -> p h d", h=HEADS),
                                rows[:, k, 0:D_HEAD].unsqueeze(1).broadcast_to([P, HEADS, D_HEAD]),
                                msg[:, k, D:AGG_W].unsqueeze(2).broadcast_to([P, HEADS, D_HEAD]),
                                ALU.mult).then_inc(s_msg, 1)

            def add(a, j):
                if not a.lives:
                    return
                node_tile = v.snap(regs[a.slots[j]], min_val=0, max_val=NODE_TILES - 1)
                v.wait_ge(s_mm, a.tile(j) + 1)
                wait(v, s_add, a.tile(j))
                o = c.AGG[:, at(node_tile), :]
                V.tensor_tensor(o, b_m[j][:, 0:AGG_W].unsqueeze(1), o, ALU.add).then_inc(s_add, 1)

            for q in range(3):
                for j in range(G):
                    build(Group(0, q), j)
            leaky(Group(0, 0))

            def step(it, q):
                for j in range(G):
                    message(Group(it, q), j)
                    add(Group(it, q, -1), j)
                    if j == G - 1 and q == 0:
                        v.load(regs, c.nt_s[0:1, at(it * UH, UH)])
                    build(Group(it, q, 3), j)
                    if j == 1:
                        leaky(Group(it, q, 1))
            steps(v, step)
            for j in range(G):
                add(Group(SLOT_TILES // UH - 1, Q4 - 1), j)


def program(nc, src, dst, typ, wgt, attr, x, w12, wrel, wqkv, wo, wd, w3, wlr, bias, out):
    def dram(name, shape):
        return nc.dram_tensor(name, shape, f32, kind="Internal").ap()
    t0, t1 = dram("rows_w2", (NODE_ROWS, D)), dram("rows_rel", (NODE_ROWS, N_RELS * D))
    t2, t3 = dram("rows_kv", (NODE_ROWS, 2 * D)), dram("rows_head", (NODE_ROWS, D_T3))
    att_rows = dram("att_rows", (SLOTS, ROW))
    with ExitStack() as ctx:
        c = Chip(nc, ctx)
        weights = [(c.w12[:, :, :], w12.rearrange("(z p) n -> p z n", p=P)),
                   (c.wrel[:, :, :], wrel.rearrange("(z p) n -> p z n", p=P)),
                   (c.wqkv[:, :, :], wqkv.rearrange("(z p) n -> p z n", p=P)),
                   (c.wo[:, :, :], wo.rearrange("(z p) n -> p z n", p=P)),
                   (c.wd[:, :], wd), (c.w3[:, :, :], w3.rearrange("(z p) n -> p z n", p=P)),
                   (c.wlr[:, :], wlr), (c.bias[:, :], bias.broadcast_to([P, BIAS_W]))]
        with ExitStack() as ctx2:
            def sb(name, shape, dt):
                return ctx2.enter_context(nc.sbuf_tensor(name, shape, dt))
            prep = {"sb": sb, "cut": sb("cut", [P, EDGE_COLS], f32), "slot_d": sb("slot_d", [P, EDGE_COLS], i32),
                    "pos_lo": sb("pos_lo", [P, 2, EDGE_COLS], f32), "pos_hi": sb("pos_hi", [P, 2, EDGE_COLS], f32),
                    "part": sb("part", [P, 2, 3, EDGE_COLS], f32)}
            rank_stage(nc, c, src, dst, typ, wgt, x, weights, att_rows, prep)
            place_stage(nc, c, attr, att_rows, prep)
        node_stage_0(nc, c, t0)
        sum_stage(nc, c, "l0", c.idx_s, c.lo_s, c.nt_s, t0, True)
        node_stage_1(nc, c, t1)
        sum_stage(nc, c, "l1", c.idx_d1, c.lo_d, c.nt_d, t1.rearrange("n (r d) -> (n r) d", r=N_RELS), False)
        batch_norm_stage(nc, c)
        node_stage_2(nc, c, t2)
        attention_stage(nc, c, t2, att_rows)
        node_stage_3(nc, c, t3)
        head_stage(nc, c, t3)
        output_stage(nc, c, out)


def kernel(x, src, dst, edge_attr_64, edge_type_8, edge_weight, L0_gnn_W1, L0_gnn_b1, L0_gnn_W2, L0_gnn_b2,
           L1_gnn_weight, L1_gnn_gamma, L1_gnn_beta, L2_gnn_ln_g, L2_gnn_ln_b, L2_gnn_Wq, L2_gnn_bq, L2_gnn_Wk,
           L2_gnn_bk, L2_gnn_Wv, L2_gnn_bv, L2_gnn_Wo, L2_gnn_bo, L2_gnn_Wdk, L2_gnn_bdk, L2_gnn_Wdv, L2_gnn_bdv,
           L3_gnn_W, L3_gnn_Wl, L3_gnn_Wr, L3_gnn_b):
    import concourse.bacc as bacc
    from concourse.bass_utils import run_bass_kernel_spmd

    def edges(a, pad):
        a = np.asarray(a)
        full = np.full((EDGE_ROWS,) + a.shape[1:], pad, a.dtype)
        full[:N_EDGES] = a
        return full.reshape((P, EDGE_COLS) + a.shape[1:])

    def turned(*ws):
        return np.ascontiguousarray(np.concatenate([np.asarray(w).T for w in ws], axis=1))

    xs = np.zeros((NODE_ROWS, D), np.float32)
    xs[:N_NODES] = np.asarray(x)
    ins = {
        "src": edges(src, PAD_NODE), "dst": edges(dst, PAD_NODE), "typ": edges(edge_type_8, 0),
        "wgt": edges(edge_weight, 0), "attr": edges(edge_attr_64, 0), "x": xs,
        "w12": turned(L0_gnn_W1, L0_gnn_W2),
        "wrel": np.ascontiguousarray(np.asarray(L1_gnn_weight).transpose(1, 0, 2).reshape(D, N_RELS * D)),
        "wqkv": turned(L2_gnn_Wq, L2_gnn_Wk, L2_gnn_Wv), "wo": turned(L2_gnn_Wo),
        "wd": np.concatenate([turned(L2_gnn_Wdk, L2_gnn_Wdv),
                              np.concatenate([np.asarray(L2_gnn_bdk), np.asarray(L2_gnn_bdv)])[None]]),
        "w3": np.asarray(L3_gnn_W),
        "wlr": np.concatenate([np.eye(D_HEAD, dtype=np.float32), turned(L3_gnn_Wr, L3_gnn_Wl)], axis=1),
        "bias": np.concatenate([np.asarray(a) for a in (
            L0_gnn_b1, L0_gnn_b2, L1_gnn_gamma, L1_gnn_beta, L2_gnn_ln_g, L2_gnn_ln_b, L2_gnn_bq, L2_gnn_bk,
            L2_gnn_bv, L2_gnn_bo, L3_gnn_b)])[None],
    }
    nc = bacc.Bacc("TRN2", target_bir_lowering=False, num_devices=1)
    aps = {k: nc.dram_tensor("in_" + k, a.shape, mybir.dt.from_np(a.dtype), kind="ExternalInput").ap()
           for k, a in ins.items()}
    out = nc.dram_tensor("out_0", (N_NODES, D), f32, kind="ExternalOutput").ap()
    program(nc, *[aps[k] for k in ("src", "dst", "typ", "wgt", "attr", "x", "w12", "wrel", "wqkv", "wo", "wd", "w3",
                                   "wlr", "bias")], out)
    r = run_bass_kernel_spmd(nc, [{"in_" + k: a for k, a in ins.items()}], core_ids=[0])
    return r.results[0]["out_0"]
```

```python
import numpy as np
import concourse.bass as bass
import concourse.mybir as mybir
from contextlib import ExitStack

P = 128
N_NODES, N_EDGES, D, D_EDGE, N_RELS, HEADS, D_HEAD = 3125, 50000, 256, 64, 8, 4, 64
NODE_TILES = -(-N_NODES // P)
NODE_ROWS = NODE_TILES * P
PAD_NODE = NODE_ROWS - 1
LAST_ROWS = N_NODES - (NODE_TILES - 1) * P
EDGE_COLS = 8 * -(-N_EDGES // (8 * P))
EDGE_ROWS = EDGE_COLS * P
SLOT_TILES = (EDGE_COLS + NODE_TILES - 1) // 8 * 8
SLOTS = SLOT_TILES * P
ROW = D_EDGE + 2
PART_BITS = 10
PART = 1 << PART_BITS
AGG_W = D + HEADS
LN_EPS, BN_EPS, SUM_EPS = 1e-5, 1e-5, 1e-12
U = 8
UH = 16
G = 4
Q4 = UH // G
NK = 5
WORK = 12800
D_T3 = D_HEAD + HEADS

f32, bf16, f16, i32 = mybir.dt.float32, mybir.dt.bfloat16, mybir.dt.float16, mybir.dt.int32
ALU = mybir.AluOpType
ACT = mybir.ActivationFunctionType
AXX = mybir.AxisListType.X
assert PAD_NODE * 2 * P + P < PART * PART
assert EDGE_COLS * P + NODE_TILES * (P - 1) < (SLOT_TILES + 1) * P

BIAS = {}
_at = 0
for _n, _w in (("b1", D), ("b2", D), ("gamma", D), ("beta", D), ("ln_g", D), ("ln_b", D),
               ("bqkv", 3 * D), ("bo", D), ("b3", D_HEAD)):
    BIAS[_n] = (_at, _at + _w)
    _at += _w
BIAS_W = _at


def wait(eng, sem, value):
    if isinstance(value, int) and value <= 0:
        return
    eng.wait_ge(sem, value)


def at(t, n=1):
    return bass.ds(t, n)


class Chip:

    def __init__(self, nc, ctx):
        self.nc, self.ctx = nc, ctx
        sb, ps = self.sb, self.ps
        self.X = sb("X", [P, NODE_TILES, D], f32)
        self.AGG = sb("AGG", [P, NODE_TILES, AGG_W], f32)
        self.Q = sb("Q", [P, NODE_TILES, D], f32)
        self.work = sb("work", [P, WORK], f32)
        self.w12 = sb("w12", [P, 2, 2 * D], f32)
        self.wrel = sb("wrel", [P, 2, N_RELS * D], f32)
        self.wqkv = sb("wqkv", [P, 2, 3 * D], f32)
        self.wo = sb("wo", [P, 2, D], f32)
        self.wd = sb("wd", [D_EDGE + 1, 2 * D], f32)
        self.w3 = sb("w3", [P, 2, D_HEAD], f32)
        self.wlr = sb("wlr", [D_HEAD, D_HEAD + 2 * HEADS], f32)
        self.bias = sb("bias", [P, BIAS_W], f32)
        self.iota_f = sb("iota_f", [P, P], f32)
        self.iota_b = sb("iota_b", [P, P], bf16)
        self.iota_slot = sb("iota_slot", [P, SLOT_TILES], f16)
        self.ident = sb("ident", [P, P], f32)
        self.ident_b = sb("ident_b", [P, P], bf16)
        self.lower = sb("lower", [P, P], f32)
        self.ones = sb("ones", [P, P], f32)
        self.ones_last = sb("ones_last", [P, P], f32)
        self.eps = sb("eps", [P, 3], f32)
        self.idx_s = sb("idx_s", [P, SLOT_TILES], i32)
        self.idx_d1 = sb("idx_d1", [P, SLOT_TILES], i32)
        self.idx_d2 = sb("idx_d2", [P, SLOT_TILES], i32)
        self.lo_s = sb("lo_s", [P, SLOT_TILES], f32)
        self.lo_d = sb("lo_d", [P, SLOT_TILES], f32)
        self.nt_s = sb("nt_s", [1, SLOT_TILES], i32)
        self.nt_d = sb("nt_d", [1, SLOT_TILES], i32)
        self.bank = [ps(f"bank{k}", [P, 512], f32) for k in range(8)]
        self.ix = sb("ix", [P, UH], i32)
        self.EL = sb("EL", [P, NODE_TILES, HEADS], f32)
        self.mv = sb("mv", [P, NODE_TILES, 2], f32)
        self.st = sb("st", [P, NODE_TILES, 6], f32)
        self.rs = sb("rs", [P, NODE_TILES], f32)
        self.nmr = sb("nmr", [P, NODE_TILES], f32)
        self.s_rows = [self.sem(f"s_rows{k}") for k in range(UH)]
        self.rows_base = [0] * UH
        self.s_ix, self.s_go = self.sem("s_ix"), self.sem("s_go")
        self.ix_base = 0
        self.s_store = [self.sem(f"s_store{k}") for k in range(NK)]
        self.store_base = 0
        self.s_st, self.s_sq, self.s_rs = self.sem("s_stats"), self.sem("s_sqrt"), self.sem("s_rstd")
        self.norms = 0
        self.own = Own(self.sem("s_own"))

    def sb(self, name, shape, dt):
        return self.ctx.enter_context(self.nc.sbuf_tensor(name, shape, dt))

    def ps(self, name, shape, dt):
        return self.ctx.enter_context(self.nc.psum_tensor(name, shape, dt))

    def sem(self, name):
        return self.ctx.enter_context(self.nc.semaphore(name))

    def b(self, name):
        return self.bias[:, BIAS[name][0]:BIAS[name][1]]


class Own:

    def __init__(self, sem):
        self.sem, self.n = sem, 0

    def __call__(self, ins):
        self.n += 1
        ins.then_inc(self.sem, 1)
        return self.n


class Carve:

    def __init__(self, work):
        self.work, self.n = work, 0

    def __call__(self, *shape, dt=f32):
        n = int(np.prod(shape))
        words = n if dt not in (bf16, f16) else (n + 1) // 2
        v = self.work[:, self.n:self.n + words]
        self.n += words
        assert self.n <= WORK, self.n
        if dt != f32:
            v = v.bitcast(dt)
        names = "abcd"[:len(shape)]
        if len(shape) > 1:
            v = v.rearrange(f"p ({' '.join(names)}) -> p {' '.join(names)}", **dict(zip(names, shape)))
        return v


class Prep:

    def __init__(self, nc, c, ctx):
        def sb(name, shape, dt=f32):
            return ctx.enter_context(nc.sbuf_tensor(name, shape, dt))
        self.carry = sb("carry", [P, EDGE_COLS, ROW - D_EDGE])
        self.slot_d = sb("slot_d", [P, EDGE_COLS], i32)
        self.pos_lo, self.pos_hi = sb("pos_lo", [P, EDGE_COLS]), sb("pos_hi", [P, EDGE_COLS])
        self.part = sb("part", [P, 2, EDGE_COLS])
        self.small = sb("rank_small", [P, 8, NODE_TILES + 1])
        self.smallI = sb("rank_smallI", [P, NODE_TILES], i32)
        self.tile_no = sb("tile_no", [P, SLOT_TILES])
        self.one_bf = c.Q[:, :, :].rearrange("p a b -> p (a b)").bitcast(bf16)[:, 0:NODE_TILES * EDGE_COLS]
        self.one3 = self.one_bf.rearrange("p (b t) -> p b t", b=NODE_TILES)
        self.scan = c.work[:, 0:NODE_TILES * EDGE_COLS]
        self.scan3 = self.scan.rearrange("p (b t) -> p b t", b=NODE_TILES)
        agg = c.AGG[:, :, :].rearrange("p a b -> p (a b)")
        cols = [agg[:, k * EDGE_COLS:(k + 1) * EDGE_COLS] for k in range(14)]
        self.src, self.dst, self.typ = (a.bitcast(i32) for a in cols[0:3])
        self.w_in = cols[3]
        self.tI = [a.bitcast(i32) for a in cols[4:8]]
        self.tF = cols[8:12]
        self.keyb = cols[12].bitcast(bf16)[:, 0:EDGE_COLS]
        self.cmp = agg[0:NODE_TILES - 1, 14 * EDGE_COLS:14 * EDGE_COLS + SLOT_TILES]
        self.s_in, self.s_mm = c.sem("s_rank_in"), c.sem("s_rank_mm")


class Ranks:

    def __init__(self, nc, c, prep, n, key, nt, banks):
        self.nc, self.c, self.prep, self.n, self.key, self.nt, self.banks = nc, c, prep, n, key, nt, banks

    def tensor(self, pe):
        nc, c, r = self.nc, self.c, self.prep
        below, all_, ends, tiles = self.banks
        B = NODE_TILES
        pe.wait_ge(r.s_in, 3 * self.n + 1)
        nc.tensor.matmul(below[:, 0:B], c.lower[:], r.small[:, 1, 0:B], start=True, stop=True)
        nc.tensor.matmul(all_[:, 0:B], c.ones[:], r.small[:, 1, 0:B], start=True, stop=True).then_inc(r.s_mm, 1)
        pe.wait_ge(r.s_in, 3 * self.n + 2)
        nc.tensor.transpose(ends[0:B, 0:P], r.small[:, 3, 0:B], c.ident[:]).then_inc(r.s_mm, 1)
        pe.wait_ge(r.s_in, 3 * self.n + 3)
        nc.tensor.matmul(tiles[0:1, 0:SLOT_TILES], c.ones[0:B - 1, 0:1], r.cmp, start=True,
                         stop=True).then_inc(r.s_mm, 1)

    def vector(self, v):
        nc, c, r, V = self.nc, self.c, self.prep, self.nc.vector
        below, all_, ends, tiles = self.banks
        B = NODE_TILES
        small = r.small
        cum, cnt, used, end, off, one_end = (small[:, j, 0:B] for j in range(6))

        def own(ins):
            v.wait_ge(c.own.sem, c.own(ins))
        V.tensor_scalar(r.tI[1], self.key, P - 1, None, ALU.bitwise_and)
        own(V.tensor_scalar(r.tI[0], self.key, 7, None, ALU.logical_shift_right))
        V.tensor_copy(r.tF[1], r.tI[1])
        own(V.tensor_copy(r.keyb, r.tI[0]))
        for b in range(B):
            ins = V.tensor_scalar(r.one3[:, b, :], r.keyb, float(b), None, ALU.is_equal)
        own(ins)
        V.memset(small[:, 0, 0:1], 0.0)
        own(V.tensor_tensor_scan(r.scan, r.one_bf, r.one_bf, 0.0, ALU.add, ALU.max))
        own(V.tensor_copy(small[:, 0, 1:B + 1], r.scan3[:, :, EDGE_COLS - 1]))
        V.tensor_tensor(cnt, small[:, 0, 1:B + 1], cum, ALU.subtract).then_inc(r.s_in, 1)
        v.wait_ge(r.s_mm, 3 * self.n + 1)
        own(V.tensor_scalar(used, all_[:, 0:B], float(P - 1), None, ALU.add))
        own(V.tensor_copy(r.smallI[:], used))
        own(V.tensor_scalar(r.smallI[:], r.smallI[:], 7, None, ALU.logical_shift_right))
        own(V.tensor_copy(used, r.smallI[:]))
        own(V.tensor_tensor_scan(end, used, used, 0.0, ALU.add, ALU.max))
        V.tensor_tensor(off, end, used, ALU.subtract).then_inc(r.s_in, 1)
        v.wait_ge(r.s_in, 3 * self.n + 2)
        own(V.scalar_tensor_tensor(out=off, in0=off, scalar=float(P), in1=below[:, 0:B], op0=ALU.mult, op1=ALU.add))
        own(V.scalar_tensor_tensor(out=off, in0=off, scalar=-1.0, in1=cum, op0=ALU.add, op1=ALU.subtract))
        for b in range(B):
            ins = V.scalar_tensor_tensor(out=r.scan3[:, b, :], in0=r.scan3[:, b, :], scalar=small[:, 4, b:b + 1],
                                         in1=r.one3[:, b, :], op0=ALU.add, op1=ALU.mult)
        placed = c.own(ins)
        v.wait_ge(r.s_mm, 3 * self.n + 2)
        own(V.tensor_copy(small[0:B - 1, 5, 0:1], ends[0:B - 1, 0:1]))
        V.tensor_scalar(r.cmp, r.tile_no[0:B - 1, :], small[0:B - 1, 5, 0:1], None, ALU.is_ge).then_inc(r.s_in, 1)
        v.wait_ge(c.own.sem, placed)
        own(V.tensor_reduce(r.tF[2], r.scan3.rearrange("p b t -> p t b"), AXX, ALU.add))
        v.wait_ge(r.s_mm, 3 * self.n + 3)
        V.tensor_copy(self.nt[:], tiles[0:1, 0:SLOT_TILES])
        own(V.tensor_copy(r.tI[0], r.tF[2]))


def load_stage(nc, c, src, dst, typ, wgt, x, weights, att_rows, prep):
    s_key, s_load, s_zero, s_fill = c.sem("s_key"), c.sem("s_load"), c.sem("s_zero"), c.sem("s_fill")
    s_const, s_sin, s_turn, s_cst = c.sem("s_const"), c.sem("s_sin"), c.sem("s_turn"), c.sem("s_cst_own")
    ztiles = 32
    zeros = c.work[:, WORK - ztiles * ROW:WORK]
    tF, tI = prep.tF, prep.tI
    n_loads = len(weights) + 1
    ranks = Ranks(nc, c, prep, 0, prep.dst, c.nt_d, c.bank[0:4])

    with nc.Block() as block:
        @block.sync
        def _(sp):
            for into, a in ((prep.w_in, wgt), (prep.dst, dst), (prep.src, src), (prep.typ, typ)):
                sp.dma_start(into, a[:, :]).then_inc(s_key, 16)
            sp.wait_ge(s_zero, 1)
            dest = att_rows.rearrange("(p r) c -> p (r c)", p=P)
            fills = SLOT_TILES // ztiles
            for k in range(fills):
                sp.dma_start(dest[:, k * ztiles * ROW:(k + 1) * ztiles * ROW], zeros).then_inc(s_fill, 16)
            sp.dma_start(c.X[:, :, :], x.rearrange("(i p) d -> p i d", p=P)).then_inc(s_load, 16)
            for into, a in weights:
                sp.dma_start(into, a).then_inc(s_load, 16)
            sp.wait_ge(s_fill, 16 * fills)
            sp.wait_ge(s_load, 16 * n_loads)

        @block.gpsimd
        def _(p):
            n = [0]

            def own(ins):
                n[0] += 1
                ins.then_inc(s_cst, 1)
                p.wait_ge(s_cst, n[0])

            nc.gpsimd.memset(c.eps[:, 1:2], float(np.pi / 2)).then_inc(s_const, 1)
            nc.gpsimd.memset(zeros, 0.0).then_inc(s_zero, 1)
            nc.gpsimd.memset(c.ones[:], 1.0).then_inc(s_const, 1)
            nc.gpsimd.iota(prep.tile_no[:], [[1, SLOT_TILES]], base=0, channel_multiplier=0,
                           allow_small_or_imprecise_dtypes=True).then_inc(s_const, 1)
            nc.gpsimd.iota(c.iota_f[:], [[1, P]], base=0, channel_multiplier=0,
                           allow_small_or_imprecise_dtypes=True).then_inc(s_const, 1)
            nc.gpsimd.iota(c.iota_b[:], [[1, P]], base=0, channel_multiplier=0,
                           allow_small_or_imprecise_dtypes=True).then_inc(s_const, 1)
            nc.gpsimd.iota(c.iota_slot[:], [[1, SLOT_TILES]], base=0, channel_multiplier=0,
                           allow_small_or_imprecise_dtypes=True).then_inc(s_const, 1)
            own(nc.gpsimd.memset(c.lower[:], 0.0))
            nc.gpsimd.affine_select(out=c.lower[:], in_=c.lower[:], compare_op=ALU.is_ge, fill=1.0, base=0,
                                    pattern=[[-1, P]], channel_multiplier=1).then_inc(s_const, 1)
            own(nc.gpsimd.memset(c.ident[:], 0.0))
            nc.gpsimd.affine_select(out=c.ident[:], in_=c.ident[:], compare_op=ALU.not_equal, fill=1.0, base=0,
                                    pattern=[[-1, P]], channel_multiplier=1).then_inc(s_const, 1)
            own(nc.gpsimd.memset(c.ident_b[:], 0.0))
            nc.gpsimd.affine_select(out=c.ident_b[:], in_=c.ident_b[:], compare_op=ALU.not_equal, fill=1.0,
                                    base=0, pattern=[[-1, P]], channel_multiplier=1).then_inc(s_const, 1)
            own(nc.gpsimd.memset(c.ones_last[:], 1.0))
            nc.gpsimd.affine_select(out=c.ones_last[:], in_=c.ones_last[:], compare_op=ALU.is_ge, fill=0.0,
                                    base=LAST_ROWS - 1, pattern=[[0, P]],
                                    channel_multiplier=-1).then_inc(s_const, 1)
            nc.gpsimd.memset(c.eps[:, 0:1], LN_EPS).then_inc(s_const, 1)
            nc.gpsimd.memset(c.eps[:, 2:3], BN_EPS).then_inc(s_const, 1)

        @block.scalar
        def _(act):
            act.wait_ge(s_turn, 1)
            act.wait_ge(s_const, 1)
            nc.scalar.activation(tF[2], tF[0], ACT.Sin, bias=c.eps[:, 1:2],
                                 scale=-2.0 * float(np.pi)).then_inc(s_sin, 1)

        @block.tensor
        def _(pe):
            pe.wait_ge(s_const, 12)
            ranks.tensor(pe)

        @block.vector
        def _(v):
            def own(ins):
                v.wait_ge(c.own.sem, c.own(ins))

            V = nc.vector
            v.wait_ge(s_key, 64)
            own(V.tensor_scalar(tF[0], prep.w_in, 0.1, None, ALU.mult))
            own(V.tensor_copy(tI[0], tF[0]))
            own(V.tensor_copy(tF[1], tI[0]))
            own(V.tensor_tensor(tF[0], tF[0], tF[1], ALU.subtract))
            own(V.scalar_tensor_tensor(out=tF[0], in0=tF[0], scalar=-1.0, in1=tF[0], op0=ALU.mult, op1=ALU.max))
            own(V.tensor_scalar(tF[1], tF[0], -1.0, 1.0, ALU.mult, ALU.add))
            V.tensor_tensor(tF[0], tF[0], tF[1], ALU.min).then_inc(s_turn, 1)
            own(V.tensor_scalar(tF[3], prep.w_in, 5.0, 0.5, ALU.is_lt, ALU.mult))
            v.wait_ge(s_sin, 1)
            own(V.scalar_tensor_tensor(out=prep.carry[:, :, 0], in0=tF[2], scalar=1.0, in1=tF[3], op0=ALU.add,
                                       op1=ALU.mult))
            v.wait_ge(s_const, 12)
            ranks.vector(v)
            V.tensor_scalar(tI[1], tI[0], P - 1, None, ALU.bitwise_and)
            V.tensor_scalar(tI[2], tI[0], 7, None, ALU.logical_shift_right)
            V.tensor_copy(tF[3], prep.src)
            own(V.tensor_copy(tF[0], prep.typ))
            own(V.scalar_tensor_tensor(out=tF[3], in0=tF[3], scalar=-float(2 * P * N_RELS), in1=tF[1],
                                       op0=ALU.mult, op1=ALU.subtract))
            V.tensor_copy(tF[2], tI[2])
            own(V.tensor_scalar(tF[0], tF[0], float(2 * P), float(PAD_NODE * N_RELS * 2 * P + P), ALU.mult, ALU.add))
            own(V.tensor_copy(tF[1], tI[1]))
            V.tensor_tensor(prep.carry[:, :, 1], tF[3], tF[0], ALU.add)
            V.scalar_tensor_tensor(out=prep.slot_d[:], in0=tF[1], scalar=float(SLOT_TILES), in1=tF[2],
                                   op0=ALU.mult, op1=ALU.add)


def edge_stage(nc, c, attr, att_rows, table, prep):
    S4 = 4
    UP = 14
    HP = UP // 2
    steps = EDGE_COLS // UP
    assert EDGE_COLS % UP == 0
    cv = Carve(c.work)
    hi1, lo1 = cv(S4, SLOT_TILES, dt=f16), cv(S4, 2, P, dt=f16)
    zero = cv(512, dt=f16)
    tmp, vI, wI = cv(SLOT_TILES), cv(SLOT_TILES, dt=i32), cv(SLOT_TILES, dt=i32)
    layer = LayerZero(nc, c, cv, table)
    tail = Carve(c.work)
    tail.n = max(cv.n, NODE_TILES * EDGE_COLS)
    rows = tail(UP, ROW)
    s_z, s_oh, s_acc, s_ixc, s_go = (c.sem("s_place_zero"), c.sem("s_place_oh"), c.sem("s_place_mm"), c.s_ix, c.s_go)
    s_row = [c.sem(f"s_row{h}") for h in range(2)]
    s_sc = c.s_rows
    c.rows_base[0:UP], c.ix_base = [16 * steps] * UP, 2 * steps
    acc = c.bank[4:6]
    ranks = Ranks(nc, c, prep, 1, prep.src, c.nt_s, (c.bank[6], c.bank[7], c.bank[0], c.bank[1]))

    with nc.Block() as block:
        @block.sync
        def _(sp):
            def load(it, h):
                sp.dma_start(rows[:, HP * h:HP * h + HP, 0:D_EDGE],
                             attr[:, at(it * UP + HP * h, HP), :]).then_inc(s_row[h], 16)
            for h in range(2):
                load(0, h)
            with sp.Fori(1, steps) as it:
                for h in range(2):
                    for k in range(HP * h, HP * h + HP):
                        sp.wait_ge(s_sc[k], it * 16)
                    load(it, h)

        @block.gpsimd
        def _(p):
            def scatter(it, h, first):
                if not first:
                    for k in range(HP * h, HP * h + HP):
                        p.wait_ge(s_sc[k], it * 16)
                cols = at(it * UP + HP * h, HP)
                nc.gpsimd.tensor_copy(c.ix[:, HP * h:HP * h + HP], prep.slot_d[:, cols])
                nc.gpsimd.tensor_copy(rows[:, HP * h:HP * h + HP, D_EDGE:ROW],
                                      prep.carry[:, cols, :]).then_inc(s_ixc, 1)
                p.wait_ge(s_row[h], it * 16 + 16)
                p.wait_ge(s_ixc, it * 2 + (h + 1))
                p.sem_inc(s_go, 1)
                for k in range(HP * h, HP * h + HP):
                    p.indirect_dma_start(att_rows, bass.IndirectOffsetOnAxis(ap=c.ix[:, k:k + 1], axis=0),
                                         rows[:, k, :], None).then_inc(s_sc[k], 16)
            for h in range(2):
                scatter(0, h, True)
            with p.Fori(1, steps) as it:
                for h in range(2):
                    scatter(it, h, False)
            for k in range(UP):
                p.wait_ge(s_sc[k], 16 * steps)

        @block.tensor
        def _(pe):
            ranks.tensor(pe)
            pe.wait_ge(s_z, 1)
            for k in range(2):
                nc.tensor.matmul(acc[k][:, 0:SLOT_TILES], zero[:, 0:P], zero[:, 0:SLOT_TILES], start=True,
                                 stop=False, skip_group_check=True)
            with pe.Fori(0, EDGE_COLS // S4) as it:
                for s in range(S4):
                    pe.wait_ge(s_oh, it * S4 + s + 1)
                    for k in range(2):
                        mm = nc.tensor.matmul(acc[k][:, 0:SLOT_TILES], lo1[:, s, k, :], hi1[:, s, :], start=False,
                                              stop=False, skip_group_check=True)
                    mm.then_inc(s_acc, 1)
            for k in range(2):
                mm = nc.tensor.matmul(acc[k][:, 0:SLOT_TILES], zero[:, 0:P], zero[:, 0:SLOT_TILES], start=False,
                                      stop=True, skip_group_check=True)
            mm.then_inc(s_acc, 1)
            layer.tensor(pe)

        @block.scalar
        def _(act):
            layer.scalar(act)

        @block.vector
        def _(v):
            V = nc.vector

            def own(ins):
                v.wait_ge(c.own.sem, c.own(ins))
            tF, tI = prep.tF, prep.tI
            ranks.vector(v)
            V.tensor_scalar(tI[1], tI[0], P - 1, None, ALU.bitwise_and)
            V.tensor_scalar(tI[2], tI[0], 7, None, ALU.logical_shift_right)
            own(V.tensor_copy(tF[3], prep.dst))
            V.tensor_copy(prep.pos_lo[:], tI[1])
            V.tensor_copy(prep.pos_hi[:], tI[2])
            own(V.scalar_tensor_tensor(out=tF[3], in0=tF[3], scalar=-float(2 * P), in1=tF[1], op0=ALU.mult,
                                       op1=ALU.subtract))
            own(V.tensor_scalar(tI[3], tF[3], float(PAD_NODE * 2 * P + P), None, ALU.add))
            V.tensor_scalar(tI[1], tI[3], PART - 1, None, ALU.bitwise_and)
            own(V.tensor_scalar(tI[2], tI[3], PART_BITS, None, ALU.logical_shift_right))
            V.tensor_copy(prep.part[:, 0, :], tI[1])
            own(V.tensor_copy(prep.part[:, 1, :], tI[2]))
            V.memset(zero, 0.0).then_inc(s_z, 1)

            def onehots(it, first):
                for s in range(S4):
                    t = it * S4 + s
                    if not first:
                        v.wait_ge(s_acc, t - S4 + 1)
                    V.tensor_scalar(hi1[:, s, :], c.iota_slot[:], prep.pos_hi[:, at(t)], None, ALU.is_equal)
                    for j in range(2):
                        ins = V.tensor_scalar(lo1[:, s, j, :], c.iota_b[:], prep.pos_lo[:, at(t)],
                                              prep.part[:, j, at(t)], ALU.is_equal, ALU.mult)
                    ins.then_inc(s_oh, 1)
            onehots(0, True)
            with v.Fori(1, EDGE_COLS // S4) as it:
                onehots(it, False)

            v.wait_ge(s_acc, EDGE_COLS + 1)
            own(V.tensor_copy(tmp, acc[0][:, 0:SLOT_TILES]))
            own(V.scalar_tensor_tensor(out=vI, in0=acc[1][:, 0:SLOT_TILES], scalar=float(PART), in1=tmp,
                                       op0=ALU.mult, op1=ALU.add))
            own(V.tensor_scalar(wI, vI, 2 * P - 1, None, ALU.bitwise_and))
            own(V.tensor_scalar(vI, vI, 8, None, ALU.logical_shift_right))
            V.tensor_scalar(c.lo_s[:], wI, -1.0, float(P), ALU.mult, ALU.add)
            own(V.tensor_scalar(c.idx_s[:], vI, -1.0, float(PAD_NODE), ALU.mult, ALU.add))
            layer.vector(v)


class Norm:

    def __init__(self, nc, c):
        self.nc, self.c, self.n = nc, c, c.norms
        c.norms += 1

    def vector(self, v, of, before=None):
        nc, c = self.nc, self.c
        with v.Fori(0, NODE_TILES // NK) as it:
            for k in range(NK):
                i = it * NK + k
                if before:
                    before(v, i)
                nc.vector.bn_stats(c.st[:, at(i), :], of[:, at(i), 0:D]).then_inc(c.s_st, 1)
        v.wait_ge(c.s_st, (NODE_TILES + 1) * self.n + NODE_TILES)

        def own(ins):
            v.wait_ge(c.own.sem, c.own(ins))
        mean, var, diff = c.mv[:, :, 0], c.mv[:, :, 1], c.rs[:]
        own(nc.vector.tensor_tensor(diff, c.st[:, :, 1], c.st[:, :, 4], ALU.subtract))
        own(nc.vector.tensor_tensor(mean, c.st[:, :, 1], c.st[:, :, 4], ALU.add))
        own(nc.vector.tensor_scalar(mean, mean, 0.5, None, ALU.mult))
        own(nc.vector.scalar_tensor_tensor(out=diff, in0=diff, scalar=D / 4.0, in1=diff, op0=ALU.mult,
                                           op1=ALU.mult))
        own(nc.vector.tensor_tensor(var, c.st[:, :, 2], c.st[:, :, 5], ALU.add))
        nc.vector.tensor_tensor(var, var, diff, ALU.add).then_inc(c.s_st, 1)
        v.wait_ge(c.s_sq, self.n + 1)
        nc.vector.reciprocal(c.rs[:], c.rs[:]).then_inc(c.s_rs, 1)
        v.wait_ge(c.s_rs, 2 * self.n + 1)
        nc.vector.scalar_tensor_tensor(out=c.nmr[:], in0=c.mv[:, :, 0], scalar=-1.0, in1=c.rs[:],
                                       op0=ALU.mult, op1=ALU.mult).then_inc(c.s_rs, 1)

    def scalar(self, act):
        act.wait_ge(self.c.s_st, (NODE_TILES + 1) * (self.n + 1))
        self.nc.scalar.activation(self.c.rs[:], self.c.mv[:, :, 1], ACT.Sqrt, bias=self.c.eps[:, 0:1],
                                  scale=1.0 / D).then_inc(self.c.s_sq, 1)

    def ready(self, eng):
        eng.wait_ge(self.c.s_rs, 2 * self.n + 2)


class Product:

    def __init__(self, nc, c, name, carve, chunks, first_bank=2):
        self.nc, self.c, self.chunks, self.fb = nc, c, chunks, first_bank
        self.h = carve(NK, D)
        self.hT = carve(NK, 2, P)
        self.s_h, self.s_tp, self.s_ht = (c.sem(f"s_{name}_h"), c.sem(f"s_{name}_tp"), c.sem(f"s_{name}_ht"))
        self.s_mm = [c.sem(f"s_{name}_mm{q}") for q in range(len(chunks))]
        self.s_ev = [c.sem(f"s_{name}_ev{q}") for q in range(len(chunks))]

    def loop(self, eng, body):
        last = NODE_TILES // NK - 1
        body(0, True)
        with eng.Fori(1, last) as it:
            body(it, False)
        body(last, False)

    def products(self, pe, i, k):
        for q, (w, n, _, _) in enumerate(self.chunks):
            wait(pe, self.s_ev[q], i)
            for z in range(2):
                mm = self.nc.tensor.matmul(self.c.bank[self.fb + q][:, 0:n], self.hT[:, k, z, :], w[:, z, :],
                                           start=(z == 0), stop=(z == 1))
            mm.then_inc(self.s_mm[q], 1)

    def tensor(self, pe, ready=None):
        def body(it, first):
            for k in range(NK):
                i = it * NK + k
                pe.wait_ge(ready or self.s_h, i + 1)
                wait(pe, self.s_ht, i)
                for q in range(2):
                    mm = self.nc.tensor.transpose(self.c.bank[0][:, q * P:(q + 1) * P],
                                                  self.h[:, k, q * P:(q + 1) * P], self.c.ident[:])
                mm.then_inc(self.s_tp, 1)
                pe.wait_ge(self.s_ht, i + 1)
                self.products(pe, i, k)
        self.loop(pe, body)

    def take(self, eng, name, it, i, k):
        for q, (_, n, who, f) in enumerate(self.chunks):
            if who == name:
                eng.wait_ge(self.s_mm[q], i + 1)
                f(eng, it, i, k, self.c.bank[self.fb + q][:, 0:n]).then_inc(self.s_ev[q], 1)

    def ahead(self, eng, name, begin):
        begin(0, 0)

        def body(it, first):
            for k in range(NK):
                i = it * NK + k
                if not (isinstance(i, int) and i == NODE_TILES - 1):
                    begin(i + 1, (k + 1) % NK)
                self.take(eng, name, it, i, k)
        self.loop(eng, body)

    def scalar(self, act, make):
        def begin(i, k):
            wait(act, self.s_tp, i - NK + 1)
            make(i, self.h[:, k, :]).then_inc(self.s_h, 1)
        self.ahead(act, "act", begin)

    def vector(self, v, finish=None):
        def begin(i, k):
            if finish:
                v.wait_ge(self.s_h, i + 1)
                finish(i, self.h[:, k, :])
            v.wait_ge(self.s_tp, i + 1)
            self.nc.vector.tensor_copy(self.hT[:, k, :, :].rearrange("p a b -> p (a b)"),
                                       self.c.bank[0][:, 0:2 * P]).then_inc(self.s_ht, 1)
        self.ahead(v, "dve", begin)


def flat(ap):
    return ap.rearrange("p a b -> p (a b)")


def normed(nc, c, of, func):
    return lambda i, out: nc.scalar.activation(out, flat(of[:, at(i), 0:D]), func, bias=c.nmr[:, at(i)],
                                               scale=c.rs[:, at(i)])


class Store:

    def __init__(self, c, rows, table, signals):
        self.rows, self.table, self.signals = rows, table, signals
        self.s, self.base = c.s_store, c.store_base
        c.store_base += 16 * (NODE_TILES // NK)

    def free(self, eng, it, k):
        wait(eng, self.s[k], it * 16 + self.base)

    def sync(self, sp):
        with sp.Fori(0, NODE_TILES // NK) as it:
            for k in range(NK):
                self.put(sp, it * NK + k, k)
        self.landed(sp)

    def put(self, eng, i, k):
        for s in self.signals:
            eng.wait_ge(s, i + 1)
        eng.dma_start(self.table[at(i * P, P), :], self.rows(k)).then_inc(self.s[k], 16)

    def landed(self, eng):
        for k in range(NK):
            eng.wait_ge(self.s[k], self.base + 16 * (NODE_TILES // NK))


class LayerZero:

    def __init__(self, nc, c, cv, table):
        self.nc, self.c = nc, c
        self.out, self.b12 = cv(NK, D), cv(D)
        self.s_b, self.s_x = c.sem("s_n0_b"), c.sem("s_n0_x")
        self.norm = Norm(nc, c)
        self.prod = Product(nc, c, "n0", cv, [(c.w12[:, :, 0:D], D, "dve", self.keep_x),
                                              (c.w12[:, :, D:2 * D], D, "act", self.keep_table)])
        self.store = Store(c, lambda k: self.out[:, k, :], table, [self.prod.s_ev[1]])

    def keep_x(self, v, it, i, k, ps):
        V, x = self.nc.vector, self.c.X[:, at(i), :]
        V.tensor_tensor(x, ps.unsqueeze(1), x, ALU.add).then_inc(self.s_x, 1)
        v.wait_ge(self.s_x, i + 1)
        return V.tensor_tensor(x, x, self.b12.unsqueeze(1), ALU.add)

    def keep_table(self, act, it, i, k, ps):
        if not (isinstance(i, int) and i == 0):
            self.store.put(act, i - 1, (k - 1) % NK)
        self.store.free(act, it, k)
        return self.nc.scalar.copy(self.out[:, k, :], ps)

    def vector(self, v):
        self.nc.vector.tensor_tensor(self.b12, self.c.b("b1"), self.c.b("b2"), ALU.add).then_inc(self.s_b, 1)
        self.norm.vector(v, self.c.X)
        v.wait_ge(self.s_b, 1)
        self.prod.vector(v)

    def scalar(self, act):
        self.norm.scalar(act)
        self.norm.ready(act)
        self.prod.scalar(act, normed(self.nc, self.c, self.c.X, ACT.Relu))
        self.store.put(act, NODE_TILES - 1, (NODE_TILES - 1) % NK)
        self.store.landed(act)

    def tensor(self, pe):
        self.prod.tensor(pe)


def node_stage_1(nc, c, table, payload):
    cv = Carve(c.work)
    out = cv(NK, N_RELS * D)
    q = flat(c.Q[:, :, :])
    vI, wI = q[:, 0:SLOT_TILES].bitcast(i32), q[:, SLOT_TILES:2 * SLOT_TILES].bitcast(i32)
    relation = q[:, 2 * SLOT_TILES:3 * SLOT_TILES]
    cinv = c.sb("cinv", [P, NODE_TILES], f32)
    s_c = c.sem("s_n1_c")
    s_x = c.sem("s_n1_x")
    norm = Norm(nc, c)

    def add_mean(v, i):
        nc.vector.scalar_tensor_tensor(out=c.X[:, at(i), :], in0=c.AGG[:, at(i), 0:D], scalar=cinv[:, at(i)],
                                       in1=c.X[:, at(i), :], op0=ALU.mult, op1=ALU.add).then_inc(s_x, 1)
        v.wait_ge(s_x, i + 1)

    def keep(q):
        def f(eng, it, i, k, ps):
            store.free(eng, it, k)
            o = out[:, k, q * 2 * D:(q + 1) * 2 * D]
            return nc.scalar.copy(o, ps) if q % 2 == 0 else nc.vector.tensor_copy(o, ps)
        return f

    prod = Product(nc, c, "n1", cv, [(c.wrel[:, :, q * 2 * D:(q + 1) * 2 * D], 2 * D, ("act", "dve")[q % 2], keep(q))
                                     for q in range(N_RELS // 2)])
    store = Store(c, lambda k: out[:, k, :], table, prod.s_ev)

    with nc.Block() as block:
        @block.vector
        def _(v):
            nc.vector.tensor_scalar(cinv[:], c.AGG[:, :, D], 1.0, None, ALU.max).then_inc(s_c, 1)
            v.wait_ge(s_c, 1)
            nc.vector.reciprocal(cinv[:], cinv[:]).then_inc(s_c, 1)
            v.wait_ge(s_c, 2)
            norm.vector(v, c.X, add_mean)
            prod.vector(v)

            def own(ins):
                v.wait_ge(c.own.sem, c.own(ins))
            V = nc.vector
            own(V.tensor_copy(vI, payload[:]))
            own(V.tensor_scalar(wI, vI, 2 * P - 1, None, ALU.bitwise_and))
            V.tensor_scalar(c.lo_d[:], wI, -1.0, float(P), ALU.mult, ALU.add)
            own(V.tensor_scalar(vI, vI, 8, None, ALU.logical_shift_right))
            own(V.tensor_scalar(wI, vI, N_RELS - 1, None, ALU.bitwise_and))
            V.tensor_copy(relation, wI)
            own(V.tensor_scalar(vI, vI, 3, None, ALU.logical_shift_right))
            own(V.tensor_scalar(c.idx_d2[:], vI, -1.0, float(PAD_NODE), ALU.mult, ALU.add))
            V.scalar_tensor_tensor(out=c.idx_d1[:], in0=c.idx_d2[:], scalar=float(N_RELS), in1=relation,
                                   op0=ALU.mult, op1=ALU.add)

        @block.scalar
        def _(act):
            norm.scalar(act)
            norm.ready(act)
            prod.scalar(act, normed(nc, c, c.X, ACT.Relu))

        @block.tensor
        def _(pe):
            prod.tensor(pe)

        @block.sync
        def _(sp):
            store.sync(sp)


def batch_norm_stage(nc, c):
    cv = Carve(c.work)
    sq = cv(NODE_TILES, D)
    neg_mean, scale = cv(D), cv(D)
    s_sum, s_nm, s_cen, s_sq, s_std = (c.sem("s_bn_sum"), c.sem("s_bn_nm"), c.sem("s_bn_cen"), c.sem("s_bn_sq"),
                                       c.sem("s_bn_std"))
    agg = c.AGG[:, :, 0:D]

    with nc.Block() as block:
        @block.tensor
        def _(pe):
            def column_sums(bank, of):
                nc.tensor.matmul(bank[:, 0:D], c.ones[:], of[:, 0, 0:D], start=True, stop=False)
                with pe.Fori(1, NODE_TILES - 1) as i:
                    nc.tensor.matmul(bank[:, 0:D], c.ones[:], of[:, at(i), 0:D], start=False, stop=False)
                nc.tensor.matmul(bank[:, 0:D], c.ones_last[:], of[:, NODE_TILES - 1, 0:D], start=False,
                                 stop=True).then_inc(s_sum, 1)
            column_sums(c.bank[0], c.AGG)
            pe.wait_ge(s_sq, 1)
            column_sums(c.bank[1], sq)

        @block.scalar
        def _(act):
            act.wait_ge(s_sum, 1)
            nc.scalar.mul(neg_mean, c.bank[0][:, 0:D], -1.0 / N_NODES).then_inc(s_nm, 1)
            act.wait_ge(s_cen, 1)
            nc.scalar.activation(sq, agg, ACT.Square).then_inc(s_sq, 1)
            act.wait_ge(s_sum, 2)
            nc.scalar.activation(scale, c.bank[1][:, 0:D], ACT.Sqrt, bias=c.eps[:, 2:3],
                                 scale=1.0 / N_NODES).then_inc(s_std, 1)

        @block.vector
        def _(v):
            def own(ins):
                v.wait_ge(c.own.sem, c.own(ins))

            def rows(ap):
                return ap.unsqueeze(1).broadcast_to([P, NODE_TILES, D])
            v.wait_ge(s_nm, 1)
            nc.vector.tensor_tensor(agg, agg, rows(neg_mean), ALU.add).then_inc(s_cen, 1)
            v.wait_ge(s_std, 1)
            own(nc.vector.reciprocal(scale, scale))
            own(nc.vector.tensor_tensor(scale, scale, c.b("gamma"), ALU.mult))
            own(nc.vector.tensor_tensor(agg, agg, rows(scale), ALU.mult))
            own(nc.vector.tensor_tensor(agg, agg, rows(c.b("beta")), ALU.add))
            own(nc.vector.tensor_tensor(c.X[:, :, :], c.X[:, :, :], agg, ALU.add))


def node_stage_2(nc, c, table):
    cv = Carve(c.work)
    out = cv(NK, 2 * D)
    H = c.AGG
    s_h, s_g, s_hn, s_x = c.sem("s_n2_rows"), c.sem("s_n2_g"), c.sem("s_n2_rows_ready"), c.sem("s_n2_x")
    norm, norm2 = Norm(nc, c), Norm(nc, c)

    def keep_q(act, it, i, k, ps):
        return nc.vector.tensor_tensor(c.Q[:, at(i), :], ps.unsqueeze(1), c.b("bqkv")[:, 0:D].unsqueeze(1), ALU.add)

    def keep_kv(v, it, i, k, ps):
        store.free(v, it, k)
        return nc.vector.tensor_tensor(out[:, k, :], ps, c.b("bqkv")[:, D:3 * D], ALU.add)

    prod = Product(nc, c, "n2", cv, [(c.wqkv[:, :, 0:D], D, "dve", keep_q),
                                     (c.wqkv[:, :, D:3 * D], 2 * D, "dve", keep_kv)])
    store = Store(c, lambda k: out[:, k, :], table, [prod.s_ev[1]])

    with nc.Block() as block:
        @block.vector
        def _(v):
            norm.vector(v, c.X)
            v.wait_ge(s_h, NODE_TILES)
            norm2.vector(v, H)
            nc.vector.tensor_tensor(c.X[:, :, :], c.X[:, :, :], H[:, :, 0:D], ALU.add).then_inc(s_x, 1)
            v.wait_ge(s_x, 1)
            nc.vector.tensor_tensor(c.X[:, :, :], c.X[:, :, :],
                                    c.b("bo").unsqueeze(1).broadcast_to([P, NODE_TILES, D]),
                                    ALU.add).then_inc(s_x, 1)

            def gain_and_bias(i, rows):
                nc.vector.tensor_tensor(rows, rows, c.b("ln_g"), ALU.mult).then_inc(s_g, 1)
                v.wait_ge(s_g, i + 1)
                nc.vector.tensor_tensor(rows, rows, c.b("ln_b"), ALU.add).then_inc(s_hn, 1)
            prod.vector(v, gain_and_bias)

        @block.scalar
        def _(act):
            norm.scalar(act)
            norm.ready(act)
            make = normed(nc, c, c.X, ACT.Relu)
            with act.Fori(0, NODE_TILES) as i:
                make(i, flat(H[:, at(i), 0:D])).then_inc(s_h, 1)
            norm2.scalar(act)
            norm2.ready(act)
            prod.scalar(act, normed(nc, c, H, ACT.Identity))

        @block.tensor
        def _(pe):
            prod.tensor(pe, s_hn)

        @block.sync
        def _(sp):
            store.sync(sp)


class HeadProduct(Product):

    def products(self, pe, i, k):
        (w, _, _, _), (wlr, n, _, _) = self.chunks
        wait(pe, self.s_ev[0], i)
        for z in range(2):
            mm = self.nc.tensor.matmul(self.c.bank[self.fb][0:D_HEAD, 0:P], w[:, z, :], self.hT[:, k, z, :],
                                       start=(z == 0), stop=(z == 1))
        mm.then_inc(self.s_mm[0], 1)
        pe.wait_ge(self.s_ev[0], i + 1)
        wait(pe, self.s_ev[1], i)
        self.nc.tensor.matmul(self.c.bank[self.fb + 1][:, 0:n], self.xT[0:D_HEAD, k, :], wlr, start=True,
                              stop=True).then_inc(self.s_mm[1], 1)


def node_stage_3(nc, c, table):
    cv = Carve(c.work)
    xT = cv(NK, P)
    out = cv(NK, D_HEAD + 2 * HEADS)
    s_el = c.sem("s_n3_el")
    norm = Norm(nc, c)

    def add_x(v, it, i, k, ps):
        return nc.vector.tensor_tensor(c.X[:, at(i), :], ps.unsqueeze(1), c.X[:, at(i), :], ALU.add)

    def keep_xT(act, it, i, k, ps):
        return nc.scalar.copy(xT[0:D_HEAD, k, :], c.bank[5][0:D_HEAD, 0:P])

    def keep_rows(act, it, i, k, ps):
        store.free(act, it, k)
        return nc.scalar.copy(out[:, k, :], ps)

    back = Product(nc, c, "n3o", cv, [(c.wo, D, "dve", add_x)])
    prod = HeadProduct(nc, c, "n3", cv, [(c.w3, P, "act", keep_xT),
                                         (c.wlr[:, :], D_HEAD + 2 * HEADS, "act", keep_rows)], first_bank=5)
    prod.xT = xT
    store = Store(c, lambda k: out[:, k, 0:D_T3], table, [prod.s_ev[1], s_el])

    with nc.Block() as block:
        @block.vector
        def _(v):
            back.vector(v)
            v.wait_ge(back.s_ev[0], NODE_TILES)
            norm.vector(v, c.X)
            prod.vector(v)

        @block.scalar
        def _(act):
            back.scalar(act, lambda i, o: nc.scalar.copy(o, flat(c.AGG[:, at(i), 0:D])))
            norm.scalar(act)
            norm.ready(act)
            prod.scalar(act, normed(nc, c, c.X, ACT.Relu))

        @block.tensor
        def _(pe):
            back.tensor(pe)
            prod.tensor(pe)

        @block.gpsimd
        def _(p):
            with p.Fori(0, NODE_TILES // NK) as it:
                for k in range(NK):
                    i = it * NK + k
                    p.wait_ge(prod.s_ev[1], i + 1)
                    nc.gpsimd.tensor_copy(c.EL[:, at(i), :], out[:, k, D_T3:D_T3 + HEADS].unsqueeze(1)).then_inc(s_el, 1)

        @block.sync
        def _(sp):
            store.sync(sp)


def output_stage(nc, c, out):
    cv = Carve(c.work)
    CH = NK
    low = cv(2, CH * D)
    rinv = c.sb("rinv", [P, NODE_TILES, HEADS], f32)
    s_low, s_exp, s_y, s_o = c.sem("s_out_low"), c.sem("s_out_exp"), c.sem("s_out_y"), c.sem("s_out_dma")
    n_ch = NODE_TILES // CH

    with nc.Block() as block:
        @block.vector
        def _(v):
            def own(ins):
                v.wait_ge(c.own.sem, c.own(ins))
            V = nc.vector
            own(V.tensor_scalar(rinv[:, :, :], c.AGG[:, :, D:D + HEADS], SUM_EPS, None, ALU.max))
            own(V.reciprocal(rinv[:, :, :], rinv[:, :, :]))

            def begin(g):
                y = c.AGG[:, g * CH:(g + 1) * CH, 0:D]
                for i in range(g * CH, (g + 1) * CH):
                    yh = c.AGG[:, i, 0:D].rearrange("p (h d) -> p h d", h=HEADS)
                    own(V.tensor_tensor(yh, yh, rinv[:, i, :].unsqueeze(2).broadcast_to([P, HEADS, D_HEAD]),
                                        ALU.mult))
                    own(V.tensor_tensor(yh, yh, c.b("b3").unsqueeze(1).broadcast_to([P, HEADS, D_HEAD]), ALU.add))
                if g >= 2:
                    v.wait_ge(s_y, g - 1)
                V.tensor_scalar(low[:, g % 2, :].rearrange("p (a b) -> p a b", a=CH), y, 0.0, None,
                                ALU.min).then_inc(s_low, 1)

            def end(g):
                y = c.AGG[:, g * CH:(g + 1) * CH, 0:D]
                x = c.X[:, g * CH:(g + 1) * CH, :]
                e = low[:, g % 2, :].rearrange("p (a b) -> p a b", a=CH)
                v.wait_ge(s_exp, g + 1)
                own(V.scalar_tensor_tensor(out=y, in0=y, scalar=0.0, in1=e, op0=ALU.max, op1=ALU.add))
                V.scalar_tensor_tensor(out=x, in0=y, scalar=-1.0, in1=x, op0=ALU.add, op1=ALU.add).then_inc(s_y, 1)
            begin(0)
            for g in range(n_ch):
                if g + 1 < n_ch:
                    begin(g + 1)
                end(g)

        @block.scalar
        def _(act):
            for g in range(n_ch):
                act.wait_ge(s_low, g + 1)
                nc.scalar.activation(low[:, g % 2, :], low[:, g % 2, :], ACT.Exp).then_inc(s_exp, 1)

        @block.sync
        def _(sp):
            for g in range(n_ch):
                sp.wait_ge(s_y, g + 1)
                full = CH if g < n_ch - 1 else CH - 1
                r0 = g * CH * P
                sp.dma_start(out[r0:r0 + full * P, :].rearrange("(i p) d -> p i d", p=P),
                             c.X[:, g * CH:g * CH + full, :]).then_inc(s_o, 16)
            sp.dma_start(out[(NODE_TILES - 1) * P:N_NODES, :], c.X[0:LAST_ROWS, NODE_TILES - 1, :]).then_inc(s_o, 16)
            sp.wait_ge(s_o, 16 * (n_ch + 1))


class Gather:

    def __init__(self, nc, c, idx, table, rows, n=U):
        self.nc, self.c, self.idx, self.table, self.rows, self.n = nc, c, idx, table, rows, n
        self.s, self.s_ix, self.s_go = c.s_rows, c.s_ix, c.s_go
        self.base, self.ix_base = list(c.rows_base), c.ix_base
        for k in range(n):
            c.rows_base[k] += 16 * (SLOT_TILES // n)
        c.ix_base += SLOT_TILES // G

    def issue(self, p, k):
        p.indirect_dma_start(self.rows(k), None, self.table,
                             bass.IndirectOffsetOnAxis(ap=self.c.ix[:, k:k + 1], axis=0)).then_inc(self.s[k], 16)

    def copy_indices(self, act, it, h):
        for k in range(G * h, G * h + G):
            wait(act, self.s[k], it * 16 + self.base[k])
        self.nc.scalar.copy(self.c.ix[:, G * h:G * h + G], self.idx[:, at(it * self.n + G * h, G)]).then_inc(self.s_ix, 1)

    def gpsimd(self, p, s_used):
        n = self.n

        def body(it, first):
            for k in range(n):
                if k % G == 0:
                    p.wait_ge(self.s_ix, it * (n // G) + (self.ix_base + k // G + 1))
                if not first:
                    p.wait_ge(s_used, (it - 1) * n + k + 1)
                p.sem_inc(self.s_go, 1)
                self.issue(p, k)
        body(0, True)
        with p.Fori(1, SLOT_TILES // n) as it:
            body(it, False)

    def landed(self, eng, it, k):
        eng.wait_ge(self.s[k], it * 16 + (16 + self.base[k]))


def edge_loop(eng, body, n=U):
    last = SLOT_TILES // n - 1
    body(0, True, False)
    with eng.Fori(1, last) as it:
        body(it, False, False)
    body(last, False, True)


class Group:

    def __init__(self, it, q, ahead=0):
        q = q + ahead
        self.it, self.q = it + q // Q4, q % Q4
        self.g = self.it * Q4 + self.q
        self.lives = not isinstance(it, int) or 0 <= self.g < SLOT_TILES // G
        self.slots = range(G * self.q, G * self.q + G)

    def at8(self, j):
        return self.it * (UH // U) + self.q // (U // G), G * self.q % U + j

    def tile(self, j):
        return self.it * UH + G * self.q + j


def sum_stage(nc, c, name, idx, lo, nt, table, counted, carried=None):
    W = D + 1 if counted else D
    cv = Carve(c.work)
    rows, onehot = cv(U, W), cv(U, P)
    s_0, s_oh, s_mm, s_add = c.sem(f"s_{name}_zero"), c.sem(f"s_{name}_oh"), c.sem(f"s_{name}_mm"), c.sem(f"s_{name}_add")
    gather = Gather(nc, c, idx, table, lambda k: rows[:, k, 0:D])
    if carried:
        att_rows, payload = carried
        att = cv(U, ROW)
        s_at = [c.sem(f"s_{name}_att{h}") for h in range(2)]
        s_pay = c.sem(f"s_{name}_pay")

        def load_rows(sp, it, h):
            sp.dma_start(att[:, G * h:G * h + G, :], att_rows[:, at(it * U + G * h, G), :]).then_inc(s_at[h], 16)

        def keep_payload(act, it, h):
            act.wait_ge(s_at[h], it * 16 + 16)
            nc.scalar.copy(payload[:, at(it * U + G * h, G)], att[:, G * h:G * h + G, ROW - 1]).then_inc(s_pay, 1)

    with nc.Block() as block:
        @block.sync
        def _(sp):
            if not carried:
                return
            for h in range(2):
                load_rows(sp, 0, h)
            with sp.Fori(1, SLOT_TILES // U) as it:
                for h in range(2):
                    sp.wait_ge(s_pay, it * 2 + (h - 1))
                    load_rows(sp, it, h)

        @block.gpsimd
        def _(p):
            gather.gpsimd(p, s_mm)

        @block.scalar
        def _(act):
            gather.copy_indices(act, 0, 0)
            gather.copy_indices(act, 0, 1)
            with act.Fori(1, SLOT_TILES // U) as it:
                for h in range(2):
                    gather.copy_indices(act, it, h)
                    if carried:
                        keep_payload(act, it - 1, h)
            if carried:
                for h in range(2):
                    keep_payload(act, SLOT_TILES // U - 1, h)

        @block.tensor
        def _(pe):
            pe.wait_ge(s_0, 2)

            def body(it, first, last):
                for k in range(U):
                    t = it * U + k
                    gather.landed(pe, it, k)
                    pe.wait_ge(s_oh, t + 1)
                    wait(pe, s_add, t - G + 1)
                    nc.tensor.matmul(c.bank[k % G][:, 0:W], onehot[:, k, :], rows[:, k, :], start=True,
                                     stop=True).then_inc(s_mm, 1)
            edge_loop(pe, body)

        @block.vector
        def _(v):
            V = nc.vector
            if counted:
                V.memset(rows[:, :, D:W], 1.0).then_inc(s_0, 1)
            else:
                v.sem_inc(s_0, 1)
            V.memset(c.AGG[:, :, :], 0.0).then_inc(s_0, 1)
            regs = [v.alloc_register(f"{name}_nt{k}") for k in range(U)]

            def build(t, k):
                V.tensor_scalar(onehot[:, k, :], c.iota_f[:], lo[:, at(t)], None, ALU.is_equal).then_inc(s_oh, 1)
            for t in range(G):
                build(t, t)
            v.wait_ge(s_0, 2)

            def body(it, first, last):
                v.load(regs, nt[0:1, at(it * U, U)])
                for k in range(U):
                    t = it * U + k
                    node_tile = v.snap(regs[k], min_val=0, max_val=NODE_TILES - 1)
                    v.wait_ge(s_mm, t + 1)
                    if not (last and k + G >= U):
                        build(t + G, (k + G) % U)
                    wait(v, s_add, t)
                    sums = c.AGG[:, at(node_tile), 0:W]
                    V.tensor_tensor(sums, c.bank[k % G][:, 0:W].unsqueeze(1), sums, ALU.add).then_inc(s_add, 1)
            edge_loop(v, body)


def attention_stage(nc, c, table, att_rows):
    cv = Carve(c.work)
    kv = c.wrel[:, :, :].rearrange("p a (b c) -> p (a b) c", c=2 * D)
    assert 2 * N_RELS * D == U * 2 * D
    dkv = cv(G, 2 * D)
    prod, scratch = cv(2, D), cv(D)
    msg = cv(U, D)
    att = cv(UH, ROW)
    attT, nodeT = cv(2, G, P), cv(2, G, P)
    onehot = cv(UH, P, dt=bf16)
    weighted = cv(G, P)
    dot, act_dot, weight = cv(UH), cv(UH), cv(UH)
    s_att = [c.sem(f"s_l2_att{q}") for q in range(Q4)]
    (s_0, s_oh, s_tr, s_cp, s_dk, s_q, s_si, s_t1, s_dot, s_msg, s_sd, s_w, s_wo, s_mm, s_add) = (
        c.sem(f"s_l2_{n}") for n in ("zero", "oh", "tr", "cp", "dk", "q", "si", "t1", "dot", "msg", "sd", "w", "wo",
                                     "mm", "add"))
    gather = Gather(nc, c, c.idx_d2, table, lambda k: kv[:, k, :])
    b_oT = c.bank[0][:, 0:G * P // 2].bitcast(bf16).rearrange("p (a b) -> p a b", a=G)
    b_aT, b_d, b_q, b_m = c.bank[1], (c.bank[2], c.bank[3]), (c.bank[4], c.bank[5]), (c.bank[6], c.bank[7])

    def steps(eng, step):
        def body(it, first, last):
            for q in range(Q4):
                step(it, q)
        step(0, -1)
        edge_loop(eng, body, UH)

    with nc.Block() as block:
        @block.gpsimd
        def _(p):
            def message(it, it8, k, t, gathers):
                gather.landed(p, it8, k)
                p.wait_ge(s_si, t + 1)
                wait(p, s_mm, t - U + 1)
                nc.gpsimd.tensor_tensor(msg[:, k, :], kv[:, k, D:2 * D], dkv[:, k % G, D:2 * D],
                                        ALU.mult).then_inc(s_msg, 1)
                if gathers:
                    if k % G == 0:
                        p.wait_ge(gather.s_ix, it8 * (U // G) + (gather.ix_base + U // G + k // G + 1))
                    p.wait_ge(s_t1, t + 1)
                    p.wait_ge(s_msg, t + 1)
                    p.sem_inc(gather.s_go, 1)
                    gather.issue(p, k)

            for k in range(U):
                if k % G == 0:
                    p.wait_ge(gather.s_ix, gather.ix_base + k // G + 1)
                gather.issue(p, k)
            last = SLOT_TILES // U - 1
            for k in range(U):
                message(0, 0, k, k, True)
            with p.Fori(1, last) as it:
                for k in range(U):
                    message(it, it, k, it * U + k, True)
            for k in range(U):
                message(last, last, k, last * U + k, False)

        @block.sync
        def _(sp):
            def load(it, q):
                g = it * Q4 + q
                wait(sp, s_w, g - Q4 + 1)
                sp.dma_start(att[:, G * q:G * q + G, :],
                             att_rows[:, at(g * G, G), :]).then_inc(s_att[q], 16)
            for q in range(Q4):
                load(0, q)
            with sp.Fori(1, SLOT_TILES // UH) as it:
                for q in range(Q4):
                    load(it, q)

        @block.tensor
        def _(pe):
            pe.wait_ge(s_0, 1)
            regs = [pe.alloc_register(f"l2_pe_nt{k}") for k in range(UH)]

            def turn(a):
                if not a.lives:
                    return
                pe.wait_ge(s_oh, a.tile(0) + G)
                pe.wait_ge(s_att[a.q], a.it * 16 + 16)
                wait(pe, s_cp, a.g)
                for j, k in enumerate(a.slots):
                    nc.tensor.transpose(b_oT[:, j, :], onehot[:, k, :], c.ident_b[:])
                for j, k in enumerate(a.slots):
                    mm = nc.tensor.transpose(b_aT[0:D_EDGE, j * P:(j + 1) * P], att[:, k, 0:D_EDGE], c.ident[:])
                mm.then_inc(s_tr, 1)

            def dots(a, j):
                if not a.lives:
                    return
                t = a.tile(j)
                if j == 0:
                    pe.wait_ge(s_cp, a.g + 1)
                    if a.q == 0:
                        pe.load(regs, c.nt_d[0:1, at(a.it * UH, UH)])
                wait(pe, s_si, t - 1)
                nc.tensor.matmul(b_d[j % 2][:, :], attT[0:D_EDGE + 1, a.q % 2, j, :], c.wd[:, :], start=True,
                                 stop=True).then_inc(s_dk, 1)
                wait(pe, s_t1, t - 1)
                node_tile = pe.snap(regs[a.slots[j]], min_val=0, max_val=NODE_TILES - 1)
                nc.tensor.matmul(b_q[j % 2][:, 0:D], nodeT[:, a.q % 2, j, :], c.Q[:, at(node_tile), :], start=True,
                                 stop=True).then_inc(s_q, 1)

            def sums(a, j):
                if not a.lives:
                    return
                t = a.tile(j)
                pe.wait_ge(s_wo, t + 1)
                pe.wait_ge(s_msg, t + 1)
                wait(pe, s_add, t)
                nc.tensor.matmul(b_m[j % 2][:, 0:D], weighted[:, j, :], msg[:, a.slots[j] % U, :], start=True,
                                 stop=True).then_inc(s_mm, 1)

            turn(Group(0, 0))

            def step(it, q):
                dots(Group(it, q, 1), 0)
                sums(Group(it, q, -1), 2)
                dots(Group(it, q, 1), 1)
                sums(Group(it, q, -1), 3)
                turn(Group(it, q, 2))
                dots(Group(it, q, 1), 2)
                sums(Group(it, q), 0)
                dots(Group(it, q, 1), 3)
                sums(Group(it, q), 1)
            steps(pe, step)
            for j in (2, 3):
                sums(Group(SLOT_TILES // UH - 1, Q4 - 1), j)

        @block.scalar
        def _(act):
            gather.copy_indices(act, 0, 0)
            gather.copy_indices(act, 0, 1)

            def copy(a):
                if not a.lives:
                    return
                act.wait_ge(s_tr, a.g + 1)
                wait(act, s_q, (a.g - 1) * G)
                nc.scalar.copy(flat(nodeT[:, a.q % 2, :, :]), flat(b_oT))
                nc.scalar.copy(flat(attT[0:D_EDGE, a.q % 2, :, :]), b_aT[0:D_EDGE, :]).then_inc(s_cp, 1)

            def silu(a, j):
                if not a.lives:
                    return
                t = a.tile(j)
                act.wait_ge(s_dk, t + 1)
                wait(act, s_dot, t - G + 1)
                wait(act, s_msg, t - G + 1)
                nc.scalar.activation(dkv[:, j, :], b_d[j % 2][:, :], ACT.Silu).then_inc(s_si, 1)

            def silu_dot(a):
                if not a.lives:
                    return
                act.wait_ge(s_dot, a.tile(0) + G)
                wait(act, s_w, a.g - Q4 + 1)
                nc.scalar.activation(act_dot[:, a.slots[0]:a.slots[-1] + 1], dot[:, a.slots[0]:a.slots[-1] + 1],
                                     ACT.Silu).then_inc(s_sd, 1)

            def weigh(a, j):
                if not a.lives:
                    return
                act.wait_ge(s_w, a.g + 1)
                wait(act, s_mm, a.tile(j) - G + 1)
                k = a.slots[j]
                nc.scalar.activation(weighted[:, j, :], onehot[:, k, :], ACT.Copy,
                                     scale=weight[:, k:k + 1]).then_inc(s_wo, 1)

            act.wait_ge(s_0, 1)
            copy(Group(0, 0))

            def step(it, q):
                silu(Group(it, q, 1), 0)
                silu_dot(Group(it, q))
                silu(Group(it, q, 1), 1)
                weigh(Group(it, q), 0)
                a = Group(it, q, 3)
                if a.lives:
                    it8, k = a.at8(0)
                    gather.copy_indices(act, it8, k // G)
                copy(Group(it, q, 2))
                silu(Group(it, q, 1), 2)
                weigh(Group(it, q), 1)
                silu(Group(it, q, 1), 3)
                weigh(Group(it, q), 2)
                weigh(Group(it, q), 3)
            steps(act, step)

        @block.vector
        def _(v):
            V = nc.vector
            V.memset(attT[D_EDGE:D_EDGE + 1, :, :, :], 1.0).then_inc(s_0, 1)
            V.memset(c.AGG[:, :, :], 0.0).then_inc(s_add, 1)
            regs = [v.alloc_register(f"l2_nt{k}") for k in range(UH)]

            def build(a, j):
                if not a.lives:
                    return
                wait(v, s_wo, a.tile(j) - UH + 1)
                V.tensor_scalar(onehot[:, a.slots[j], :], c.iota_b[:], c.lo_d[:, at(a.tile(j))], None,
                                ALU.is_equal).then_inc(s_oh, 1)

            def q_times_k(a, j):
                if not a.lives:
                    return
                t = a.tile(j)
                it8, k = a.at8(j)
                gather.landed(v, it8, k)
                v.wait_ge(s_q, t + 1)
                wait(v, s_dot, t - 1)
                V.tensor_tensor(prod[:, j % 2, :], b_q[j % 2][:, 0:D], kv[:, k, 0:D], ALU.mult).then_inc(s_t1, 1)

            def times_dk(a, j):
                if not a.lives:
                    return
                t, k = a.tile(j), a.slots[j]
                v.wait_ge(s_si, t + 1)
                v.wait_ge(s_t1, t + 1)
                wait(v, s_sd, a.g - Q4 + 1)
                wait(v, s_dot, t)
                V.tensor_tensor_reduce(scratch, prod[:, j % 2, :], dkv[:, j, 0:D], 1.0, 0.0, ALU.mult,
                                       ALU.add, dot[:, k:k + 1]).then_inc(s_dot, 1)

            def weights(a):
                if not a.lives:
                    return
                v.wait_ge(s_sd, a.g + 1)
                s0, s1 = a.slots[0], a.slots[-1] + 1
                V.tensor_tensor(weight[:, s0:s1], act_dot[:, s0:s1], att[:, s0:s1, D_EDGE], ALU.mult).then_inc(s_w, 1)

            def add(a, j):
                if not a.lives:
                    return
                t = a.tile(j)
                node_tile = v.snap(regs[a.slots[j]], min_val=0, max_val=NODE_TILES - 1)
                v.wait_ge(s_mm, t + 1)
                v.wait_ge(s_add, t + 1)
                o = c.AGG[:, at(node_tile), 0:D]
                V.tensor_tensor(o, b_m[j % 2][:, 0:D].unsqueeze(1), o, ALU.add).then_inc(s_add, 1)

            for q in range(2):
                for j in range(G):
                    build(Group(0, q), j)

            def step(it, q):
                for j in range(G):
                    q_times_k(Group(it, q, 1), j)
                    add(Group(it, q, -1), j + 1) if j < 3 else add(Group(it, q), 0)
                    if j == 2 and q == 0:
                        v.load(regs, c.nt_d[0:1, at(it * UH, UH)])
                    build(Group(it, q, 3), j)
                    times_dk(Group(it, q, 1), j)
                    if j == 0:
                        weights(Group(it, q))
            steps(v, step)
            for j in (1, 2, 3):
                add(Group(SLOT_TILES // UH - 1, Q4 - 1), j)


def head_stage(nc, c, table):
    cv = Carve(c.work)
    rows, msg, onehot, nodeT = cv(UH, D_T3), cv(UH, AGG_W), cv(UH, P), cv(2, G, P)
    z, z2 = cv(2, G, HEADS), cv(2, G, HEADS)
    s_0, s_oh, s_tr, s_cp, s_el, s_z, s_lk, s_e, s_msg, s_mm, s_add = (
        c.sem(f"s_l3_{n}") for n in ("zero", "oh", "tr", "cp", "el", "z", "lk", "e", "msg", "mm", "add"))
    gather = Gather(nc, c, c.idx_s, table, lambda k: rows[:, k, :], UH)
    b_oT, b_el, b_m = (c.bank[0], c.bank[1]), (c.bank[2], c.bank[3]), c.bank[4:8]
    def steps(eng, step):
        def body(it, first, last):
            for q in range(Q4):
                step(it, q)
        edge_loop(eng, body, UH)

    with nc.Block() as block:
        @block.gpsimd
        def _(p):
            gather.gpsimd(p, s_msg)

        @block.tensor
        def _(pe):
            regs = [pe.alloc_register(f"l3_pe_nt{k}") for k in range(UH)]

            def turn(a):
                if not a.lives:
                    return
                pe.wait_ge(s_oh, a.tile(0) + G)
                wait(pe, s_cp, a.g - 1)
                for j, k in enumerate(a.slots):
                    mm = nc.tensor.transpose(b_oT[a.q % 2][:, j * P:(j + 1) * P], onehot[:, k, :], c.ident[:])
                mm.then_inc(s_tr, 1)

            def el(a):
                if not a.lives:
                    return
                if a.q == 0:
                    pe.load(regs, c.nt_s[0:1, at(a.it * UH, UH)])
                pe.wait_ge(s_cp, a.g + 1)
                wait(pe, s_z, a.g - 1)
                for j, k in enumerate(a.slots):
                    node_tile = pe.snap(regs[k], min_val=0, max_val=NODE_TILES - 1)
                    mm = nc.tensor.matmul(b_el[a.q % 2][:, j * HEADS:(j + 1) * HEADS], nodeT[:, a.q % 2, j, :],
                                          c.EL[:, at(node_tile), :], start=True, stop=True)
                mm.then_inc(s_el, 1)

            def sums(a):
                for j, k in enumerate(a.slots):
                    pe.wait_ge(s_msg, a.tile(j) + 1)
                    wait(pe, s_add, a.tile(j) - G + 1)
                    nc.tensor.matmul(b_m[j][:, 0:AGG_W], onehot[:, k, :], msg[:, k, :], start=True,
                                     stop=True).then_inc(s_mm, 1)

            turn(Group(0, 0))
            turn(Group(0, 1))
            el(Group(0, 0))

            def step(it, q):
                el(Group(it, q, 1))
                turn(Group(it, q, 2))
                sums(Group(it, q))
            steps(pe, step)

        @block.scalar
        def _(act):
            for q in range(Q4):
                gather.copy_indices(act, 0, q)

            def copy(a):
                if not a.lives:
                    return
                act.wait_ge(s_tr, a.g + 1)
                wait(act, s_el, a.g - 1)
                nc.scalar.copy(flat(nodeT[:, a.q % 2, :, :]), b_oT[a.q % 2][:, :]).then_inc(s_cp, 1)

            def exp(a):
                if not a.lives:
                    return
                act.wait_ge(s_lk, a.g + 1)
                wait(act, s_mm, (a.g - Q4 + 1) * G)
                nc.scalar.activation(msg[:, a.slots[0]:a.slots[-1] + 1, D:AGG_W], z2[:, a.q % 2, :, :],
                                     ACT.Exp).then_inc(s_e, 1)

            copy(Group(0, 0))
            copy(Group(0, 1))
            exp(Group(0, 0))

            def step(it, q):
                copy(Group(it, q, 2))
                exp(Group(it, q, 1))
                if not isinstance(it, int) or it < SLOT_TILES // UH - 1:
                    gather.copy_indices(act, it + 1, q)
            steps(act, step)

        @block.vector
        def _(v):
            V = nc.vector
            V.memset(c.AGG[:, :, :], 0.0).then_inc(s_0, 1)
            v.wait_ge(s_0, 1)
            regs = [v.alloc_register(f"l3_nt{k}") for k in range(UH)]

            def build(a, j):
                if not a.lives:
                    return
                wait(v, s_mm, a.tile(j) - UH + 1)
                V.tensor_scalar(onehot[:, a.slots[j], :], c.iota_f[:], c.lo_s[:, at(a.tile(j))], None,
                                ALU.is_equal).then_inc(s_oh, 1)

            def leaky(a):
                if not a.lives:
                    return
                for k in a.slots:
                    gather.landed(v, a.it, k)
                v.wait_ge(s_el, a.g + 1)
                V.tensor_tensor(z[:, a.q % 2, :, :], b_el[a.q % 2][:, 0:G * HEADS].rearrange("p (a b) -> p a b", a=G),
                                rows[:, a.slots[0]:a.slots[-1] + 1, D_HEAD:D_T3], ALU.add).then_inc(s_z, 1)
                v.wait_ge(s_z, a.g + 1)
                wait(v, s_e, a.g - 1)
                V.scalar_tensor_tensor(out=z2[:, a.q % 2, :, :], in0=z[:, a.q % 2, :, :], scalar=0.2,
                                       in1=z[:, a.q % 2, :, :], op0=ALU.mult, op1=ALU.max).then_inc(s_lk, 1)

            def message(a, j):
                v.wait_ge(s_e, a.g + 1)
                k = a.slots[j]
                V.tensor_tensor(msg[:, k, 0:D].rearrange("p (h d) -> p h d", h=HEADS),
                                rows[:, k, 0:D_HEAD].unsqueeze(1).broadcast_to([P, HEADS, D_HEAD]),
                                msg[:, k, D:AGG_W].unsqueeze(2).broadcast_to([P, HEADS, D_HEAD]),
                                ALU.mult).then_inc(s_msg, 1)

            def add(a, j):
                if not a.lives:
                    return
                node_tile = v.snap(regs[a.slots[j]], min_val=0, max_val=NODE_TILES - 1)
                v.wait_ge(s_mm, a.tile(j) + 1)
                wait(v, s_add, a.tile(j))
                o = c.AGG[:, at(node_tile), :]
                V.tensor_tensor(o, b_m[j][:, 0:AGG_W].unsqueeze(1), o, ALU.add).then_inc(s_add, 1)

            for q in range(3):
                for j in range(G):
                    build(Group(0, q), j)
            leaky(Group(0, 0))

            def step(it, q):
                for j in range(G):
                    message(Group(it, q), j)
                    add(Group(it, q, -1), j)
                    if j == G - 1 and q == 0:
                        v.load(regs, c.nt_s[0:1, at(it * UH, UH)])
                    build(Group(it, q, 3), j)
                    if j == 1:
                        leaky(Group(it, q, 1))
            steps(v, step)
            for j in range(G):
                add(Group(SLOT_TILES // UH - 1, Q4 - 1), j)


def program(nc, src, dst, typ, wgt, attr, x, w12, wrel, wqkv, wo, wd, w3, wlr, bias, out):
    def dram(name, shape):
        return nc.dram_tensor(name, shape, f32, kind="Internal").ap()
    t0, t1 = dram("rows_w2", (NODE_ROWS, D)), dram("rows_rel", (NODE_ROWS, N_RELS * D))
    t2, t3 = dram("rows_kv", (NODE_ROWS, 2 * D)), dram("rows_head", (NODE_ROWS, D_T3))
    att_rows = dram("att_rows", (SLOTS, ROW))
    with ExitStack() as ctx:
        c = Chip(nc, ctx)
        weights = [(c.w12[:, :, :], w12.rearrange("(z p) n -> p z n", p=P)),
                   (c.wrel[:, :, :], wrel.rearrange("(z p) n -> p z n", p=P)),
                   (c.wqkv[:, :, :], wqkv.rearrange("(z p) n -> p z n", p=P)),
                   (c.wo[:, :, :], wo.rearrange("(z p) n -> p z n", p=P)),
                   (c.wd[:, :], wd), (c.w3[:, :, :], w3.rearrange("(z p) n -> p z n", p=P)),
                   (c.wlr[:, :], wlr), (c.bias[:, :], bias.broadcast_to([P, BIAS_W]))]
        with ExitStack() as ctx2:
            prep = Prep(nc, c, ctx2)
            load_stage(nc, c, src, dst, typ, wgt, x, weights, att_rows, prep)
            edge_stage(nc, c, attr, att_rows, t0, prep)
        slot_rows = att_rows.rearrange("(p t) c -> p t c", p=P)
        payload = c.sb("payload", [P, SLOT_TILES], f32)
        sum_stage(nc, c, "l0", c.idx_s, c.lo_s, c.nt_s, t0, True, (slot_rows, payload))
        node_stage_1(nc, c, t1, payload)
        sum_stage(nc, c, "l1", c.idx_d1, c.lo_d, c.nt_d, t1.rearrange("n (r d) -> (n r) d", r=N_RELS), False)
        batch_norm_stage(nc, c)
        node_stage_2(nc, c, t2)
        attention_stage(nc, c, t2, slot_rows)
        node_stage_3(nc, c, t3)
        head_stage(nc, c, t3)
        output_stage(nc, c, out)


def kernel(x, src, dst, edge_attr_64, edge_type_8, edge_weight, L0_gnn_W1, L0_gnn_b1, L0_gnn_W2, L0_gnn_b2,
           L1_gnn_weight, L1_gnn_gamma, L1_gnn_beta, L2_gnn_ln_g, L2_gnn_ln_b, L2_gnn_Wq, L2_gnn_bq, L2_gnn_Wk,
           L2_gnn_bk, L2_gnn_Wv, L2_gnn_bv, L2_gnn_Wo, L2_gnn_bo, L2_gnn_Wdk, L2_gnn_bdk, L2_gnn_Wdv, L2_gnn_bdv,
           L3_gnn_W, L3_gnn_Wl, L3_gnn_Wr, L3_gnn_b):
    import concourse.bacc as bacc
    from concourse.bass_utils import run_bass_kernel_spmd

    def edges(a, pad):
        a = np.asarray(a)
        full = np.full((EDGE_ROWS,) + a.shape[1:], pad, a.dtype)
        full[:N_EDGES] = a
        return full.reshape((P, EDGE_COLS) + a.shape[1:])

    def turned(*ws):
        return np.ascontiguousarray(np.concatenate([np.asarray(w).T for w in ws], axis=1))

    xs = np.zeros((NODE_ROWS, D), np.float32)
    xs[:N_NODES] = np.asarray(x)
    ins = {
        "src": edges(src, PAD_NODE), "dst": edges(dst, PAD_NODE), "typ": edges(edge_type_8, 0),
        "wgt": edges(edge_weight, 0), "attr": edges(edge_attr_64, 0), "x": xs,
        "w12": turned(L0_gnn_W1, L0_gnn_W2),
        "wrel": np.ascontiguousarray(np.asarray(L1_gnn_weight).transpose(1, 0, 2).reshape(D, N_RELS * D)),
        "wqkv": turned(L2_gnn_Wq, L2_gnn_Wk, L2_gnn_Wv), "wo": turned(L2_gnn_Wo),
        "wd": np.concatenate([turned(L2_gnn_Wdk, L2_gnn_Wdv),
                              np.concatenate([np.asarray(L2_gnn_bdk), np.asarray(L2_gnn_bdv)])[None]]),
        "w3": np.asarray(L3_gnn_W),
        "wlr": np.concatenate([np.eye(D_HEAD, dtype=np.float32), turned(L3_gnn_Wr, L3_gnn_Wl)], axis=1),
        "bias": np.concatenate([np.asarray(a) for a in (
            L0_gnn_b1, L0_gnn_b2, L1_gnn_gamma, L1_gnn_beta, L2_gnn_ln_g, L2_gnn_ln_b, L2_gnn_bq, L2_gnn_bk,
            L2_gnn_bv, L2_gnn_bo, L3_gnn_b)])[None],
    }
    nc = bacc.Bacc("TRN2", target_bir_lowering=False, num_devices=1)
    aps = {k: nc.dram_tensor("in_" + k, a.shape, mybir.dt.from_np(a.dtype), kind="ExternalInput").ap()
           for k, a in ins.items()}
    out = nc.dram_tensor("out_0", (N_NODES, D), f32, kind="ExternalOutput").ap()
    program(nc, *[aps[k] for k in ("src", "dst", "typ", "wgt", "attr", "x", "w12", "wrel", "wqkv", "wo", "wd", "w3",
                                   "wlr", "bias")], out)
    r = run_bass_kernel_spmd(nc, [{"in_" + k: a for k, a in ins.items()}], core_ids=[0])
    return r.results[0]["out_0"]
```

```python
import numpy as np
import concourse.bass as bass
import concourse.mybir as mybir
from contextlib import ExitStack

P = 128
N_NODES, N_EDGES, D, D_EDGE, N_RELS, HEADS, D_HEAD = 3125, 50000, 256, 64, 8, 4, 64
NODE_TILES = -(-N_NODES // P)
NODE_ROWS = NODE_TILES * P
PAD_NODE = NODE_ROWS - 1
LAST_ROWS = N_NODES - (NODE_TILES - 1) * P
EDGE_COLS = 8 * -(-N_EDGES // (8 * P))
EDGE_ROWS = EDGE_COLS * P
SLOT_TILES = (EDGE_COLS + NODE_TILES - 1) // 8 * 8
SLOTS = SLOT_TILES * P
ROW = D_EDGE + 2
PART_BITS = 10
PART = 1 << PART_BITS
AGG_W = D + HEADS
LN_EPS, BN_EPS, SUM_EPS = 1e-5, 1e-5, 1e-12
U = 8
UH = 16
G = 4
Q4 = UH // G
NK = 5
SCATTER_0 = 21
WORK = 12800
Q3_AT = WORK - NODE_TILES * D // 2
D_T3 = D_HEAD + HEADS

f32, bf16, f16, i32 = mybir.dt.float32, mybir.dt.bfloat16, mybir.dt.float16, mybir.dt.int32
ALU = mybir.AluOpType
ACT = mybir.ActivationFunctionType
AXX = mybir.AxisListType.X
assert PAD_NODE * 2 * P + P < PART * PART
assert EDGE_COLS * P + NODE_TILES * (P - 1) < (SLOT_TILES + 1) * P

BIAS = {}
_at = 0
for _n, _w in (("b1", D), ("b2", D), ("gamma", D), ("beta", D), ("ln_g", D), ("ln_b", D),
               ("bqkv", 3 * D), ("bo", D), ("b3", D_HEAD)):
    BIAS[_n] = (_at, _at + _w)
    _at += _w
BIAS_W = _at


def wait(eng, sem, value):
    if isinstance(value, int) and value <= 0:
        return
    eng.wait_ge(sem, value)


def at(t, n=1):
    return bass.ds(t, n)


class Chip:

    def __init__(self, nc, ctx):
        self.nc, self.ctx = nc, ctx
        sb, ps = self.sb, self.ps
        self.X = sb("X", [P, NODE_TILES, D], f32)
        self.AGG = sb("AGG", [P, NODE_TILES, AGG_W], f32)
        self.Q = sb("Q", [P, NODE_TILES, D], f32)
        self.work = sb("work", [P, WORK], f32)
        q12 = self.Q[:, :, :].rearrange("p a b -> p (a b)").bitcast(bf16)
        q12 = q12.rearrange("p (i z d) -> p i z d", z=2, d=D)
        q3 = self.work[:, Q3_AT:WORK].bitcast(bf16).rearrange("p (i d) -> p i d", d=D)
        self.q_parts = [lambda i: q12[:, at(i), 0, :], lambda i: q12[:, at(i), 1, :], lambda i: q3[:, at(i), :]]
        self.w12 = sb("w12", [P, 2, 2 * D], f32)
        self.wrel = sb("wrel", [P, 2, N_RELS * D], f32)
        self.wqkv = sb("wqkv", [P, 2, 3 * D], f32)
        self.wo = sb("wo", [P, 2, D], f32)
        self.wd = sb("wd", [D_EDGE + 1, 2 * D], f32)
        self.w3 = sb("w3", [P, 2, D_HEAD], f32)
        self.wlr = sb("wlr", [D_HEAD, D_HEAD + 2 * HEADS], f32)
        self.bias = sb("bias", [P, BIAS_W], f32)
        self.iota_f = sb("iota_f", [P, P], f32)
        self.iota_b = sb("iota_b", [P, P], bf16)
        self.iota_slot = sb("iota_slot", [P, SLOT_TILES], f16)
        self.ident = sb("ident", [P, P], f32)
        self.ident_b = sb("ident_b", [P, P], bf16)
        self.lower = sb("lower", [P, P], f32)
        self.ones = sb("ones", [P, P], f32)
        self.ones_last = sb("ones_last", [P, P], f32)
        self.eps = sb("eps", [P, 3], f32)
        self.idx_s = sb("idx_s", [P, SLOT_TILES], i32)
        self.idx_d1 = sb("idx_d1", [P, SLOT_TILES], i32)
        self.idx_d2 = sb("idx_d2", [P, SLOT_TILES], i32)
        self.lo_s = sb("lo_s", [P, SLOT_TILES], f32)
        self.lo_d = sb("lo_d", [P, SLOT_TILES], f32)
        self.nt_s = sb("nt_s", [1, SLOT_TILES], i32)
        self.nt_d = sb("nt_d", [1, SLOT_TILES], i32)
        self.bank = [ps(f"bank{k}", [P, 512], f32) for k in range(8)]
        self.ix = sb("ix", [P, UH], i32)
        self.EL = sb("EL", [P, NODE_TILES, HEADS], f32)
        self.mv = sb("mv", [P, NODE_TILES, 2], f32)
        self.st = sb("st", [P, NODE_TILES, 6], f32)
        self.rs = sb("rs", [P, NODE_TILES], f32)
        self.nmr = sb("nmr", [P, NODE_TILES], f32)
        self.s_rows = [self.sem(f"s_rows{k}") for k in range(UH)]
        self.rows_base = [0] * UH
        self.s_ix, self.s_go = self.sem("s_ix"), self.sem("s_go")
        self.ix_base = 0
        self.s_store = [self.sem(f"s_store{k}") for k in range(NK)]
        self.store_base = 0
        self.s_st, self.s_sq, self.s_rs = self.sem("s_stats"), self.sem("s_sqrt"), self.sem("s_rstd")
        self.norms = 0
        self.own = Own(self.sem("s_own"))

    def sb(self, name, shape, dt):
        return self.ctx.enter_context(self.nc.sbuf_tensor(name, shape, dt))

    def ps(self, name, shape, dt):
        return self.ctx.enter_context(self.nc.psum_tensor(name, shape, dt))

    def sem(self, name):
        return self.ctx.enter_context(self.nc.semaphore(name))

    def b(self, name):
        return self.bias[:, BIAS[name][0]:BIAS[name][1]]


class Own:

    def __init__(self, sem):
        self.sem, self.n = sem, 0

    def __call__(self, ins):
        self.n += 1
        ins.then_inc(self.sem, 1)
        return self.n


class Carve:

    def __init__(self, work):
        self.work, self.n = work, 0

    def __call__(self, *shape, dt=f32):
        n = int(np.prod(shape))
        words = n if dt not in (bf16, f16) else (n + 1) // 2
        v = self.work[:, self.n:self.n + words]
        self.n += words
        assert self.n <= WORK, self.n
        if dt != f32:
            v = v.bitcast(dt)
        names = "abcd"[:len(shape)]
        if len(shape) > 1:
            v = v.rearrange(f"p ({' '.join(names)}) -> p {' '.join(names)}", **dict(zip(names, shape)))
        return v


class Prep:

    def __init__(self, nc, c, ctx):
        def sb(name, shape, dt=f32):
            return ctx.enter_context(nc.sbuf_tensor(name, shape, dt))
        self.carry = c.sb("carry", [P, EDGE_COLS, ROW - D_EDGE], f32)
        self.slot_d = c.sb("slot_d", [P, EDGE_COLS], i32)
        self.pos_lo, self.pos_hi = sb("pos_lo", [P, EDGE_COLS]), sb("pos_hi", [P, EDGE_COLS])
        self.part = sb("part", [P, 2, EDGE_COLS])
        self.small = sb("rank_small", [P, 8, NODE_TILES + 1])
        self.smallI = sb("rank_smallI", [P, NODE_TILES], i32)
        self.tile_no = sb("tile_no", [P, SLOT_TILES])
        self.one_bf = c.Q[:, :, :].rearrange("p a b -> p (a b)").bitcast(bf16)[:, 0:NODE_TILES * EDGE_COLS]
        self.one3 = self.one_bf.rearrange("p (b t) -> p b t", b=NODE_TILES)
        self.scan = c.work[:, 0:NODE_TILES * EDGE_COLS]
        self.scan3 = self.scan.rearrange("p (b t) -> p b t", b=NODE_TILES)
        agg = c.AGG[:, :, :].rearrange("p a b -> p (a b)")
        cols = [agg[:, k * EDGE_COLS:(k + 1) * EDGE_COLS] for k in range(14)]
        self.src, self.dst, self.typ = (a.bitcast(i32) for a in cols[0:3])
        self.w_in = cols[3]
        self.tI = [a.bitcast(i32) for a in cols[4:8]]
        self.tF = cols[8:12]
        self.keyb = cols[12].bitcast(bf16)[:, 0:EDGE_COLS]
        self.cmp = agg[0:NODE_TILES - 1, 14 * EDGE_COLS:14 * EDGE_COLS + SLOT_TILES]
        self.s_in, self.s_mm = c.sem("s_rank_in"), c.sem("s_rank_mm")


class Ranks:

    def __init__(self, nc, c, prep, n, key, nt, banks):
        self.nc, self.c, self.prep, self.n, self.key, self.nt, self.banks = nc, c, prep, n, key, nt, banks

    def tensor(self, pe):
        nc, c, r = self.nc, self.c, self.prep
        below, all_, ends, tiles = self.banks
        B = NODE_TILES
        pe.wait_ge(r.s_in, 3 * self.n + 1)
        nc.tensor.matmul(below[:, 0:B], c.lower[:], r.small[:, 1, 0:B], start=True, stop=True)
        nc.tensor.matmul(all_[:, 0:B], c.ones[:], r.small[:, 1, 0:B], start=True, stop=True).then_inc(r.s_mm, 1)
        pe.wait_ge(r.s_in, 3 * self.n + 2)
        nc.tensor.transpose(ends[0:B, 0:P], r.small[:, 3, 0:B], c.ident[:]).then_inc(r.s_mm, 1)
        pe.wait_ge(r.s_in, 3 * self.n + 3)
        nc.tensor.matmul(tiles[0:1, 0:SLOT_TILES], c.ones[0:B - 1, 0:1], r.cmp, start=True,
                         stop=True).then_inc(r.s_mm, 1)

    def vector(self, v):
        nc, c, r, V = self.nc, self.c, self.prep, self.nc.vector
        below, all_, ends, tiles = self.banks
        B = NODE_TILES
        small = r.small
        cum, cnt, used, end, off, one_end = (small[:, j, 0:B] for j in range(6))

        def own(ins):
            v.wait_ge(c.own.sem, c.own(ins))
        V.tensor_scalar(r.tI[1], self.key, P - 1, None, ALU.bitwise_and)
        own(V.tensor_scalar(r.tI[0], self.key, 7, None, ALU.logical_shift_right))
        V.tensor_copy(r.tF[1], r.tI[1])
        own(V.tensor_copy(r.keyb, r.tI[0]))
        for b in range(B):
            ins = V.tensor_scalar(r.one3[:, b, :], r.keyb, float(b), None, ALU.is_equal)
        own(ins)
        V.memset(small[:, 0, 0:1], 0.0)
        own(V.tensor_tensor_scan(r.scan, r.one_bf, r.one_bf, 0.0, ALU.add, ALU.max))
        own(V.tensor_copy(small[:, 0, 1:B + 1], r.scan3[:, :, EDGE_COLS - 1]))
        V.tensor_tensor(cnt, small[:, 0, 1:B + 1], cum, ALU.subtract).then_inc(r.s_in, 1)
        v.wait_ge(r.s_mm, 3 * self.n + 1)
        own(V.tensor_scalar(used, all_[:, 0:B], float(P - 1), None, ALU.add))
        own(V.tensor_copy(r.smallI[:], used))
        own(V.tensor_scalar(r.smallI[:], r.smallI[:], 7, None, ALU.logical_shift_right))
        own(V.tensor_copy(used, r.smallI[:]))
        own(V.tensor_tensor_scan(end, used, used, 0.0, ALU.add, ALU.max))
        V.tensor_tensor(off, end, used, ALU.subtract).then_inc(r.s_in, 1)
        v.wait_ge(r.s_in, 3 * self.n + 2)
        own(V.scalar_tensor_tensor(out=off, in0=off, scalar=float(P), in1=below[:, 0:B], op0=ALU.mult, op1=ALU.add))
        own(V.scalar_tensor_tensor(out=off, in0=off, scalar=-1.0, in1=cum, op0=ALU.add, op1=ALU.subtract))
        for b in range(B):
            ins = V.scalar_tensor_tensor(out=r.scan3[:, b, :], in0=r.scan3[:, b, :], scalar=small[:, 4, b:b + 1],
                                         in1=r.one3[:, b, :], op0=ALU.add, op1=ALU.mult)
        placed = c.own(ins)
        v.wait_ge(r.s_mm, 3 * self.n + 2)
        own(V.tensor_copy(small[0:B - 1, 5, 0:1], ends[0:B - 1, 0:1]))
        V.tensor_scalar(r.cmp, r.tile_no[0:B - 1, :], small[0:B - 1, 5, 0:1], None, ALU.is_ge).then_inc(r.s_in, 1)
        v.wait_ge(c.own.sem, placed)
        own(V.tensor_reduce(r.tF[2], r.scan3.rearrange("p b t -> p t b"), AXX, ALU.add))
        v.wait_ge(r.s_mm, 3 * self.n + 3)
        V.tensor_copy(self.nt[:], tiles[0:1, 0:SLOT_TILES])
        own(V.tensor_copy(r.tI[0], r.tF[2]))


def rank_stage(nc, c, src, dst, typ, wgt, att_rows, prep):
    s_key, s_zero, s_fill = c.sem("s_key"), c.sem("s_zero"), c.sem("s_fill")
    s_const, s_sin, s_turn, s_cst = c.sem("s_const"), c.sem("s_sin"), c.sem("s_turn"), c.sem("s_cst_own")
    ztiles = 32
    zeros = c.work[:, WORK - ztiles * ROW:WORK]
    tF, tI = prep.tF, prep.tI
    ranks = Ranks(nc, c, prep, 0, prep.dst, c.nt_d, c.bank[0:4])

    with nc.Block() as block:
        @block.sync
        def _(sp):
            for into, a in ((prep.w_in, wgt), (prep.dst, dst), (prep.src, src), (prep.typ, typ)):
                sp.dma_start(into, a[:, :]).then_inc(s_key, 16)
            sp.wait_ge(s_zero, 1)
            dest = att_rows.rearrange("(p r) c -> p (r c)", p=P)
            fills = SLOT_TILES // ztiles
            for k in range(fills):
                sp.dma_start(dest[:, k * ztiles * ROW:(k + 1) * ztiles * ROW], zeros).then_inc(s_fill, 16)
            sp.wait_ge(s_fill, 16 * fills)

        @block.gpsimd
        def _(p):
            n = [0]

            def own(ins):
                n[0] += 1
                ins.then_inc(s_cst, 1)
                p.wait_ge(s_cst, n[0])

            nc.gpsimd.memset(c.eps[:, 1:2], float(np.pi / 2)).then_inc(s_const, 1)
            nc.gpsimd.memset(zeros, 0.0).then_inc(s_zero, 1)
            nc.gpsimd.memset(c.ones[:], 1.0).then_inc(s_const, 1)
            nc.gpsimd.iota(prep.tile_no[:], [[1, SLOT_TILES]], base=0, channel_multiplier=0,
                           allow_small_or_imprecise_dtypes=True).then_inc(s_const, 1)
            nc.gpsimd.iota(c.iota_f[:], [[1, P]], base=0, channel_multiplier=0,
                           allow_small_or_imprecise_dtypes=True).then_inc(s_const, 1)
            nc.gpsimd.iota(c.iota_b[:], [[1, P]], base=0, channel_multiplier=0,
                           allow_small_or_imprecise_dtypes=True).then_inc(s_const, 1)
            nc.gpsimd.iota(c.iota_slot[:], [[1, SLOT_TILES]], base=0, channel_multiplier=0,
                           allow_small_or_imprecise_dtypes=True).then_inc(s_const, 1)
            own(nc.gpsimd.memset(c.lower[:], 0.0))
            nc.gpsimd.affine_select(out=c.lower[:], in_=c.lower[:], compare_op=ALU.is_ge, fill=1.0, base=0,
                                    pattern=[[-1, P]], channel_multiplier=1).then_inc(s_const, 1)
            own(nc.gpsimd.memset(c.ident[:], 0.0))
            nc.gpsimd.affine_select(out=c.ident[:], in_=c.ident[:], compare_op=ALU.not_equal, fill=1.0, base=0,
                                    pattern=[[-1, P]], channel_multiplier=1).then_inc(s_const, 1)
            own(nc.gpsimd.memset(c.ident_b[:], 0.0))
            nc.gpsimd.affine_select(out=c.ident_b[:], in_=c.ident_b[:], compare_op=ALU.not_equal, fill=1.0,
                                    base=0, pattern=[[-1, P]], channel_multiplier=1).then_inc(s_const, 1)
            own(nc.gpsimd.memset(c.ones_last[:], 1.0))
            nc.gpsimd.affine_select(out=c.ones_last[:], in_=c.ones_last[:], compare_op=ALU.is_ge, fill=0.0,
                                    base=LAST_ROWS - 1, pattern=[[0, P]],
                                    channel_multiplier=-1).then_inc(s_const, 1)
            nc.gpsimd.memset(c.eps[:, 0:1], LN_EPS).then_inc(s_const, 1)
            nc.gpsimd.memset(c.eps[:, 2:3], BN_EPS).then_inc(s_const, 1)

        @block.scalar
        def _(act):
            act.wait_ge(s_turn, 1)
            act.wait_ge(s_const, 1)
            nc.scalar.activation(tF[2], tF[0], ACT.Sin, bias=c.eps[:, 1:2],
                                 scale=-2.0 * float(np.pi)).then_inc(s_sin, 1)

        @block.tensor
        def _(pe):
            pe.wait_ge(s_const, 12)
            ranks.tensor(pe)

        @block.vector
        def _(v):
            def own(ins):
                v.wait_ge(c.own.sem, c.own(ins))

            V = nc.vector
            v.wait_ge(s_key, 64)
            own(V.tensor_scalar(tF[0], prep.w_in, 0.1, None, ALU.mult))
            own(V.tensor_copy(tI[0], tF[0]))
            own(V.tensor_copy(tF[1], tI[0]))
            own(V.tensor_tensor(tF[0], tF[0], tF[1], ALU.subtract))
            own(V.scalar_tensor_tensor(out=tF[0], in0=tF[0], scalar=-1.0, in1=tF[0], op0=ALU.mult, op1=ALU.max))
            own(V.tensor_scalar(tF[1], tF[0], -1.0, 1.0, ALU.mult, ALU.add))
            V.tensor_tensor(tF[0], tF[0], tF[1], ALU.min).then_inc(s_turn, 1)
            own(V.tensor_scalar(tF[3], prep.w_in, 5.0, 0.5, ALU.is_lt, ALU.mult))
            v.wait_ge(s_sin, 1)
            own(V.scalar_tensor_tensor(out=prep.carry[:, :, 0], in0=tF[2], scalar=1.0, in1=tF[3], op0=ALU.add,
                                       op1=ALU.mult))
            v.wait_ge(s_const, 12)
            ranks.vector(v)
            V.tensor_scalar(tI[1], tI[0], P - 1, None, ALU.bitwise_and)
            V.tensor_scalar(tI[2], tI[0], 7, None, ALU.logical_shift_right)
            V.tensor_copy(tF[3], prep.src)
            own(V.tensor_copy(tF[0], prep.typ))
            own(V.scalar_tensor_tensor(out=tF[3], in0=tF[3], scalar=-float(2 * P * N_RELS), in1=tF[1],
                                       op0=ALU.mult, op1=ALU.subtract))
            V.tensor_copy(tF[2], tI[2])
            own(V.tensor_scalar(tF[0], tF[0], float(2 * P), float(PAD_NODE * N_RELS * 2 * P + P), ALU.mult, ALU.add))
            own(V.tensor_copy(tF[1], tI[1]))
            V.tensor_tensor(prep.carry[:, :, 1], tF[3], tF[0], ALU.add)
            V.scalar_tensor_tensor(out=prep.slot_d[:], in0=tF[1], scalar=float(SLOT_TILES), in1=tF[2],
                                   op0=ALU.mult, op1=ALU.add)


class Scatter:
    UP, HP = 14, 7
    STEPS = EDGE_COLS // 14

    def __init__(self, nc, c, prep, attr, att_rows, rows, s_row, first, last):
        self.nc, self.c, self.prep, self.attr, self.att_rows, self.rows = nc, c, prep, attr, att_rows, rows
        self.s_row, self.first, self.last = s_row, first, last
        assert EDGE_COLS % self.UP == 0
        self.base = [c.rows_base[k] - 16 * first for k in range(self.UP)]
        self.ix_base = c.ix_base - 2 * first
        for k in range(self.UP):
            c.rows_base[k] += 16 * (last - first)
        c.ix_base += 2 * (last - first)

    def half(self, it, h):
        return range(self.HP * h, self.HP * h + self.HP), at(it * self.UP + self.HP * h, self.HP)

    def landed(self, eng, it, buffers):
        for k in buffers:
            eng.wait_ge(self.c.s_rows[k], it * 16 + self.base[k])

    def loop(self, eng, half):
        for h in range(2):
            half(self.first, h, True)
        with eng.Fori(self.first + 1, self.last) as it:
            for h in range(2):
                half(it, h, False)

    def sync(self, sp):
        def load(it, h, first):
            ks, cols = self.half(it, h)
            if not first:
                self.landed(sp, it, ks)
            sp.dma_start(self.rows[:, ks[0]:ks[-1] + 1, 0:D_EDGE], self.attr[:, cols, :]).then_inc(self.s_row[h], 16)
        self.loop(sp, load)

    def gpsimd(self, p):
        c, prep = self.c, self.prep

        def scatter(it, h, first):
            ks, cols = self.half(it, h)
            if not first:
                self.landed(p, it, ks)
            self.nc.gpsimd.tensor_copy(c.ix[:, ks[0]:ks[-1] + 1], prep.slot_d[:, cols])
            self.nc.gpsimd.tensor_copy(self.rows[:, ks[0]:ks[-1] + 1, D_EDGE:ROW],
                                       prep.carry[:, cols, :]).then_inc(c.s_ix, 1)
            p.wait_ge(self.s_row[h], it * 16 + 16)
            p.wait_ge(c.s_ix, it * 2 + (h + 1 + self.ix_base))
            p.sem_inc(c.s_go, 1)
            for k in ks:
                p.indirect_dma_start(self.att_rows, bass.IndirectOffsetOnAxis(ap=c.ix[:, k:k + 1], axis=0),
                                     self.rows[:, k, :], None).then_inc(c.s_rows[k], 16)
        self.loop(p, scatter)
        self.landed(p, self.last, range(self.UP))


def edge_stage(nc, c, attr, x, weights, att_rows, table, prep, s_row, last):
    S4 = 4
    cv = Carve(c.work)
    hi1, lo1, lo = cv(S4, SLOT_TILES, dt=f16), cv(S4, 2, P, dt=f16), cv(S4, P, dt=f16)
    zero = cv(512, dt=f16)
    tmp, vI, wI = cv(SLOT_TILES), cv(SLOT_TILES, dt=i32), cv(SLOT_TILES, dt=i32)
    layer = LayerZero(nc, c, cv, table)
    tail = Carve(c.work)
    tail.n = max(cv.n, NODE_TILES * EDGE_COLS)
    scatter = Scatter(nc, c, prep, attr, att_rows, tail(Scatter.UP, ROW), s_row, 0, last)
    s_z, s_oh, s_lo, s_acc, s_load = (c.sem(f"s_place_{n}") for n in ("zero", "oh", "lo", "mm", "load"))
    acc = c.bank[4:6]
    loads = [(c.X[:, :, :], x.rearrange("(i p) d -> p i d", p=P))] + weights
    ranks = Ranks(nc, c, prep, 1, prep.src, c.nt_s, (c.bank[6], c.bank[7], c.bank[0], c.bank[1]))

    def by_vector(s, j):
        return s == S4 - 1 and j == 1

    with nc.Block() as block:
        @block.sync
        def _(sp):
            scatter.sync(sp)

        @block.gpsimd
        def _(p):
            scatter.gpsimd(p)

        @block.tensor
        def _(pe):
            ranks.tensor(pe)
            pe.wait_ge(s_z, 1)
            for k in range(2):
                nc.tensor.matmul(acc[k][:, 0:SLOT_TILES], zero[:, 0:P], zero[:, 0:SLOT_TILES], start=True,
                                 stop=False, skip_group_check=True)
            with pe.Fori(0, EDGE_COLS // S4) as it:
                for s in range(S4):
                    pe.wait_ge(s_oh, it * S4 + s + 1)
                    pe.wait_ge(s_lo, it * S4 + s + 1)
                    for k in range(2):
                        mm = nc.tensor.matmul(acc[k][:, 0:SLOT_TILES], lo1[:, s, k, :], hi1[:, s, :], start=False,
                                              stop=False, skip_group_check=True)
                    mm.then_inc(s_acc, 1)
            for k in range(2):
                mm = nc.tensor.matmul(acc[k][:, 0:SLOT_TILES], zero[:, 0:P], zero[:, 0:SLOT_TILES], start=False,
                                      stop=True, skip_group_check=True)
            mm.then_inc(s_acc, 1)
            pe.wait_ge(s_load, 16 * len(loads))
            layer.tensor(pe)

        @block.scalar
        def _(act):
            for into, a in loads:
                act.dma_start(into, a).then_inc(s_load, 16)

            def scaled(it, first):
                for s in range(S4):
                    t = it * S4 + s
                    act.wait_ge(s_oh, t + 1)
                    if not first:
                        act.wait_ge(s_acc, t - S4 + 1)
                    for j in range(2):
                        if not by_vector(s, j):
                            ins = nc.scalar.activation(lo1[:, s, j, :], lo[:, s, :], ACT.Copy,
                                                       scale=prep.part[:, j, at(t)])
                    ins.then_inc(s_lo, 1)
            scaled(0, True)
            with act.Fori(1, EDGE_COLS // S4) as it:
                scaled(it, False)
            act.wait_ge(s_load, 16 * len(loads))
            layer.scalar(act)

        @block.vector
        def _(v):
            V = nc.vector

            def own(ins):
                v.wait_ge(c.own.sem, c.own(ins))
            tF, tI = prep.tF, prep.tI
            ranks.vector(v)
            V.tensor_scalar(tI[1], tI[0], P - 1, None, ALU.bitwise_and)
            V.tensor_scalar(tI[2], tI[0], 7, None, ALU.logical_shift_right)
            own(V.tensor_copy(tF[3], prep.dst))
            V.tensor_copy(prep.pos_lo[:], tI[1])
            V.tensor_copy(prep.pos_hi[:], tI[2])
            own(V.scalar_tensor_tensor(out=tF[3], in0=tF[3], scalar=-float(2 * P), in1=tF[1], op0=ALU.mult,
                                       op1=ALU.subtract))
            own(V.tensor_scalar(tI[3], tF[3], float(PAD_NODE * 2 * P + P), None, ALU.add))
            V.tensor_scalar(tI[1], tI[3], PART - 1, None, ALU.bitwise_and)
            own(V.tensor_scalar(tI[2], tI[3], PART_BITS, None, ALU.logical_shift_right))
            V.tensor_copy(prep.part[:, 0, :], tI[1])
            own(V.tensor_copy(prep.part[:, 1, :], tI[2]))
            V.memset(zero, 0.0).then_inc(s_z, 1)

            def onehots(it, first):
                for s in range(S4):
                    t = it * S4 + s
                    if not first:
                        v.wait_ge(s_acc, t - S4 + 1)
                    V.tensor_scalar(hi1[:, s, :], c.iota_slot[:], prep.pos_hi[:, at(t)], None, ALU.is_equal)
                    for j in range(2):
                        if by_vector(s, j):
                            V.tensor_scalar(lo1[:, s, j, :], c.iota_b[:], prep.pos_lo[:, at(t)],
                                            prep.part[:, j, at(t)], ALU.is_equal, ALU.mult)
                    V.tensor_scalar(lo[:, s, :], c.iota_b[:], prep.pos_lo[:, at(t)], None,
                                    ALU.is_equal).then_inc(s_oh, 1)
            onehots(0, True)
            with v.Fori(1, EDGE_COLS // S4) as it:
                onehots(it, False)

            v.wait_ge(s_acc, EDGE_COLS + 1)
            own(V.tensor_copy(tmp, acc[0][:, 0:SLOT_TILES]))
            own(V.scalar_tensor_tensor(out=vI, in0=acc[1][:, 0:SLOT_TILES], scalar=float(PART), in1=tmp,
                                       op0=ALU.mult, op1=ALU.add))
            own(V.tensor_scalar(wI, vI, 2 * P - 1, None, ALU.bitwise_and))
            own(V.tensor_scalar(vI, vI, 8, None, ALU.logical_shift_right))
            V.tensor_scalar(c.lo_s[:], wI, -1.0, float(P), ALU.mult, ALU.add)
            own(V.tensor_scalar(c.idx_s[:], vI, -1.0, float(PAD_NODE), ALU.mult, ALU.add))
            v.wait_ge(s_load, 16 * len(loads))
            layer.vector(v)


class Norm:

    def __init__(self, nc, c):
        self.nc, self.c, self.n = nc, c, c.norms
        c.norms += 1

    def stats(self, v, of, i):
        self.nc.vector.bn_stats(self.c.st[:, at(i), :], of[:, at(i), 0:D]).then_inc(self.c.s_st, 1)

    def vector(self, v, of=None, before=None):
        nc, c = self.nc, self.c
        if of is not None:
            with v.Fori(0, NODE_TILES // NK) as it:
                for k in range(NK):
                    if before:
                        before(v, it * NK + k)
                    self.stats(v, of, it * NK + k)
        v.wait_ge(c.s_st, (NODE_TILES + 1) * self.n + NODE_TILES)

        def own(ins):
            v.wait_ge(c.own.sem, c.own(ins))
        mean, var, diff = c.mv[:, :, 0], c.mv[:, :, 1], c.rs[:]
        own(nc.vector.tensor_tensor(diff, c.st[:, :, 1], c.st[:, :, 4], ALU.subtract))
        own(nc.vector.tensor_tensor(mean, c.st[:, :, 1], c.st[:, :, 4], ALU.add))
        own(nc.vector.tensor_scalar(mean, mean, 0.5, None, ALU.mult))
        own(nc.vector.scalar_tensor_tensor(out=diff, in0=diff, scalar=D / 4.0, in1=diff, op0=ALU.mult,
                                           op1=ALU.mult))
        own(nc.vector.tensor_tensor(var, c.st[:, :, 2], c.st[:, :, 5], ALU.add))
        nc.vector.tensor_tensor(var, var, diff, ALU.add).then_inc(c.s_st, 1)
        v.wait_ge(c.s_sq, self.n + 1)
        nc.vector.reciprocal(c.rs[:], c.rs[:]).then_inc(c.s_rs, 1)
        v.wait_ge(c.s_rs, 2 * self.n + 1)
        nc.vector.scalar_tensor_tensor(out=c.nmr[:], in0=c.mv[:, :, 0], scalar=-1.0, in1=c.rs[:],
                                       op0=ALU.mult, op1=ALU.mult).then_inc(c.s_rs, 1)

    def scalar(self, act):
        act.wait_ge(self.c.s_st, (NODE_TILES + 1) * (self.n + 1))
        self.nc.scalar.activation(self.c.rs[:], self.c.mv[:, :, 1], ACT.Sqrt, bias=self.c.eps[:, 0:1],
                                  scale=1.0 / D).then_inc(self.c.s_sq, 1)

    def ready(self, eng):
        eng.wait_ge(self.c.s_rs, 2 * self.n + 2)


class GroupNorm:
    STEPS = 8

    def __init__(self, nc, c, name, of, before, s_of):
        self.nc, self.c, self.of, self.before, self.s_of = nc, c, of, before, s_of
        self.s_st, self.s_ln, self.s_sq, self.s_seen = (c.sem(f"s_{name}_{n}") for n in ("stats", "ln", "sqrt", "seen"))

    def parts(self, g):
        c, n = self.c, at(g * NK, NK)
        return c.st[:, n, :], c.mv[:, n, 0], c.mv[:, n, 1], c.rs[:, n], c.nmr[:, n]

    def stats(self, v, g, ks):
        for k in ks:
            self.before(g * NK + k)
        for k in ks:
            i = g * NK + k
            v.wait_ge(self.s_of, i + 1)
            self.nc.vector.bn_stats(self.c.st[:, at(i), :], self.of[:, at(i), 0:D]).then_inc(self.s_st, 1)

    def variance(self, v, g):
        V = self.nc.vector
        st, mean, var, diff, _ = self.parts(g)
        n = g * self.STEPS
        v.wait_ge(self.s_st, g * NK + NK)
        V.tensor_tensor(diff, st[:, :, 1], st[:, :, 4], ALU.subtract).then_inc(self.s_ln, 1)
        V.tensor_tensor(mean, st[:, :, 1], st[:, :, 4], ALU.add).then_inc(self.s_ln, 1)
        V.tensor_tensor(var, st[:, :, 2], st[:, :, 5], ALU.add).then_inc(self.s_ln, 1)
        v.wait_ge(self.s_ln, n + 1)
        V.scalar_tensor_tensor(out=diff, in0=diff, scalar=D / 4.0, in1=diff, op0=ALU.mult,
                               op1=ALU.mult).then_inc(self.s_ln, 1)
        v.wait_ge(self.s_ln, n + 2)
        V.tensor_scalar(mean, mean, 0.5, None, ALU.mult).then_inc(self.s_ln, 1)
        v.wait_ge(self.s_ln, n + 4)
        V.tensor_tensor(var, var, diff, ALU.add).then_inc(self.s_ln, 1)

    def scales(self, v, g):
        V = self.nc.vector
        _, mean, _, rs, nmr = self.parts(g)
        n = g * self.STEPS
        v.wait_ge(self.s_sq, g + 1)
        v.sem_inc(self.s_seen, 1)
        V.reciprocal(rs, rs).then_inc(self.s_ln, 1)
        v.wait_ge(self.s_ln, n + 7)
        V.scalar_tensor_tensor(out=nmr, in0=mean, scalar=-1.0, in1=rs, op0=ALU.mult,
                               op1=ALU.mult).then_inc(self.s_ln, 1)

    def first(self, v):
        self.stats(v, 0, range(NK))
        self.variance(v, 0)
        self.scales(v, 0)

    def between(self, v):
        def f(it, k):
            if isinstance(it, int) and it + 1 >= NODE_TILES // NK:
                return
            if k < 2:
                self.stats(v, it + 1, (2 * k, 2 * k + 1))
            elif k == 2:
                self.stats(v, it + 1, range(4, NK))
                self.variance(v, it + 1)
            elif k == 3:
                self.scales(v, it + 1)
        return f

    def scalar(self, act):
        def f(g):
            _, _, var, rs, _ = self.parts(g)
            act.wait_ge(self.s_ln, g * self.STEPS + 6)
            self.nc.scalar.activation(rs, var, ACT.Sqrt, bias=self.c.eps[:, 0:1], scale=1.0 / D).then_inc(self.s_sq, 1)
            act.wait_ge(self.s_ln, g * self.STEPS + 8)
        return f


class Product:

    TURNS = (0, 1, 0, 1, 7)

    def __init__(self, nc, c, name, carve, chunks):
        self.nc, self.c, self.chunks = nc, c, chunks
        self.banks = {1: [(2, 3, 2, 3, 4)], 2: [(2, 4, 2, 4, 2), (3, 5, 3, 5, 6)],
                      4: [(b,) * NK for b in (2, 3, 4, 5)]}[len(chunks)]
        self.h = carve(NK, D)
        self.hT = carve(NK, 2, P)
        self.s_h, self.s_tp, self.s_ht = (c.sem(f"s_{name}_h"), c.sem(f"s_{name}_tp"), c.sem(f"s_{name}_ht"))
        self.s_mm = [c.sem(f"s_{name}_mm{q}") for q in range(len(chunks))]
        self.s_ev = [c.sem(f"s_{name}_ev{q}") for q in range(len(chunks))]

    def loop(self, eng, body):
        last = NODE_TILES // NK - 1
        body(0, True)
        with eng.Fori(1, last) as it:
            body(it, False)
        body(last, False)

    def bank_free(self, pe, q, i, k):
        same = self.banks[q][k] == self.banks[q][(k - 1) % NK]
        wait(pe, self.s_ev[q], i if same else i - 1)

    def products(self, pe, i, k):
        for q, (w, n, _, _) in enumerate(self.chunks):
            self.bank_free(pe, q, i, k)
            for z in range(2):
                mm = self.nc.tensor.matmul(self.c.bank[self.banks[q][k]][:, 0:n], self.hT[:, k, z, :], w[:, z, :],
                                           start=(z == 0), stop=(z == 1))
            mm.then_inc(self.s_mm[q], 1)

    def turn(self, pe, i, k, ready):
        pe.wait_ge(ready, i + 1)
        wait(pe, self.s_ht, i - 1)
        for q in range(2):
            mm = self.nc.tensor.transpose(self.c.bank[self.TURNS[k]][:, q * P:(q + 1) * P],
                                          self.h[:, k, q * P:(q + 1) * P], self.c.ident[:])
        mm.then_inc(self.s_tp, 1)

    def tensor(self, pe, ready=None):
        ready = ready or self.s_h
        self.turn(pe, 0, 0, ready)

        def body(it, first):
            for k in range(NK):
                i = it * NK + k
                if not (isinstance(i, int) and i == NODE_TILES - 1):
                    self.turn(pe, i + 1, (k + 1) % NK, ready)
                pe.wait_ge(self.s_ht, i + 1)
                self.products(pe, i, k)
        self.loop(pe, body)

    def take(self, eng, name, it, i, k):
        for q, (_, n, who, f) in enumerate(self.chunks):
            if who == name:
                eng.wait_ge(self.s_mm[q], i + 1)
                f(eng, it, i, k, self.c.bank[self.banks[q][k]][:, 0:n]).then_inc(self.s_ev[q], 1)

    def ahead(self, eng, name, begin, n, between=None):
        for i in range(n):
            begin(0, i, i)

        def body(it, first):
            for k in range(NK):
                i = it * NK + k
                if not (isinstance(i, int) and i + n >= NODE_TILES):
                    begin(it + (k + n) // NK, i + n, (k + n) % NK)
                if between:
                    between(it, k)
                self.take(eng, name, it, i, k)
        self.loop(eng, body)

    def scalar(self, act, make, before=None, between=None):
        def begin(g, i, k):
            if before and k == 0:
                before(g)
            wait(act, self.s_tp, i - NK + 1)
            make(i, self.h[:, k, :]).then_inc(self.s_h, 1)
        self.ahead(act, "act", begin, 2, between)

    def vector(self, v, between=None):
        def begin(g, i, k):
            v.wait_ge(self.s_tp, i + 1)
            self.nc.vector.tensor_copy(self.hT[:, k, :, :].rearrange("p a b -> p (a b)"),
                                       self.c.bank[self.TURNS[k]][:, 0:2 * P]).then_inc(self.s_ht, 1)
        self.ahead(v, "dve", begin, 1, between)


def flat(ap):
    return ap.rearrange("p a b -> p (a b)")


def normed(nc, c, of, func):
    return lambda i, out: nc.scalar.activation(out, flat(of[:, at(i), 0:D]), func, bias=c.nmr[:, at(i)],
                                               scale=c.rs[:, at(i)])


class Store:

    def __init__(self, c, rows, table, signals):
        self.rows, self.table, self.signals = rows, table, signals
        self.s, self.base = c.s_store, c.store_base
        c.store_base += 16 * (NODE_TILES // NK)

    def free(self, eng, it, k):
        wait(eng, self.s[k], it * 16 + self.base)

    def sync(self, sp):
        with sp.Fori(0, NODE_TILES // NK) as it:
            for k in range(NK):
                self.put(sp, it * NK + k, k)
        self.landed(sp)

    def put(self, eng, i, k):
        for s in self.signals:
            eng.wait_ge(s, i + 1)
        eng.dma_start(self.table[at(i * P, P), :], self.rows(k)).then_inc(self.s[k], 16)

    def landed(self, eng):
        for k in range(NK):
            eng.wait_ge(self.s[k], self.base + 16 * (NODE_TILES // NK))


class LayerZero:

    def __init__(self, nc, c, cv, table):
        self.nc, self.c = nc, c
        self.out, self.b12 = cv(NK, D), cv(D)
        self.s_b, self.s_x = c.sem("s_n0_b"), c.sem("s_n0_x")
        self.norm = Norm(nc, c)
        self.prod = Product(nc, c, "n0", cv, [(c.w12[:, :, 0:D], D, "dve", self.keep_x),
                                              (c.w12[:, :, D:2 * D], D, "act", self.keep_table)])
        self.store = Store(c, lambda k: self.out[:, k, :], table, [self.prod.s_ev[1]])

    def keep_x(self, v, it, i, k, ps):
        V, x = self.nc.vector, self.c.X[:, at(i), :]
        V.tensor_tensor(x, ps.unsqueeze(1), x, ALU.add).then_inc(self.s_x, 1)
        v.wait_ge(self.s_x, i + 1)
        return V.tensor_tensor(x, x, self.b12.unsqueeze(1), ALU.add)

    def keep_table(self, act, it, i, k, ps):
        if not (isinstance(i, int) and i == 0):
            self.store.put(act, i - 1, (k - 1) % NK)
        self.store.free(act, it, k)
        return self.nc.scalar.copy(self.out[:, k, :], ps)

    def vector(self, v):
        self.nc.vector.tensor_tensor(self.b12, self.c.b("b1"), self.c.b("b2"), ALU.add).then_inc(self.s_b, 1)
        self.norm.vector(v, self.c.X)
        v.wait_ge(self.s_b, 1)
        self.prod.vector(v)

    def scalar(self, act):
        self.norm.scalar(act)
        self.norm.ready(act)
        self.prod.scalar(act, normed(self.nc, self.c, self.c.X, ACT.Relu))
        self.store.put(act, NODE_TILES - 1, (NODE_TILES - 1) % NK)
        self.store.landed(act)

    def tensor(self, pe):
        self.prod.tensor(pe)


def node_stage_1(nc, c, table, prep, attr, att_rows, s_row, first):
    cv = Carve(c.work)
    out = cv(NK, N_RELS * D)
    q = flat(c.Q[:, :, :])
    q_cv = Carve(q)
    vI, wI = q_cv(SLOT_TILES, dt=i32), q_cv(SLOT_TILES, dt=i32)
    relation, payload = q_cv(SLOT_TILES), q_cv(SLOT_TILES)
    scatter = Scatter(nc, c, prep, attr, att_rows, q_cv(Scatter.UP, ROW), s_row, first, Scatter.STEPS)
    slot_rows = att_rows.rearrange("(p t) c -> p t c", p=P)
    PB = 4
    att = q_cv(PB, U, ROW)
    assert q_cv.n <= NODE_TILES * D
    s_at, s_pay = [c.sem(f"s_pay_rows{k}") for k in range(PB)], c.sem("s_pay")
    cinv = c.sb("cinv", [P, NODE_TILES], f32)
    s_c = c.sem("s_n1_c")
    s_x = c.sem("s_n1_x")

    def add_mean(i):
        nc.vector.scalar_tensor_tensor(out=c.X[:, at(i), :], in0=c.AGG[:, at(i), 0:D], scalar=cinv[:, at(i)],
                                       in1=c.X[:, at(i), :], op0=ALU.mult, op1=ALU.add).then_inc(s_x, 1)

    norm = GroupNorm(nc, c, "n1", c.X, add_mean, s_x)

    def keep(q):
        def f(eng, it, i, k, ps):
            if q == 0 and not (isinstance(i, int) and i == 0):
                store.put(eng, i - 1, (k - 1) % NK)
            store.free(eng, it, k)
            o = out[:, k, q * 2 * D:(q + 1) * 2 * D]
            return nc.scalar.copy(o, ps) if q % 2 == 0 else nc.vector.tensor_copy(o, ps)
        return f

    prod = Product(nc, c, "n1", cv, [(c.wrel[:, :, q * 2 * D:(q + 1) * 2 * D], 2 * D, ("act", "dve")[q % 2], keep(q))
                                     for q in range(N_RELS // 2)])
    store = Store(c, lambda k: out[:, k, :], table, prod.s_ev)

    with nc.Block() as block:
        @block.vector
        def _(v):
            nc.vector.tensor_scalar(cinv[:], c.AGG[:, :, D], 1.0, None, ALU.max).then_inc(s_c, 1)
            v.wait_ge(s_c, 1)
            nc.vector.reciprocal(cinv[:], cinv[:]).then_inc(s_c, 1)
            v.wait_ge(s_c, 2)
            norm.first(v)
            prod.vector(v, norm.between(v))

            def own(ins):
                v.wait_ge(c.own.sem, c.own(ins))
            V = nc.vector
            v.wait_ge(s_pay, SLOT_TILES // U)
            own(V.tensor_copy(vI, payload))
            own(V.tensor_scalar(wI, vI, 2 * P - 1, None, ALU.bitwise_and))
            V.tensor_scalar(c.lo_d[:], wI, -1.0, float(P), ALU.mult, ALU.add)
            own(V.tensor_scalar(vI, vI, 8, None, ALU.logical_shift_right))
            own(V.tensor_scalar(wI, vI, N_RELS - 1, None, ALU.bitwise_and))
            V.tensor_copy(relation, wI)
            own(V.tensor_scalar(vI, vI, 3, None, ALU.logical_shift_right))
            own(V.tensor_scalar(c.idx_d2[:], vI, -1.0, float(PAD_NODE), ALU.mult, ALU.add))
            V.scalar_tensor_tensor(out=c.idx_d1[:], in0=c.idx_d2[:], scalar=float(N_RELS), in1=relation,
                                   op0=ALU.mult, op1=ALU.add)

        @block.scalar
        def _(act):
            prod.scalar(act, normed(nc, c, c.X, ACT.Relu), norm.scalar(act))
            store.put(act, NODE_TILES - 1, (NODE_TILES - 1) % NK)
            store.landed(act)

        @block.tensor
        def _(pe):
            prod.tensor(pe)

        @block.sync
        def _(sp):
            scatter.sync(sp)
            scatter.landed(sp, scatter.last, range(Scatter.UP))

            def load(it, k, first):
                if not first:
                    sp.wait_ge(s_pay, it * PB + (k - PB + 1))
                sp.dma_start(att[:, k, :, :], slot_rows[:, at(it * (PB * U) + k * U, U), :]).then_inc(s_at[k], 16)
            for k in range(PB):
                load(0, k, True)
            with sp.Fori(1, SLOT_TILES // (PB * U)) as it:
                for k in range(PB):
                    load(it, k, False)

        @block.gpsimd
        def _(p):
            scatter.gpsimd(p)
            with p.Fori(0, SLOT_TILES // (PB * U)) as it:
                for k in range(PB):
                    p.wait_ge(s_at[k], it * 16 + 16)
                    p.sem_inc(c.s_go, 1)
                    nc.gpsimd.tensor_copy(payload[:, at(it * (PB * U) + k * U, U)],
                                          att[:, k, :, ROW - 1]).then_inc(s_pay, 1)


def batch_norm_stage(nc, c):
    cv = Carve(c.work)
    sq = cv(NODE_TILES, D)
    neg_mean, scale = cv(D), cv(D)
    s_sum, s_nm, s_cen, s_sq, s_std, s_x = (c.sem(f"s_bn_{n}") for n in ("sum", "nm", "cen", "sq", "std", "x"))
    chunks = [(g * NK, (g + 1) * NK) for g in range(NODE_TILES // NK)]

    with nc.Block() as block:
        @block.tensor
        def _(pe):
            def column_sums(bank, of, ready=None):
                for g, (i0, i1) in enumerate(chunks):
                    if ready:
                        pe.wait_ge(ready, g + 1)
                    for i in range(i0, i1):
                        ones = c.ones if i < NODE_TILES - 1 else c.ones_last
                        mm = nc.tensor.matmul(bank[:, 0:D], ones[:], of[:, i, 0:D], start=(i == 0),
                                              stop=(i == NODE_TILES - 1))
                mm.then_inc(s_sum, 1)
            column_sums(c.bank[0], c.AGG)
            column_sums(c.bank[1], sq, s_sq)

        @block.scalar
        def _(act):
            act.wait_ge(s_sum, 1)
            nc.scalar.mul(neg_mean, c.bank[0][:, 0:D], -1.0 / N_NODES).then_inc(s_nm, 1)
            for g, (i0, i1) in enumerate(chunks):
                act.wait_ge(s_cen, g + 1)
                nc.scalar.activation(sq[:, i0:i1, :], c.AGG[:, i0:i1, 0:D], ACT.Square).then_inc(s_sq, 1)
            act.wait_ge(s_sum, 2)
            nc.scalar.activation(scale, c.bank[1][:, 0:D], ACT.Sqrt, bias=c.eps[:, 2:3],
                                 scale=1.0 / N_NODES).then_inc(s_std, 1)

        @block.gpsimd
        def _(p):
            nc.gpsimd.tensor_tensor(c.X[:, :, :], c.X[:, :, :],
                                    c.b("beta").unsqueeze(1).broadcast_to([P, NODE_TILES, D]),
                                    ALU.add).then_inc(s_x, 1)

        @block.vector
        def _(v):
            def own(ins):
                v.wait_ge(c.own.sem, c.own(ins))

            def rows(ap):
                return ap.unsqueeze(1).broadcast_to([P, NK, D])
            v.wait_ge(s_nm, 1)
            for i0, i1 in chunks:
                a = c.AGG[:, i0:i1, 0:D]
                nc.vector.tensor_tensor(a, a, rows(neg_mean), ALU.add).then_inc(s_cen, 1)
            v.wait_ge(s_std, 1)
            own(nc.vector.reciprocal(scale, scale))
            own(nc.vector.tensor_tensor(scale, scale, c.b("gamma"), ALU.mult))
            v.wait_ge(s_x, 1)
            scaled = []
            for i0, i1 in chunks:
                a = c.AGG[:, i0:i1, 0:D]
                scaled.append(c.own(nc.vector.tensor_tensor(a, a, rows(scale), ALU.mult)))
            for (i0, i1), done in zip(chunks, scaled):
                v.wait_ge(c.own.sem, done)
                x = c.X[:, i0:i1, :]
                nc.vector.tensor_tensor(x, x, c.AGG[:, i0:i1, 0:D], ALU.add)


def node_stage_2(nc, c, table):
    cv = Carve(c.work)
    out = cv(NK, 2 * D)
    H = c.AGG
    s_h, s_g, s_hn, s_x = c.sem("s_n2_rows"), c.sem("s_n2_g"), c.sem("s_n2_rows_ready"), c.sem("s_n2_x")
    q = cv(NK, D)
    s_q1, s_r, s_q2, s_q3 = (c.sem(f"s_n2_{n}") for n in ("q1", "rest", "q2", "q3"))
    norm, norm2 = Norm(nc, c), Norm(nc, c)

    def keep_q(v, it, i, k, ps):
        wait(v, s_q3, i - NK + 1)
        return nc.vector.tensor_tensor(q[:, k, :], ps, c.b("bqkv")[:, 0:D], ALU.add)

    def lagged(it, k, lag):
        i = it * NK + k - lag
        return i, (k - lag) % NK, not isinstance(i, int) or 0 <= i < NODE_TILES

    def row(k):
        return q[:, k, :].unsqueeze(1)

    def parts_scalar(act):
        def f(it, k):
            i, b, lives = lagged(it, k, 1)
            if lives:
                act.wait_ge(prod.s_ev[0], i + 1)
                nc.scalar.copy(c.q_parts[0](i), row(b)).then_inc(s_q1, 1)
            i, b, lives = lagged(it, k, 3)
            if lives:
                act.wait_ge(s_r, i + 1)
                nc.scalar.copy(c.q_parts[1](i), row(b)).then_inc(s_q2, 1)
        return f

    def parts_vector(v):
        def f(it, k):
            i, b, lives = lagged(it, k, 2)
            if lives:
                v.wait_ge(s_q1, i + 1)
                nc.vector.tensor_tensor(row(b), row(b), c.q_parts[0](i), ALU.subtract).then_inc(s_r, 1)
            i, b, lives = lagged(it, k, 4)
            if lives:
                v.wait_ge(s_q2, i + 1)
                nc.vector.tensor_tensor(c.q_parts[2](i), row(b), c.q_parts[1](i), ALU.subtract).then_inc(s_q3, 1)
        return f

    def keep_kv(v, it, i, k, ps):
        store.free(v, it, k)
        return nc.vector.tensor_tensor(out[:, k, :], ps, c.b("bqkv")[:, D:3 * D], ALU.add)

    prod = Product(nc, c, "n2", cv, [(c.wqkv[:, :, 0:D], D, "dve", keep_q),
                                     (c.wqkv[:, :, D:3 * D], 2 * D, "dve", keep_kv)])
    store = Store(c, lambda k: out[:, k, :], table, [prod.s_ev[1]])

    with nc.Block() as block:
        @block.vector
        def _(v):
            norm.vector(v, c.X)
            norm2.vector(v, H, lambda v, i: v.wait_ge(s_h, i + 1))
            parts = parts_vector(v)
            prod.vector(v, parts)
            for k in range(4):
                parts(NODE_TILES // NK, k)

        @block.gpsimd
        def _(p):
            def rows_and_x(it, k):
                i, rows, x = it * NK + k, prod.h[:, k, :], c.X[:, at(it * NK + k), :]
                p.wait_ge(prod.s_h, i + 1)
                nc.gpsimd.tensor_tensor(rows, rows, c.b("ln_g"), ALU.mult).then_inc(s_g, 1)
                nc.gpsimd.tensor_tensor(x, x, H[:, at(i), 0:D], ALU.add).then_inc(s_x, 1)
                p.wait_ge(s_g, i + 1)
                nc.gpsimd.tensor_tensor(rows, rows, c.b("ln_b"), ALU.add).then_inc(s_hn, 1)
                p.wait_ge(s_x, i + 1)
                p.sem_inc(c.s_go, 1)
                nc.gpsimd.tensor_tensor(x, x, c.b("bo").unsqueeze(1), ALU.add)
            with p.Fori(0, NODE_TILES // NK) as it:
                for k in range(NK):
                    rows_and_x(it, k)

        @block.scalar
        def _(act):
            norm.scalar(act)
            norm.ready(act)
            make = normed(nc, c, c.X, ACT.Relu)
            with act.Fori(0, NODE_TILES) as i:
                make(i, flat(H[:, at(i), 0:D])).then_inc(s_h, 1)
            norm2.scalar(act)
            norm2.ready(act)
            parts = parts_scalar(act)
            prod.scalar(act, normed(nc, c, H, ACT.Identity), between=parts)
            for k in range(3):
                parts(NODE_TILES // NK, k)

        @block.tensor
        def _(pe):
            prod.tensor(pe, s_hn)

        @block.sync
        def _(sp):
            store.sync(sp)


class HeadProduct(Product):

    def second(self, pe, i, k):
        wlr, n, _, _ = self.chunks[1]
        pe.wait_ge(self.s_ev[0], i + 1)
        self.bank_free(pe, 1, i, k)
        self.nc.tensor.matmul(self.c.bank[self.banks[1][k]][:, 0:n], self.xT[0:D_HEAD, k, :], wlr, start=True,
                              stop=True).then_inc(self.s_mm[1], 1)

    def products(self, pe, i, k):
        w = self.chunks[0][0]
        self.bank_free(pe, 0, i, k)
        for z in range(2):
            mm = self.nc.tensor.matmul(self.c.bank[self.banks[0][k]][0:D_HEAD, 0:P], w[:, z, :], self.hT[:, k, z, :],
                                       start=(z == 0), stop=(z == 1))
        mm.then_inc(self.s_mm[0], 1)
        if not (isinstance(i, int) and i == 0):
            self.second(pe, i - 1, (k - 1) % NK)

    def tensor(self, pe):
        super().tensor(pe)
        self.second(pe, NODE_TILES - 1, NK - 1)

    def take_one(self, eng, q, it, i, k):
        _, n, _, f = self.chunks[q]
        eng.wait_ge(self.s_mm[q], i + 1)
        f(eng, it, i, k, self.c.bank[self.banks[q][k]][:, 0:n]).then_inc(self.s_ev[q], 1)

    def take(self, eng, name, it, i, k):
        if name == "act":
            self.take_one(eng, 0, it, i, k)
            if not (isinstance(i, int) and i == 0):
                self.take_one(eng, 1, it if k else it - 1, i - 1, (k - 1) % NK)

    def scalar(self, act, make):
        super().scalar(act, make)
        self.take_one(act, 1, NODE_TILES // NK - 1, NODE_TILES - 1, NK - 1)


def node_stage_3(nc, c, table):
    cv = Carve(c.work)
    xT = cv(NK, P)
    out = cv(NK, D_HEAD + 2 * HEADS)
    s_el = c.sem("s_n3_el")
    norm = Norm(nc, c)

    def add_x(v, it, i, k, ps):
        return nc.vector.tensor_tensor(c.X[:, at(i), :], ps.unsqueeze(1), c.X[:, at(i), :], ALU.add)

    def keep_xT(act, it, i, k, ps):
        return nc.scalar.copy(xT[0:D_HEAD, k, :], ps[0:D_HEAD, :])

    def keep_rows(act, it, i, k, ps):
        store.free(act, it, k)
        return nc.scalar.copy(out[:, k, :], ps)

    back = Product(nc, c, "n3o", cv, [(c.wo, D, "dve", add_x)])
    prod = HeadProduct(nc, c, "n3", cv, [(c.w3, P, "act", keep_xT),
                                         (c.wlr[:, :], D_HEAD + 2 * HEADS, "act", keep_rows)])
    prod.xT = xT
    store = Store(c, lambda k: out[:, k, 0:D_T3], table, [prod.s_ev[1], s_el])

    with nc.Block() as block:
        @block.vector
        def _(v):
            def stats_before(it, k):
                i = it * NK + k
                if not (isinstance(i, int) and i == 0):
                    v.wait_ge(back.s_ev[0], i)
                    norm.stats(v, c.X, i - 1)
            back.vector(v, stats_before)
            v.wait_ge(back.s_ev[0], NODE_TILES)
            norm.stats(v, c.X, NODE_TILES - 1)
            norm.vector(v)
            prod.vector(v)

        @block.scalar
        def _(act):
            back.scalar(act, lambda i, o: nc.scalar.copy(o, flat(c.AGG[:, at(i), 0:D])))
            norm.scalar(act)
            norm.ready(act)
            prod.scalar(act, normed(nc, c, c.X, ACT.Relu))

        @block.tensor
        def _(pe):
            back.tensor(pe)
            prod.tensor(pe)

        @block.gpsimd
        def _(p):
            with p.Fori(0, NODE_TILES // NK) as it:
                for k in range(NK):
                    i = it * NK + k
                    p.wait_ge(prod.s_ev[1], i + 1)
                    nc.gpsimd.tensor_copy(c.EL[:, at(i), :], out[:, k, D_T3:D_T3 + HEADS].unsqueeze(1)).then_inc(s_el, 1)

        @block.sync
        def _(sp):
            store.sync(sp)


def output_stage(nc, c, out):
    cv = Carve(c.work)
    CH = NK
    low = cv(2, CH * D)
    rinv = c.sb("rinv", [P, NODE_TILES, HEADS], f32)
    s_low, s_exp, s_y, s_o = c.sem("s_out_low"), c.sem("s_out_exp"), c.sem("s_out_y"), c.sem("s_out_dma")
    s_m, s_b = c.sem("s_out_mean"), c.sem("s_out_bias")
    n_ch = NODE_TILES // CH

    def heads(g):
        return c.AGG[:, g * CH:(g + 1) * CH, 0:D].rearrange("p i (h d) -> p i h d", h=HEADS)

    with nc.Block() as block:
        @block.vector
        def _(v):
            def own(ins):
                v.wait_ge(c.own.sem, c.own(ins))
            V = nc.vector
            own(V.tensor_scalar(rinv[:, :, :], c.AGG[:, :, D:D + HEADS], SUM_EPS, None, ALU.max))
            own(V.reciprocal(rinv[:, :, :], rinv[:, :, :]))

            def begin(g):
                i0, i1 = g * CH, (g + 1) * CH
                yh = heads(g)
                V.tensor_tensor(yh, yh, rinv[:, i0:i1, :].unsqueeze(3).broadcast_to([P, CH, HEADS, D_HEAD]),
                                ALU.mult).then_inc(s_m, 1)

            def middle(g):
                v.wait_ge(s_b, g + 1)
                if g >= 2:
                    v.wait_ge(s_y, g - 1)
                V.tensor_scalar(low[:, g % 2, :].rearrange("p (a b) -> p a b", a=CH),
                                c.AGG[:, g * CH:(g + 1) * CH, 0:D], 0.0, None, ALU.min).then_inc(s_low, 1)

            def end(g):
                y = c.AGG[:, g * CH:(g + 1) * CH, 0:D]
                x = c.X[:, g * CH:(g + 1) * CH, :]
                e = low[:, g % 2, :].rearrange("p (a b) -> p a b", a=CH)
                v.wait_ge(s_exp, g + 1)
                own(V.scalar_tensor_tensor(out=y, in0=y, scalar=0.0, in1=e, op0=ALU.max, op1=ALU.add))
                V.scalar_tensor_tensor(out=x, in0=y, scalar=-1.0, in1=x, op0=ALU.add, op1=ALU.add).then_inc(s_y, 1)
            begin(0)
            begin(1)
            middle(0)
            for g in range(n_ch):
                if g + 2 < n_ch:
                    begin(g + 2)
                if g + 1 < n_ch:
                    middle(g + 1)
                end(g)

        @block.gpsimd
        def _(p):
            for g in range(n_ch):
                p.wait_ge(s_m, g + 1)
                nc.gpsimd.tensor_tensor(heads(g), heads(g), c.b("b3").unsqueeze(1).unsqueeze(1).broadcast_to(
                    [P, CH, HEADS, D_HEAD]), ALU.add).then_inc(s_b, 1)

        @block.scalar
        def _(act):
            for g in range(n_ch):
                act.wait_ge(s_low, g + 1)
                nc.scalar.activation(low[:, g % 2, :], low[:, g % 2, :], ACT.Exp).then_inc(s_exp, 1)

        @block.sync
        def _(sp):
            for g in range(n_ch):
                sp.wait_ge(s_y, g + 1)
                full = CH if g < n_ch - 1 else CH - 1
                r0 = g * CH * P
                sp.dma_start(out[r0:r0 + full * P, :].rearrange("(i p) d -> p i d", p=P),
                             c.X[:, g * CH:g * CH + full, :]).then_inc(s_o, 16)
            sp.dma_start(out[(NODE_TILES - 1) * P:N_NODES, :], c.X[0:LAST_ROWS, NODE_TILES - 1, :]).then_inc(s_o, 16)
            sp.wait_ge(s_o, 16 * (n_ch + 1))


class Gather:

    def __init__(self, nc, c, idx, table, rows, n=U):
        self.nc, self.c, self.idx, self.table, self.rows, self.n = nc, c, idx, table, rows, n
        self.s, self.s_ix, self.s_go = c.s_rows, c.s_ix, c.s_go
        self.base, self.ix_base = list(c.rows_base), c.ix_base
        for k in range(n):
            c.rows_base[k] += 16 * (SLOT_TILES // n)
        c.ix_base += SLOT_TILES // G

    def issue(self, p, k):
        p.indirect_dma_start(self.rows(k), None, self.table,
                             bass.IndirectOffsetOnAxis(ap=self.c.ix[:, k:k + 1], axis=0)).then_inc(self.s[k], 16)

    def copy_indices(self, act, it, h):
        for k in range(G * h, G * h + G):
            wait(act, self.s[k], it * 16 + self.base[k])
        self.nc.scalar.copy(self.c.ix[:, G * h:G * h + G], self.idx[:, at(it * self.n + G * h, G)]).then_inc(self.s_ix, 1)

    def gpsimd(self, p, s_used):
        n = self.n

        def body(it, first):
            for k in range(n):
                if k % G == 0:
                    p.wait_ge(self.s_ix, it * (n // G) + (self.ix_base + k // G + 1))
                if not first:
                    p.wait_ge(s_used, (it - 1) * n + k + 1)
                p.sem_inc(self.s_go, 1)
                self.issue(p, k)
        body(0, True)
        with p.Fori(1, SLOT_TILES // n) as it:
            body(it, False)

    def landed(self, eng, it, k):
        eng.wait_ge(self.s[k], it * 16 + (16 + self.base[k]))


def edge_loop(eng, body, n=U):
    last = SLOT_TILES // n - 1
    body(0, True, False)
    with eng.Fori(1, last) as it:
        body(it, False, False)
    body(last, False, True)


class Group:

    def __init__(self, it, q, ahead=0):
        q = q + ahead
        self.it, self.q = it + q // Q4, q % Q4
        self.g = self.it * Q4 + self.q
        self.lives = not isinstance(it, int) or 0 <= self.g < SLOT_TILES // G
        self.slots = range(G * self.q, G * self.q + G)

    def at8(self, j):
        return self.it * (UH // U) + self.q // (U // G), G * self.q % U + j

    def tile(self, j):
        return self.it * UH + G * self.q + j


def sum_stage(nc, c, name, idx, lo, nt, table, counted):
    W = D + 1 if counted else D
    cv = Carve(c.work)
    rows, onehot = cv(U, W), cv(U, P)
    s_0, s_oh, s_mm, s_add = c.sem(f"s_{name}_zero"), c.sem(f"s_{name}_oh"), c.sem(f"s_{name}_mm"), c.sem(f"s_{name}_add")
    gather = Gather(nc, c, idx, table, lambda k: rows[:, k, 0:D])

    with nc.Block() as block:
        @block.gpsimd
        def _(p):
            gather.gpsimd(p, s_mm)

        @block.scalar
        def _(act):
            gather.copy_indices(act, 0, 0)
            gather.copy_indices(act, 0, 1)
            with act.Fori(1, SLOT_TILES // U) as it:
                for h in range(2):
                    gather.copy_indices(act, it, h)

        @block.tensor
        def _(pe):
            pe.wait_ge(s_0, 2)

            def body(it, first, last):
                for k in range(U):
                    t = it * U + k
                    gather.landed(pe, it, k)
                    pe.wait_ge(s_oh, t + 1)
                    wait(pe, s_add, t - G + 1)
                    nc.tensor.matmul(c.bank[k % G][:, 0:W], onehot[:, k, :], rows[:, k, :], start=True,
                                     stop=True).then_inc(s_mm, 1)
            edge_loop(pe, body)

        @block.vector
        def _(v):
            V = nc.vector
            if counted:
                V.memset(rows[:, :, D:W], 1.0).then_inc(s_0, 1)
            else:
                v.sem_inc(s_0, 1)
            V.memset(c.AGG[:, :, :], 0.0).then_inc(s_0, 1)
            regs = [v.alloc_register(f"{name}_nt{k}") for k in range(U)]

            def build(t, k):
                V.tensor_scalar(onehot[:, k, :], c.iota_f[:], lo[:, at(t)], None, ALU.is_equal).then_inc(s_oh, 1)
            for t in range(G):
                build(t, t)
            v.wait_ge(s_0, 2)

            def body(it, first, last):
                v.load(regs, nt[0:1, at(it * U, U)])
                for k in range(U):
                    t = it * U + k
                    node_tile = v.snap(regs[k], min_val=0, max_val=NODE_TILES - 1)
                    v.wait_ge(s_mm, t + 1)
                    if not (last and k + G >= U):
                        build(t + G, (k + G) % U)
                    wait(v, s_add, t)
                    sums = c.AGG[:, at(node_tile), 0:W]
                    V.tensor_tensor(sums, c.bank[k % G][:, 0:W].unsqueeze(1), sums, ALU.add).then_inc(s_add, 1)
            edge_loop(v, body)


def attention_stage(nc, c, table, att_rows):
    cv = Carve(c.work)
    kv = c.wrel[:, :, :].rearrange("p a (b c) -> p (a b) c", c=2 * D)
    assert 2 * N_RELS * D == U * 2 * D
    dkv = cv(G, 2 * D)
    prod, scratch = cv(2, D), cv(D)
    msg = cv(U, D)
    att = cv(UH, ROW)
    attT, nodeT = cv(2, G, P), cv(2, G, P, dt=bf16)
    onehot = cv(UH, P, dt=bf16)
    weighted = cv(G, P)
    dot, act_dot, weight = cv(UH), cv(UH), cv(UH)
    assert cv.n <= Q3_AT
    s_att = [c.sem(f"s_l2_att{q}") for q in range(Q4)]
    (s_0, s_oh, s_tr, s_cp, s_dk, s_q, s_si, s_t1, s_dot, s_msg, s_msg_v, s_sd, s_w, s_wo, s_mm, s_add) = (
        c.sem(f"s_l2_{n}") for n in ("zero", "oh", "tr", "cp", "dk", "q", "si", "t1", "dot", "msg", "msg_v", "sd", "w",
                                     "wo", "mm", "add"))
    gather = Gather(nc, c, c.idx_d2, table, lambda k: kv[:, k, :])
    b_oT = c.bank[0][:, 0:G * P // 2].bitcast(bf16).rearrange("p (a b) -> p a b", a=G)
    b_aT, b_d, b_q, b_m = c.bank[1], (c.bank[2], c.bank[3]), (c.bank[4], c.bank[5]), (c.bank[6], c.bank[7])

    def loop_steps(eng, step):
        def body(it, first, last):
            for q in range(Q4):
                step(it, q)
        edge_loop(eng, body, UH)

    def steps(eng, step):
        step(0, -1)
        loop_steps(eng, step)

    def message_made(eng, g, j):
        if j == G - 1:
            wait(eng, s_msg_v, g + 1)
        else:
            wait(eng, s_msg, g * (G - 1) + (j + 1))

    with nc.Block() as block:
        @block.gpsimd
        def _(p):
            def message(it8, k, gathers):
                t, g, j = it8 * U + k, it8 * (U // G) + k // G, k % G
                if j < G - 1:
                    gather.landed(p, it8, k)
                    p.wait_ge(s_si, t + 1)
                    wait(p, s_mm, t - U + 1)
                    nc.gpsimd.tensor_tensor(msg[:, k, :], kv[:, k, D:2 * D], dkv[:, j, D:2 * D],
                                            ALU.mult).then_inc(s_msg, 1)
                if gathers:
                    if k % G == 0:
                        p.wait_ge(gather.s_ix, it8 * (U // G) + (gather.ix_base + U // G + k // G + 1))
                    p.wait_ge(s_t1, t + 1)
                    message_made(p, g, j)
                    p.sem_inc(gather.s_go, 1)
                    gather.issue(p, k)

            for k in range(U):
                if k % G == 0:
                    p.wait_ge(gather.s_ix, gather.ix_base + k // G + 1)
                gather.issue(p, k)
            last = SLOT_TILES // U - 1
            for k in range(U):
                message(0, k, True)
            with p.Fori(1, last) as it:
                for k in range(U):
                    message(it, k, True)
            for k in range(U):
                message(last, k, False)

        @block.sync
        def _(sp):
            def load(it, q):
                g = it * Q4 + q
                wait(sp, s_w, g - Q4 + 1)
                sp.dma_start(att[:, G * q:G * q + G, :],
                             att_rows[:, at(g * G, G), :]).then_inc(s_att[q], 16)
            for q in range(Q4):
                load(0, q)
            with sp.Fori(1, SLOT_TILES // UH) as it:
                for q in range(Q4):
                    load(it, q)

        @block.tensor
        def _(pe):
            pe.wait_ge(s_0, 1)
            regs = [pe.alloc_register(f"l2_pe_nt{k}") for k in range(UH)]

            def turn(a):
                if not a.lives:
                    return
                pe.wait_ge(s_oh, a.tile(0) + G)
                pe.wait_ge(s_att[a.q], a.it * 16 + 16)
                wait(pe, s_cp, a.g)
                for j, k in enumerate(a.slots):
                    nc.tensor.transpose(b_oT[:, j, :], onehot[:, k, :], c.ident_b[:])
                for j, k in enumerate(a.slots):
                    mm = nc.tensor.transpose(b_aT[0:D_EDGE, j * P:(j + 1) * P], att[:, k, 0:D_EDGE], c.ident[:])
                mm.then_inc(s_tr, 1)

            def dots(a, j):
                if not a.lives:
                    return
                t = a.tile(j)
                if j == 0:
                    pe.wait_ge(s_cp, a.g + 1)
                    if a.q == 0:
                        pe.load(regs, c.nt_d[0:1, at(a.it * UH, UH)])
                wait(pe, s_si, t - 1)
                nc.tensor.matmul(b_d[j % 2][:, :], attT[0:D_EDGE + 1, a.q % 2, j, :], c.wd[:, :], start=True,
                                 stop=True).then_inc(s_dk, 1)
                wait(pe, s_t1, t - 1)
                node_tile = pe.snap(regs[a.slots[j]], min_val=0, max_val=NODE_TILES - 1)
                for z, part in enumerate(c.q_parts):
                    mm = nc.tensor.matmul(b_q[j % 2][:, 0:D], nodeT[:, a.q % 2, j, :], part(node_tile),
                                          start=(z == 0), stop=(z == 2))
                mm.then_inc(s_q, 1)

            def sums(a, j):
                if not a.lives:
                    return
                t = a.tile(j)
                pe.wait_ge(s_wo, t + 1)
                message_made(pe, a.g, j)
                wait(pe, s_add, t)
                nc.tensor.matmul(b_m[j % 2][:, 0:D], weighted[:, j, :], msg[:, a.slots[j] % U, :], start=True,
                                 stop=True).then_inc(s_mm, 1)

            turn(Group(0, 0))

            def step(it, q):
                dots(Group(it, q, 1), 0)
                sums(Group(it, q, -1), 2)
                dots(Group(it, q, 1), 1)
                sums(Group(it, q, -1), 3)
                turn(Group(it, q, 2))
                dots(Group(it, q, 1), 2)
                sums(Group(it, q), 0)
                dots(Group(it, q, 1), 3)
                sums(Group(it, q), 1)
            steps(pe, step)
            for j in (2, 3):
                sums(Group(SLOT_TILES // UH - 1, Q4 - 1), j)

        @block.scalar
        def _(act):
            gather.copy_indices(act, 0, 0)
            gather.copy_indices(act, 0, 1)

            def copy(a):
                if not a.lives:
                    return
                act.wait_ge(s_tr, a.g + 1)
                wait(act, s_q, (a.g - 1) * G)
                nc.scalar.copy(flat(nodeT[:, a.q % 2, :, :]), flat(b_oT))
                nc.scalar.copy(flat(attT[0:D_EDGE, a.q % 2, :, :]), b_aT[0:D_EDGE, :]).then_inc(s_cp, 1)

            def silu(a, j):
                if not a.lives:
                    return
                t = a.tile(j)
                act.wait_ge(s_dk, t + 1)
                wait(act, s_dot, t - G + 1)
                message_made(act, a.g - 1, j)
                nc.scalar.activation(dkv[:, j, :], b_d[j % 2][:, :], ACT.Silu).then_inc(s_si, 1)

            def silu_dot(a):
                if not a.lives:
                    return
                act.wait_ge(s_dot, a.tile(0) + G)
                wait(act, s_w, a.g - Q4 + 1)
                nc.scalar.activation(act_dot[:, a.slots[0]:a.slots[-1] + 1], dot[:, a.slots[0]:a.slots[-1] + 1],
                                     ACT.Silu).then_inc(s_sd, 1)

            def weigh(a, j):
                if not a.lives:
                    return
                act.wait_ge(s_w, a.g + 1)
                wait(act, s_mm, a.tile(j) - G + 1)
                k = a.slots[j]
                nc.scalar.activation(weighted[:, j, :], onehot[:, k, :], ACT.Copy,
                                     scale=weight[:, k:k + 1]).then_inc(s_wo, 1)

            act.wait_ge(s_0, 1)
            copy(Group(0, 0))

            def step(it, q):
                silu(Group(it, q, 1), 0)
                silu_dot(Group(it, q))
                silu(Group(it, q, 1), 1)
                weigh(Group(it, q), 0)
                a = Group(it, q, 3)
                if a.lives:
                    it8, k = a.at8(0)
                    gather.copy_indices(act, it8, k // G)
                copy(Group(it, q, 2))
                silu(Group(it, q, 1), 2)
                weigh(Group(it, q), 1)
                silu(Group(it, q, 1), 3)
                weigh(Group(it, q), 2)
                weigh(Group(it, q), 3)
            steps(act, step)

        @block.vector
        def _(v):
            V = nc.vector
            V.memset(attT[D_EDGE:D_EDGE + 1, :, :, :], 1.0).then_inc(s_0, 1)
            regs = [v.alloc_register(f"l2_nt{k}") for k in range(UH)]

            def build(a, j):
                if not a.lives:
                    return
                wait(v, s_wo, a.tile(j) - UH + 1)
                V.tensor_scalar(onehot[:, a.slots[j], :], c.iota_b[:], c.lo_d[:, at(a.tile(j))], None,
                                ALU.is_equal).then_inc(s_oh, 1)

            def q_times_k(a, j):
                if not a.lives:
                    return
                t = a.tile(j)
                it8, k = a.at8(j)
                gather.landed(v, it8, k)
                v.wait_ge(s_q, t + 1)
                wait(v, s_dot, t - 1)
                V.tensor_tensor(prod[:, j % 2, :], b_q[j % 2][:, 0:D], kv[:, k, 0:D], ALU.mult).then_inc(s_t1, 1)

            def times_dk(a, j):
                if not a.lives:
                    return
                t, k = a.tile(j), a.slots[j]
                v.wait_ge(s_si, t + 1)
                v.wait_ge(s_t1, t + 1)
                wait(v, s_sd, a.g - Q4 + 1)
                wait(v, s_dot, t)
                V.tensor_tensor_reduce(scratch, prod[:, j % 2, :], dkv[:, j, 0:D], 1.0, 0.0, ALU.mult,
                                       ALU.add, dot[:, k:k + 1]).then_inc(s_dot, 1)

            def message(a, j):
                if not a.lives:
                    return
                it8, k = a.at8(j)
                wait(v, s_mm, a.tile(j) - U + 1)
                V.tensor_tensor(msg[:, k, :], kv[:, k, D:2 * D], dkv[:, j, D:2 * D], ALU.mult).then_inc(s_msg_v, 1)

            def weights(a):
                if not a.lives:
                    return
                v.wait_ge(s_sd, a.g + 1)
                s0, s1 = a.slots[0], a.slots[-1] + 1
                V.tensor_tensor(weight[:, s0:s1], act_dot[:, s0:s1], att[:, s0:s1, D_EDGE], ALU.mult).then_inc(s_w, 1)

            def add(a, j):
                if not a.lives:
                    return
                t = a.tile(j)
                node_tile = v.snap(regs[a.slots[j]], min_val=0, max_val=NODE_TILES - 1)
                v.wait_ge(s_mm, t + 1)
                v.wait_ge(s_add, t + 1)
                o = c.AGG[:, at(node_tile), 0:D]
                V.tensor_tensor(o, b_m[j % 2][:, 0:D].unsqueeze(1), o, ALU.add).then_inc(s_add, 1)

            for q in range(2):
                for j in range(G):
                    build(Group(0, q), j)

            def step(it, q):
                for j in range(G):
                    q_times_k(Group(it, q, 1), j)
                    add(Group(it, q, -1), j + 1) if j < 3 else add(Group(it, q), 0)
                    if j == 2 and q == 0:
                        v.load(regs, c.nt_d[0:1, at(it * UH, UH)])
                    build(Group(it, q, 3), j)
                    times_dk(Group(it, q, 1), j)
                    if j == 0:
                        weights(Group(it, q))
                message(Group(it, q, 1), G - 1)
            step(0, -1)
            V.memset(c.AGG[:, :, :], 0.0).then_inc(s_add, 1)
            loop_steps(v, step)
            for j in (1, 2, 3):
                add(Group(SLOT_TILES // UH - 1, Q4 - 1), j)


def head_stage(nc, c, table):
    cv = Carve(c.work)
    rows, msg, onehot, nodeT = cv(UH, D_T3), cv(UH, AGG_W), cv(UH, P), cv(2, G, P)
    z, z2 = cv(2, G, HEADS), cv(2, G, HEADS)
    s_0, s_oh, s_tr, s_cp, s_el, s_z, s_lk, s_e, s_msg, s_mm, s_add = (
        c.sem(f"s_l3_{n}") for n in ("zero", "oh", "tr", "cp", "el", "z", "lk", "e", "msg", "mm", "add"))
    gather = Gather(nc, c, c.idx_s, table, lambda k: rows[:, k, :], UH)
    b_oT, b_el, b_m = (c.bank[0], c.bank[1]), (c.bank[2], c.bank[3]), c.bank[4:8]
    def steps(eng, step):
        def body(it, first, last):
            for q in range(Q4):
                step(it, q)
        edge_loop(eng, body, UH)

    with nc.Block() as block:
        @block.gpsimd
        def _(p):
            gather.gpsimd(p, s_msg)

        @block.tensor
        def _(pe):
            regs = [pe.alloc_register(f"l3_pe_nt{k}") for k in range(UH)]

            def turn(a):
                if not a.lives:
                    return
                pe.wait_ge(s_oh, a.tile(0) + G)
                wait(pe, s_cp, a.g - 1)
                for j, k in enumerate(a.slots):
                    mm = nc.tensor.transpose(b_oT[a.q % 2][:, j * P:(j + 1) * P], onehot[:, k, :], c.ident[:])
                mm.then_inc(s_tr, 1)

            def el(a):
                if not a.lives:
                    return
                if a.q == 0:
                    pe.load(regs, c.nt_s[0:1, at(a.it * UH, UH)])
                pe.wait_ge(s_cp, a.g + 1)
                wait(pe, s_z, a.g - 1)
                for j, k in enumerate(a.slots):
                    node_tile = pe.snap(regs[k], min_val=0, max_val=NODE_TILES - 1)
                    mm = nc.tensor.matmul(b_el[a.q % 2][:, j * HEADS:(j + 1) * HEADS], nodeT[:, a.q % 2, j, :],
                                          c.EL[:, at(node_tile), :], start=True, stop=True)
                mm.then_inc(s_el, 1)

            def sums(a):
                for j, k in enumerate(a.slots):
                    pe.wait_ge(s_msg, a.tile(j) + 1)
                    wait(pe, s_add, a.tile(j) - G + 1)
                    nc.tensor.matmul(b_m[j][:, 0:AGG_W], onehot[:, k, :], msg[:, k, :], start=True,
                                     stop=True).then_inc(s_mm, 1)

            turn(Group(0, 0))
            turn(Group(0, 1))
            el(Group(0, 0))

            def step(it, q):
                el(Group(it, q, 1))
                turn(Group(it, q, 2))
                sums(Group(it, q))
            steps(pe, step)

        @block.scalar
        def _(act):
            for q in range(Q4):
                gather.copy_indices(act, 0, q)

            def copy(a):
                if not a.lives:
                    return
                act.wait_ge(s_tr, a.g + 1)
                wait(act, s_el, a.g - 1)
                nc.scalar.copy(flat(nodeT[:, a.q % 2, :, :]), b_oT[a.q % 2][:, :]).then_inc(s_cp, 1)

            def exp(a):
                if not a.lives:
                    return
                act.wait_ge(s_lk, a.g + 1)
                wait(act, s_mm, (a.g - Q4 + 1) * G)
                nc.scalar.activation(msg[:, a.slots[0]:a.slots[-1] + 1, D:AGG_W], z2[:, a.q % 2, :, :],
                                     ACT.Exp).then_inc(s_e, 1)

            copy(Group(0, 0))
            copy(Group(0, 1))
            exp(Group(0, 0))

            def step(it, q):
                copy(Group(it, q, 2))
                exp(Group(it, q, 1))
                if not isinstance(it, int) or it < SLOT_TILES // UH - 1:
                    gather.copy_indices(act, it + 1, q)
            steps(act, step)

        @block.vector
        def _(v):
            V = nc.vector
            V.memset(c.AGG[:, :, :], 0.0).then_inc(s_0, 1)
            v.wait_ge(s_0, 1)
            regs = [v.alloc_register(f"l3_nt{k}") for k in range(UH)]

            def build(a, j):
                if not a.lives:
                    return
                wait(v, s_mm, a.tile(j) - UH + 1)
                V.tensor_scalar(onehot[:, a.slots[j], :], c.iota_f[:], c.lo_s[:, at(a.tile(j))], None,
                                ALU.is_equal).then_inc(s_oh, 1)

            def leaky(a):
                if not a.lives:
                    return
                for k in a.slots:
                    gather.landed(v, a.it, k)
                v.wait_ge(s_el, a.g + 1)
                V.tensor_tensor(z[:, a.q % 2, :, :], b_el[a.q % 2][:, 0:G * HEADS].rearrange("p (a b) -> p a b", a=G),
                                rows[:, a.slots[0]:a.slots[-1] + 1, D_HEAD:D_T3], ALU.add).then_inc(s_z, 1)
                v.wait_ge(s_z, a.g + 1)
                wait(v, s_e, a.g - 1)
                V.scalar_tensor_tensor(out=z2[:, a.q % 2, :, :], in0=z[:, a.q % 2, :, :], scalar=0.2,
                                       in1=z[:, a.q % 2, :, :], op0=ALU.mult, op1=ALU.max).then_inc(s_lk, 1)

            def message(a, j):
                v.wait_ge(s_e, a.g + 1)
                k = a.slots[j]
                V.tensor_tensor(msg[:, k, 0:D].rearrange("p (h d) -> p h d", h=HEADS),
                                rows[:, k, 0:D_HEAD].unsqueeze(1).broadcast_to([P, HEADS, D_HEAD]),
                                msg[:, k, D:AGG_W].unsqueeze(2).broadcast_to([P, HEADS, D_HEAD]),
                                ALU.mult).then_inc(s_msg, 1)

            def add(a, j):
                if not a.lives:
                    return
                node_tile = v.snap(regs[a.slots[j]], min_val=0, max_val=NODE_TILES - 1)
                v.wait_ge(s_mm, a.tile(j) + 1)
                wait(v, s_add, a.tile(j))
                o = c.AGG[:, at(node_tile), :]
                V.tensor_tensor(o, b_m[j][:, 0:AGG_W].unsqueeze(1), o, ALU.add).then_inc(s_add, 1)

            for q in range(3):
                for j in range(G):
                    build(Group(0, q), j)
            leaky(Group(0, 0))

            def step(it, q):
                for j in range(G):
                    message(Group(it, q), j)
                    add(Group(it, q, -1), j)
                    if j == G - 1 and q == 0:
                        v.load(regs, c.nt_s[0:1, at(it * UH, UH)])
                    build(Group(it, q, 3), j)
                    if j == 1:
                        leaky(Group(it, q, 1))
            steps(v, step)
            for j in range(G):
                add(Group(SLOT_TILES // UH - 1, Q4 - 1), j)


def program(nc, src, dst, typ, wgt, attr, x, w12, wrel, wqkv, wo, wd, w3, wlr, bias, out):
    def dram(name, shape):
        return nc.dram_tensor(name, shape, f32, kind="Internal").ap()
    t0, t1 = dram("rows_w2", (NODE_ROWS, D)), dram("rows_rel", (NODE_ROWS, N_RELS * D))
    t2, t3 = dram("rows_kv", (NODE_ROWS, 2 * D)), dram("rows_head", (NODE_ROWS, D_T3))
    att_rows = dram("att_rows", (SLOTS, ROW))
    with ExitStack() as ctx:
        c = Chip(nc, ctx)
        weights = [(c.w12[:, :, :], w12.rearrange("(z p) n -> p z n", p=P)),
                   (c.wrel[:, :, :], wrel.rearrange("(z p) n -> p z n", p=P)),
                   (c.wqkv[:, :, :], wqkv.rearrange("(z p) n -> p z n", p=P)),
                   (c.wo[:, :, :], wo.rearrange("(z p) n -> p z n", p=P)),
                   (c.wd[:, :], wd), (c.w3[:, :, :], w3.rearrange("(z p) n -> p z n", p=P)),
                   (c.wlr[:, :], wlr), (c.bias[:, :], bias.broadcast_to([P, BIAS_W]))]
        s_row = [c.sem(f"s_row{h}") for h in range(2)]
        with ExitStack() as ctx2:
            prep = Prep(nc, c, ctx2)
            rank_stage(nc, c, src, dst, typ, wgt, att_rows, prep)
            edge_stage(nc, c, attr, x, weights, att_rows, t0, prep, s_row, SCATTER_0)
        sum_stage(nc, c, "l0", c.idx_s, c.lo_s, c.nt_s, t0, True)
        node_stage_1(nc, c, t1, prep, attr, att_rows, s_row, SCATTER_0)
        sum_stage(nc, c, "l1", c.idx_d1, c.lo_d, c.nt_d, t1.rearrange("n (r d) -> (n r) d", r=N_RELS), False)
        batch_norm_stage(nc, c)
        node_stage_2(nc, c, t2)
        attention_stage(nc, c, t2, att_rows.rearrange("(p t) c -> p t c", p=P))
        node_stage_3(nc, c, t3)
        head_stage(nc, c, t3)
        output_stage(nc, c, out)


def kernel(x, src, dst, edge_attr_64, edge_type_8, edge_weight, L0_gnn_W1, L0_gnn_b1, L0_gnn_W2, L0_gnn_b2,
           L1_gnn_weight, L1_gnn_gamma, L1_gnn_beta, L2_gnn_ln_g, L2_gnn_ln_b, L2_gnn_Wq, L2_gnn_bq, L2_gnn_Wk,
           L2_gnn_bk, L2_gnn_Wv, L2_gnn_bv, L2_gnn_Wo, L2_gnn_bo, L2_gnn_Wdk, L2_gnn_bdk, L2_gnn_Wdv, L2_gnn_bdv,
           L3_gnn_W, L3_gnn_Wl, L3_gnn_Wr, L3_gnn_b):
    import concourse.bacc as bacc
    from concourse.bass_utils import run_bass_kernel_spmd

    def edges(a, pad):
        a = np.asarray(a)
        full = np.full((EDGE_ROWS,) + a.shape[1:], pad, a.dtype)
        full[:N_EDGES] = a
        return full.reshape((P, EDGE_COLS) + a.shape[1:])

    def turned(*ws):
        return np.ascontiguousarray(np.concatenate([np.asarray(w).T for w in ws], axis=1))

    xs = np.zeros((NODE_ROWS, D), np.float32)
    xs[:N_NODES] = np.asarray(x)
    ins = {
        "src": edges(src, PAD_NODE), "dst": edges(dst, PAD_NODE), "typ": edges(edge_type_8, 0),
        "wgt": edges(edge_weight, 0), "attr": edges(edge_attr_64, 0), "x": xs,
        "w12": turned(L0_gnn_W1, L0_gnn_W2),
        "wrel": np.ascontiguousarray(np.asarray(L1_gnn_weight).transpose(1, 0, 2).reshape(D, N_RELS * D)),
        "wqkv": turned(L2_gnn_Wq, L2_gnn_Wk, L2_gnn_Wv), "wo": turned(L2_gnn_Wo),
        "wd": np.concatenate([turned(L2_gnn_Wdk, L2_gnn_Wdv),
                              np.concatenate([np.asarray(L2_gnn_bdk), np.asarray(L2_gnn_bdv)])[None]]),
        "w3": np.asarray(L3_gnn_W),
        "wlr": np.concatenate([np.eye(D_HEAD, dtype=np.float32), turned(L3_gnn_Wr, L3_gnn_Wl)], axis=1),
        "bias": np.concatenate([np.asarray(a) for a in (
            L0_gnn_b1, L0_gnn_b2, L1_gnn_gamma, L1_gnn_beta, L2_gnn_ln_g, L2_gnn_ln_b, L2_gnn_bq, L2_gnn_bk,
            L2_gnn_bv, L2_gnn_bo, L3_gnn_b)])[None],
    }
    nc = bacc.Bacc("TRN2", target_bir_lowering=False, num_devices=1)
    aps = {k: nc.dram_tensor("in_" + k, a.shape, mybir.dt.from_np(a.dtype), kind="ExternalInput").ap()
           for k, a in ins.items()}
    out = nc.dram_tensor("out_0", (N_NODES, D), f32, kind="ExternalOutput").ap()
    program(nc, *[aps[k] for k in ("src", "dst", "typ", "wgt", "attr", "x", "w12", "wrel", "wqkv", "wo", "wd", "w3",
                                   "wlr", "bias")], out)
    r = run_bass_kernel_spmd(nc, [{"in_" + k: a for k, a in ins.items()}], core_ids=[0])
    return r.results[0]["out_0"]
```
